# Optimizing a Trainium2 kernel written in Bass

```python
import numpy as np
import jax
import jax.numpy as jnp

def _softmax(x, axis=-1):
    return jax.nn.softmax(x, axis=axis)

def _gelu(x):
    return jax.nn.gelu(x, approximate=True)

def _silu(x):
    return jax.nn.silu(x)

def _sigmoid(x):
    return jax.nn.sigmoid(x)

def _layernorm(x, axis=-1, eps=1e-05):
    m = jnp.mean(x, axis=axis, keepdims=True)
    v = jnp.var(x, axis=axis, keepdims=True)
    return (x - m) / jnp.sqrt(v + eps)

def _scatter_add(tgt, idx, src, axis=0):
    return tgt.at[idx].add(src)

def _segment_sum(src, seg, n):
    return jax.ops.segment_sum(src, seg, n)
kernel_name = 'mk_cond_resid_d4_seqx_r4_323825'

def setup_inputs(seed: int=0):
    np.random.seed(seed)
    _w = jnp.asarray

    def _rec_inputs():
        import jax
        import jax.numpy as jnp
        _rk = jax.random.key(seed)
        x = -0.000125 + 0.9999 * jax.random.normal(jax.random.fold_in(_rk, 1), (64, 64, 256), jnp.float32)
        _lenS = 64 - jax.random.randint(jax.random.fold_in(_rk, 7), (64,), 0, max(1, 64 // 4) + 1, jnp.int32)
        _lenS2 = 64 - jax.random.randint(jax.random.fold_in(_rk, 8), (64,), 0, max(1, 64 // 4) + 1, jnp.int32)
        cond_512 = 0.0061147 + 1.02565 * jax.random.normal(jax.random.fold_in(_rk, 11), (64, 128), jnp.float32)
        itok_BxS_0_999 = jax.random.randint(jax.random.fold_in(_rk, 12), (64, 64), 0, 250, jnp.int32)
        itok_BxS_0_4 = jax.random.randint(jax.random.fold_in(_rk, 13), (64, 64), 0, 5, jnp.int32)
        cond_64 = 0.0990542 + 1.04422 * jax.random.normal(jax.random.fold_in(_rk, 15), (64, 64), jnp.float32)
        fside_Bx32_0 = -0.136436 + 0.990155 * jax.random.normal(jax.random.fold_in(_rk, 16), (64, 32), jnp.float32)
        _validS = jnp.arange(64)[None, :] < _lenS[:, None]
        _validS2 = jnp.arange(64)[None, :] < _lenS2[:, None]
        _causal = jnp.tril(jnp.ones((64, 64), dtype=bool))
        mask_BxS_ik0 = jnp.where(jnp.broadcast_to(_validS[:, :], (64, 64)), 0, 1).astype(jnp.int32)
        return (x, cond_512, itok_BxS_0_999, itok_BxS_0_4, cond_64, fside_Bx32_0, mask_BxS_ik0)
    x, cond_512, itok_BxS_0_999, itok_BxS_0_4, cond_64, fside_Bx32_0, mask_BxS_ik0 = _rec_inputs()

    def _L0_cond_setup():
        import jax, jax.numpy as jnp
        import numpy as np
        B, S, D, H, C = (8, 1024, 256, 64, 128)
        INIT_RANGE = 0.01
        key = jax.random.key(seed)
        ks = jax.random.split(key, 6)
        return {'hidden_states': jax.random.normal(ks[0], (B, S, D), dtype=jnp.float32), 'conditions': jax.random.normal(ks[1], (B, C), dtype=jnp.float32), 'down_project': jax.random.normal(ks[2], (D, H), dtype=jnp.float32) * INIT_RANGE, 'down_gamma': jax.random.normal(ks[3], (C, H), dtype=jnp.float32), 'down_beta': jnp.zeros((C, H), dtype=jnp.float32), 'up_project': jax.random.normal(ks[4], (H, D), dtype=jnp.float32) * INIT_RANGE, 'up_gamma': jax.random.normal(ks[5], (C, D), dtype=jnp.float32), 'up_beta': jnp.zeros((C, D), dtype=jnp.float32)}
    _L0_cond_all = _L0_cond_setup()
    _L0_cond_in = {k: v for k, v in _L0_cond_all.items() if k in ('down_project', 'down_gamma', 'down_beta', 'up_project', 'up_gamma', 'up_beta')}
    del _L0_cond_all

    def _L1_cond_setup():
        import jax, jax.numpy as jnp
        import numpy as np
        IN_DIM = 256
        OUT_DIM = 256
        MU_DIM = 128
        K = 30
        key = jax.random.key(seed)
        k1, k2, k3, k4, k5 = jax.random.split(key, 5)
        B, S = (16, 512)
        x = jax.random.normal(k1, (B, S, IN_DIM), dtype=jnp.float32)
        mu = jax.random.normal(k2, (B, MU_DIM), dtype=jnp.float32)
        W_dec = jax.random.normal(k3, (MU_DIM, (IN_DIM + 1) * K), dtype=jnp.float32) / np.sqrt(MU_DIM)
        b_dec = jax.random.normal(k4, ((IN_DIM + 1) * K,), dtype=jnp.float32) * 0.01
        V = jax.random.normal(k5, (K, OUT_DIM), dtype=jnp.float32) / np.sqrt(K)
        return {'x': x, 'mu': mu, 'W_dec': W_dec, 'b_dec': b_dec, 'V': V}
    _L1_cond_all = _L1_cond_setup()
    _L1_cond_in = {k: v for k, v in _L1_cond_all.items() if k in ('W_dec', 'b_dec', 'V')}
    del _L1_cond_all

    def _L2_cond_setup():
        import jax, jax.numpy as jnp
        import numpy as np
        import math
        HEAD_NUM = 16
        EPS = 1e-08

        def modulated_linear(x, s, aff_w, aff_b, w, b):
            style = s @ aff_w.T + aff_b
            w_mod = w[None, :, :] * style[:, None, :]
            demod = jax.lax.rsqrt(jnp.sum(w_mod * w_mod, axis=2) + EPS)
            w_mod = w_mod * demod[:, :, None]
            return jnp.einsum('bni,boi->bno', x, w_mod) + b
        key = jax.random.key(seed)
        ks = jax.random.split(key, 6)
        B, N, F, S = (8, 256, 256, 128)
        return {'x': jax.random.normal(ks[0], (B, N, F), dtype=jnp.float32), 's': jax.random.normal(ks[1], (B, S), dtype=jnp.float32), 'k_aff_w': jax.random.normal(ks[2], (F, S), dtype=jnp.float32) * 0.02, 'k_aff_b': jnp.ones((F,), dtype=jnp.float32), 'k_w': jax.random.normal(ks[3], (F, F), dtype=jnp.float32) * 0.02, 'k_b': jnp.zeros((F,), dtype=jnp.float32), 'o_aff_w': jax.random.normal(ks[4], (F, S), dtype=jnp.float32) * 0.02, 'o_aff_b': jnp.ones((F,), dtype=jnp.float32), 'o_w': jax.random.normal(ks[5], (F, F), dtype=jnp.float32) * 0.02, 'o_b': jnp.zeros((F,), dtype=jnp.float32)}
    _L2_cond_all = _L2_cond_setup()
    _L2_cond_in = {k: v for k, v in _L2_cond_all.items() if k in ('k_aff_w', 'k_aff_b', 'k_w', 'k_b', 'o_aff_w', 'o_aff_b', 'o_w', 'o_b')}
    del _L2_cond_all

    def _L3_cond_setup():
        import jax, jax.numpy as jnp
        import numpy as np
        EPS = 1e-05

        def _ln(x, g, b):
            m = jnp.mean(x, axis=-1, keepdims=True)
            v = jnp.mean((x - m) ** 2, axis=-1, keepdims=True)
            return (x - m) * jax.lax.rsqrt(v + EPS) * g + b

        def _mlp_ln(s, W1, b1, W2, b2, g, b):
            h = jax.nn.silu(s @ W1 + b1) @ W2 + b2
            return _ln(h, g, b)
        key = jax.random.key(seed)
        B, S, D = (4, 512, 256)
        MEM, NOI, RES = (128, 64, 32)
        ks = jax.random.split(key, 40)
        ki = iter(range(40))

        def nrm(shape, scale=0.02):
            return jax.random.normal(ks[next(ki)], shape, jnp.float32) * scale

        def gamma(shape):
            return jnp.ones(shape, jnp.float32) + nrm(shape)
        inp = {'x': jax.random.normal(ks[next(ki)], (B, S, D), jnp.float32), 'pathway_ids': jax.random.randint(ks[next(ki)], (B, S), 0, 250), 'compartment_ids': jax.random.randint(ks[next(ki)], (B, S), 0, 5), 'time_steps': jax.random.randint(ks[next(ki)], (B, S), 0, 5), 'scale_type': jax.random.randint(ks[next(ki)], (B, S), 0, 3), 'memory_state': jax.random.normal(ks[next(ki)], (B, MEM), jnp.float32), 'noise_state': jax.random.normal(ks[next(ki)], (B, NOI), jnp.float32), 'resource_state': jax.random.normal(ks[next(ki)], (B, RES), jnp.float32), 'pw_g': gamma((250, D)), 'pw_b': nrm((250, D)), 'cp_g': gamma((5, D)), 'cp_b': nrm((5, D)), 'tm_g': gamma((5, D)), 'tm_b': nrm((5, D)), 'ms_g': gamma((3, D)), 'ms_b': nrm((3, D)), 'mem_W1': nrm((MEM, D)), 'mem_b1': jnp.zeros((D,)), 'mem_W2': nrm((D, D)), 'mem_b2': jnp.zeros((D,)), 'mem_g': gamma((D,)), 'mem_be': jnp.zeros((D,)), 'noi_W1': nrm((NOI, D)), 'noi_b1': jnp.zeros((D,)), 'noi_W2': nrm((D, D)), 'noi_b2': jnp.zeros((D,)), 'noi_g': gamma((D,)), 'noi_be': jnp.zeros((D,)), 'res_W1': nrm((RES, D)), 'res_b1': jnp.zeros((D,)), 'res_W2': nrm((D, D)), 'res_b2': jnp.zeros((D,)), 'res_g': gamma((D,)), 'res_be': jnp.zeros((D,)), 'int_W1': nrm((6 * D, D)), 'int_b1': jnp.zeros((D,)), 'int_W2': nrm((D, D)), 'int_b2': jnp.zeros((D,)), 'int_g': gamma((D,)), 'int_be': jnp.zeros((D,)), 'aw': jnp.ones((6,), jnp.float32) / 6.0}
        return inp
    _L3_cond_all = _L3_cond_setup()
    _L3_cond_in = {k: v for k, v in _L3_cond_all.items() if k in ('pw_g', 'pw_b', 'cp_g', 'cp_b', 'tm_g', 'tm_b', 'ms_g', 'ms_b', 'mem_W1', 'mem_b1', 'mem_W2', 'mem_b2', 'mem_g', 'mem_be', 'noi_W1', 'noi_b1', 'noi_W2', 'noi_b2', 'noi_g', 'noi_be', 'res_W1', 'res_b1', 'res_W2', 'res_b2', 'res_g', 'res_be', 'int_W1', 'int_b1', 'int_W2', 'int_b2', 'int_g', 'int_be', 'aw')}
    del _L3_cond_all
    return {'x': x, 'cond_512': cond_512, 'itok_BxS_0_999': itok_BxS_0_999, 'itok_BxS_0_4': itok_BxS_0_4, 'cond_64': cond_64, 'fside_Bx32_0': fside_Bx32_0, 'mask_BxS_ik0': mask_BxS_ik0, 'L0_cond_down_project': _L0_cond_in['down_project'], 'L0_cond_down_gamma': _L0_cond_in['down_gamma'], 'L0_cond_down_beta': _L0_cond_in['down_beta'], 'L0_cond_up_project': _L0_cond_in['up_project'], 'L0_cond_up_gamma': _L0_cond_in['up_gamma'], 'L0_cond_up_beta': _L0_cond_in['up_beta'], 'L1_cond_W_dec': _L1_cond_in['W_dec'], 'L1_cond_b_dec': _L1_cond_in['b_dec'], 'L1_cond_V': _L1_cond_in['V'], 'L2_cond_k_aff_w': _L2_cond_in['k_aff_w'], 'L2_cond_k_aff_b': _L2_cond_in['k_aff_b'], 'L2_cond_k_w': _L2_cond_in['k_w'], 'L2_cond_k_b': _L2_cond_in['k_b'], 'L2_cond_o_aff_w': _L2_cond_in['o_aff_w'], 'L2_cond_o_aff_b': _L2_cond_in['o_aff_b'], 'L2_cond_o_w': _L2_cond_in['o_w'], 'L2_cond_o_b': _L2_cond_in['o_b'], 'L3_cond_pw_g': _L3_cond_in['pw_g'], 'L3_cond_pw_b': _L3_cond_in['pw_b'], 'L3_cond_cp_g': _L3_cond_in['cp_g'], 'L3_cond_cp_b': _L3_cond_in['cp_b'], 'L3_cond_tm_g': _L3_cond_in['tm_g'], 'L3_cond_tm_b': _L3_cond_in['tm_b'], 'L3_cond_ms_g': _L3_cond_in['ms_g'], 'L3_cond_ms_b': _L3_cond_in['ms_b'], 'L3_cond_mem_W1': _L3_cond_in['mem_W1'], 'L3_cond_mem_b1': _L3_cond_in['mem_b1'], 'L3_cond_mem_W2': _L3_cond_in['mem_W2'], 'L3_cond_mem_b2': _L3_cond_in['mem_b2'], 'L3_cond_mem_g': _L3_cond_in['mem_g'], 'L3_cond_mem_be': _L3_cond_in['mem_be'], 'L3_cond_noi_W1': _L3_cond_in['noi_W1'], 'L3_cond_noi_b1': _L3_cond_in['noi_b1'], 'L3_cond_noi_W2': _L3_cond_in['noi_W2'], 'L3_cond_noi_b2': _L3_cond_in['noi_b2'], 'L3_cond_noi_g': _L3_cond_in['noi_g'], 'L3_cond_noi_be': _L3_cond_in['noi_be'], 'L3_cond_res_W1': _L3_cond_in['res_W1'], 'L3_cond_res_b1': _L3_cond_in['res_b1'], 'L3_cond_res_W2': _L3_cond_in['res_W2'], 'L3_cond_res_b2': _L3_cond_in['res_b2'], 'L3_cond_res_g': _L3_cond_in['res_g'], 'L3_cond_res_be': _L3_cond_in['res_be'], 'L3_cond_int_W1': _L3_cond_in['int_W1'], 'L3_cond_int_b1': _L3_cond_in['int_b1'], 'L3_cond_int_W2': _L3_cond_in['int_W2'], 'L3_cond_int_b2': _L3_cond_in['int_b2'], 'L3_cond_int_g': _L3_cond_in['int_g'], 'L3_cond_int_be': _L3_cond_in['int_be'], 'L3_cond_aw': _L3_cond_in['aw']}

def reference(x, cond_512, itok_BxS_0_999, itok_BxS_0_4, cond_64, fside_Bx32_0, mask_BxS_ik0, L0_cond_down_project, L0_cond_down_gamma, L0_cond_down_beta, L0_cond_up_project, L0_cond_up_gamma, L0_cond_up_beta, L1_cond_W_dec, L1_cond_b_dec, L1_cond_V, L2_cond_k_aff_w, L2_cond_k_aff_b, L2_cond_k_w, L2_cond_k_b, L2_cond_o_aff_w, L2_cond_o_aff_b, L2_cond_o_w, L2_cond_o_b, L3_cond_pw_g, L3_cond_pw_b, L3_cond_cp_g, L3_cond_cp_b, L3_cond_tm_g, L3_cond_tm_b, L3_cond_ms_g, L3_cond_ms_b, L3_cond_mem_W1, L3_cond_mem_b1, L3_cond_mem_W2, L3_cond_mem_b2, L3_cond_mem_g, L3_cond_mem_be, L3_cond_noi_W1, L3_cond_noi_b1, L3_cond_noi_W2, L3_cond_noi_b2, L3_cond_noi_g, L3_cond_noi_be, L3_cond_res_W1, L3_cond_res_b1, L3_cond_res_W2, L3_cond_res_b2, L3_cond_res_g, L3_cond_res_be, L3_cond_int_W1, L3_cond_int_b1, L3_cond_int_W2, L3_cond_int_b2, L3_cond_int_g, L3_cond_int_be, L3_cond_aw):
    import jax
    import jax.numpy as jnp

    def _L0_cond_ref(hidden_states, conditions, down_project, down_gamma, down_beta, up_project, up_gamma, up_beta):
        import jax, jax.numpy as jnp
        import numpy as np
        B, S, D, H, C = (8, 1024, 256, 64, 128)
        INIT_RANGE = 0.01
        dg = conditions @ down_gamma
        db = conditions @ down_beta
        ug = conditions @ up_gamma
        ub = conditions @ up_beta
        w_down = down_project[None, :, :] * dg[:, None, :] + db[:, None, :]
        down = jnp.einsum('bsd,bdh->bsh', hidden_states, w_down)
        act = jax.nn.relu(down)
        w_up = up_project[None, :, :] * ug[:, None, :] + ub[:, None, :]
        up = jnp.einsum('bsh,bhd->bsd', act, w_up)
        return up + hidden_states

    def _L1_cond_ref(x, mu, W_dec, b_dec, V):
        import jax, jax.numpy as jnp
        import numpy as np
        IN_DIM = 256
        OUT_DIM = 256
        MU_DIM = 128
        K = 30
        B = mu.shape[0]
        U = (mu @ W_dec + b_dec).reshape(B, IN_DIM + 1, K)
        param = jnp.einsum('bik,kj->bij', U, V)
        weight = param[:, :-1, :]
        bias = param[:, -1, :]
        out = jnp.einsum('bsd,bde->bse', x, weight)
        out = out + bias[:, None, :]
        return out

    def _L2_cond_ref(x, s, k_aff_w, k_aff_b, k_w, k_b, o_aff_w, o_aff_b, o_w, o_b):
        import jax, jax.numpy as jnp
        import numpy as np
        import math
        HEAD_NUM = 16
        EPS = 1e-08

        def modulated_linear(x, s, aff_w, aff_b, w, b):
            style = s @ aff_w.T + aff_b
            w_mod = w[None, :, :] * style[:, None, :]
            demod = jax.lax.rsqrt(jnp.sum(w_mod * w_mod, axis=2) + EPS)
            w_mod = w_mod * demod[:, :, None]
            return jnp.einsum('bni,boi->bno', x, w_mod) + b
        B, N, F = x.shape
        H = HEAD_NUM
        D = F // H
        kx = modulated_linear(x, s, k_aff_w, k_aff_b, k_w, k_b)
        kx = kx.reshape(B, N, H, D)
        q = k = v = kx
        scores = jnp.einsum('bnhd,bnjd->bnhj', q, k) / math.sqrt(D)
        A = jax.nn.softmax(scores, axis=-1)
        out = jnp.einsum('bnhj,bnjd->bnhd', A, v).reshape(B, N, F)
        out = modulated_linear(out, s, o_aff_w, o_aff_b, o_w, o_b)
        return out

    def _L3_cond_ref(x, pathway_ids, compartment_ids, time_steps, scale_type, memory_state, noise_state, resource_state, pw_g, pw_b, cp_g, cp_b, tm_g, tm_b, ms_g, ms_b, mem_W1, mem_b1, mem_W2, mem_b2, mem_g, mem_be, noi_W1, noi_b1, noi_W2, noi_b2, noi_g, noi_be, res_W1, res_b1, res_W2, res_b2, res_g, res_be, int_W1, int_b1, int_W2, int_b2, int_g, int_be, aw):
        import jax, jax.numpy as jnp
        import numpy as np
        EPS = 1e-05

        def _ln(x, g, b):
            m = jnp.mean(x, axis=-1, keepdims=True)
            v = jnp.mean((x - m) ** 2, axis=-1, keepdims=True)
            return (x - m) * jax.lax.rsqrt(v + EPS) * g + b

        def _mlp_ln(s, W1, b1, W2, b2, g, b):
            h = jax.nn.silu(s @ W1 + b1) @ W2 + b2
            return _ln(h, g, b)
        h = _ln(x, pw_g[pathway_ids], pw_b[pathway_ids])
        h = _ln(h, cp_g[compartment_ids], cp_b[compartment_ids])
        t = _ln(x, tm_g[time_steps], tm_b[time_steps])
        m = x + _mlp_ln(memory_state, mem_W1, mem_b1, mem_W2, mem_b2, mem_g, mem_be)[:, None, :]
        n = x + _mlp_ln(noise_state, noi_W1, noi_b1, noi_W2, noi_b2, noi_g, noi_be)[:, None, :]
        r = x + _mlp_ln(resource_state, res_W1, res_b1, res_W2, res_b2, res_g, res_be)[:, None, :]
        s = _ln(x, ms_g[scale_type], ms_b[scale_type])
        w = jax.nn.softmax(aw)
        cat = jnp.concatenate([w[0] * h, w[1] * t, w[2] * m, w[3] * n, w[4] * r, w[5] * s], axis=-1)
        return _mlp_ln(cat, int_W1, int_b1, int_W2, int_b2, int_g, int_be)
    x = x + _L0_cond_ref(x, cond_512, L0_cond_down_project, L0_cond_down_gamma, L0_cond_down_beta, L0_cond_up_project, L0_cond_up_gamma, L0_cond_up_beta)
    x = x + _L1_cond_ref(x, cond_512, L1_cond_W_dec, L1_cond_b_dec, L1_cond_V)
    x = x + _L2_cond_ref(x, cond_512, L2_cond_k_aff_w, L2_cond_k_aff_b, L2_cond_k_w, L2_cond_k_b, L2_cond_o_aff_w, L2_cond_o_aff_b, L2_cond_o_w, L2_cond_o_b)
    x = x + _L3_cond_ref(x, itok_BxS_0_999, itok_BxS_0_4, itok_BxS_0_4, mask_BxS_ik0, cond_512, cond_64, fside_Bx32_0, L3_cond_pw_g, L3_cond_pw_b, L3_cond_cp_g, L3_cond_cp_b, L3_cond_tm_g, L3_cond_tm_b, L3_cond_ms_g, L3_cond_ms_b, L3_cond_mem_W1, L3_cond_mem_b1, L3_cond_mem_W2, L3_cond_mem_b2, L3_cond_mem_g, L3_cond_mem_be, L3_cond_noi_W1, L3_cond_noi_b1, L3_cond_noi_W2, L3_cond_noi_b2, L3_cond_noi_g, L3_cond_noi_be, L3_cond_res_W1, L3_cond_res_b1, L3_cond_res_W2, L3_cond_res_b2, L3_cond_res_g, L3_cond_res_be, L3_cond_int_W1, L3_cond_int_b1, L3_cond_int_W2, L3_cond_int_b2, L3_cond_int_g, L3_cond_int_be, L3_cond_aw)
    return x

_drawn_inputs = setup_inputs


def setup_inputs(seed=0):
    import zlib

    import numpy as np

    out = dict(_drawn_inputs(seed))
    spreads = {'L0_cond_down_beta': (0.0, 0.1),
     'L0_cond_up_beta': (0.0, 0.1),
     'L2_cond_k_aff_b': (1.0, 0.2),
     'L2_cond_k_b': (0.0, 0.1),
     'L2_cond_o_aff_b': (1.0, 0.2),
     'L2_cond_o_b': (0.0, 0.1),
     'L3_cond_mem_b1': (0.0, 0.1),
     'L3_cond_mem_b2': (0.0, 0.1),
     'L3_cond_mem_be': (0.0, 0.1),
     'L3_cond_noi_b1': (0.0, 0.1),
     'L3_cond_noi_b2': (0.0, 0.1),
     'L3_cond_noi_be': (0.0, 0.1),
     'L3_cond_res_b1': (0.0, 0.1),
     'L3_cond_res_b2': (0.0, 0.1),
     'L3_cond_res_be': (0.0, 0.1),
     'L3_cond_int_b1': (0.0, 0.1),
     'L3_cond_int_b2': (0.0, 0.1),
     'L3_cond_int_be': (0.0, 0.1),
     'L3_cond_aw': (0.1666666716337204, 0.2)}
    factors = {}
    for name, (base, spread) in spreads.items():
        noise = np.random.default_rng([zlib.crc32(name.encode()), seed]).standard_normal(out[name].shape)
        drawn = base * np.exp(spread * noise) if base else spread * noise
        out[name] = jnp.asarray(drawn.astype(out[name].dtype))
    for name, factor in factors.items():
        out[name] = (out[name] * factor).astype(out[name].dtype)
    return out
```

```python
from contextlib import ExitStack

import concourse.bass as bass
from concourse import mybir

F32 = mybir.dt.float32
BF16 = mybir.dt.bfloat16
I32 = mybir.dt.int32
ALU = mybir.AluOpType
ACT = mybir.ActivationFunctionType
AX = mybir.AxisListType

B, S, D = 64, 64, 256
CB = 8
N = CB * S
NC = B // CB
NT = N // 128
NH, HD = 16, 16
H0 = 64
K1 = 30
LN_EPS = 1e-5
DEMOD_EPS = 1e-8
SCALE = HD ** -0.5
QG = 16
MLPS = ("mem", "noi", "res")


def build(nc, t, out):
    ctx = ExitStack()
    with ctx:
        def sb(name, shape, dt=F32):
            return ctx.enter_context(nc.sbuf_tensor(name, shape, dt))

        def sem(name):
            return ctx.enter_context(nc.semaphore(name))

        ident = sb("ident", [128, 128])
        batch_eye = sb("batch_eye", [128, B])
        rowclass = sb("rowclass", [128, 1])
        neghalf = sb("neghalf", [128, 128])
        ones3 = sb("ones3", [3, 128], BF16)
        w_down = sb("w_down", [128, 2, 128])
        w_up = sb("w_up", [H0, D + H0])
        db_rows = sb("db_rows", [128, H0])
        ub_rows = sb("ub_rows", [B, D])
        dg = sb("dg", [H0, B])
        ug = sb("ug", [128, 2, B])
        u_all = sb("u_all", [128, 2, B, K1])
        u_last = sb("u_last", [K1, B])
        v1 = sb("v1", [K1, D])
        kwT = sb("kwT", [128, 2, D])
        owT = sb("owT", [128, 2, D])
        style = sb("style", [128, 2, 2, B])
        demod = sb("demod", [128, 2, 2, B])
        cols = sb("cols", [128, 14])
        w1 = sb("w1", [128, 12, D])
        w2 = sb("w2", [128, 2, D])
        tables = sb("tables", [24, 4 * D], BF16)
        b2_parts = sb("b2_parts", [3, D], BF16)
        last_gb = sb("last_gb", [128, 2, D])
        vec_rows = sb("vec_rows", [B, D])
        pw_idx = sb("pw_idx", [128, NC * NT], I32)
        pw_now = sb("pw_now", [128, NT], I32)
        bd = sb("bd", [128, 128, S])
        w_dec = bd[:, :, :].rearrange("p a b -> p (a b)")[:, 0:K1 * (D + 1)].rearrange("p (k i) -> p k i", k=K1)

        xin = sb("xin", [128, NT, D])
        xT = sb("xT", [128, 2, N])
        t1 = sb("t1", [H0, N])
        row_in = sb("row_in", [128, N])
        act0 = sb("act0", [H0, N])
        row_mid = sb("row_mid", [B, N])
        x0 = sb("x0", [128, 2, N])
        u_chunk = sb("u_chunk", [128, 2, CB, K1])
        u1 = sb("u1", [K1, N])
        ys = sb("ys", [128, 2, N])
        x1 = sb("x1", [128, 2, N])
        kx = sb("kx", [128, 2, N])
        td = sb("td", [128, NH, S])
        vt = sb("vt", [128, HD + 1, S])
        rowmax = sb("rowmax", [128, S])
        dif = sb("dif", [128, S * NH])
        ex = sb("ex", [128, NH, S])
        rz = sb("rz", [128, 4, QG])
        av = sb("av", [128, HD, S])
        attnT = sb("attnT", [128, 2, N])
        tmp_o = sb("tmp_o", [128, 2, N])
        x1r = sb("x1r", [128, 2, N])
        x2T = sb("x2T", [128, 2, N])
        x2k = sb("x2k", [128, NT, D])
        stats = sb("stats", [128, 3, NT, 6])
        mv = sb("mv", [128, 3, NT, 2])
        ve = sb("ve", [128, 3, NT])
        rstd = sb("rstd", [128, 3, NT])
        xn = sb("xn", [128, NT, D])
        h1 = sb("h1", [128, NT, D])
        pwgb = sb("pwgb", [128, NT, 2 * D])
        xnT = sb("xnT", [128, 2, N])
        hnT = sb("hnT", [128, 2, N])
        tT = sb("tT", [128, 2, N])
        idx_rows = sb("idx_rows", [24, N], I32)
        onehot = sb("onehot", [24, N], BF16)
        ind = sb("ind", [B, N])
        th = sb("th", [128, 2, N])
        hid = sb("hid", [128, 2, N])
        yn = sb("yn", [128, NT, D])

        condT = xnT[:, 0, 0:B]
        c64T = xnT[0:64, 0, 64:64 + B]
        fsT = xnT[0:32, 0, 128:128 + B]
        dgam = xnT[:, 0, 192:256]
        dbet = xnT[:, 0, 256:320]
        bdec = xnT[:, 1, 0:60].rearrange("p (a k) -> p a k", a=2)
        bdec_last = xnT[0:K1, 1, 64:65]
        aw = xnT[:, 1, 72:78]
        awx = xnT[:, 1, 80:96]
        tabT = xnT[:, 1, 96:122].rearrange("p (a r) -> p a r", a=2)
        style2 = xnT[:, 1, 128:384].rearrange("p (l a b) -> p l a b", l=2, a=2)
        ugam = hnT[:, 0, 0:D]
        ubet = hnT[:, 0, D:2 * D]
        affT = hnT[:, 1, :].rearrange("p (l i) -> p l i", l=2)
        mw1 = {"mem": tT[:, 0, 0:D], "noi": tT[0:64, 0, D:2 * D], "res": tT[0:32, 1, 0:D]}
        mw2 = {"mem": tmp_o[:, 0, :].rearrange("p (k j) -> p k j", k=2),
               "noi": tmp_o[:, 1, :].rearrange("p (k j) -> p k j", k=2),
               "res": x2T[:, 0, :].rearrange("p (k j) -> p k j", k=2)}
        sq = x1r[:, :, :].rearrange("p l (k o) -> p l k o", k=2)
        rows = pwgb[0:B, :, :].rearrange("p a b -> p (a b)")[:, 0:6 * D].rearrange("p (r j) -> p r j", r=6)
        rows2 = attnT[0:B, :, :].rearrange("p a b -> p (a b)").rearrange("p (r j) -> p r j", r=4)
        mx = hid[:, 0, 0:384].rearrange("p (m a b) -> p m a b", m=3, a=2)
        mth = th[:, 0, 0:384].rearrange("p (m a b) -> p m a b", m=3, a=2)
        mvec = xn[0:B, 0:3, :]
        mvT = hid[:, 1, 0:384].rearrange("p (m a b) -> p m a b", m=3, a=2)
        src5 = yn[0:5, :, :].rearrange("p a b -> p (a b)")
        src3 = x2k[0:3, :, :].rearrange("p a b -> p (a b)")
        parts5 = h1[0:5, :, :].rearrange("p a b -> p (a b)").bitcast(BF16)[:, 0:2048].rearrange("p (s c) -> p s c", s=2)
        parts5l = th[0:5, 1, :].bitcast(BF16)
        parts3 = kx[0:3, :, :].rearrange("p a b -> p (a b)").bitcast(BF16).rearrange("p (s c) -> p s c", s=2)
        parts3l = ind[0:3, :].bitcast(BF16)
        b2src = idx_rows[0:1, 0:D].bitcast(F32)
        b2p = x2T[0:1, 1, 0:3 * D // 2].bitcast(BF16).rearrange("p (s c) -> p s c", s=3)

        pp = ctx.enter_context(nc.psum_tensor("pp", [128, 4 * 512], F32))
        ph = ctx.enter_context(nc.psum_tensor("ph", [128, 1024], F32))
        pk = ctx.enter_context(nc.psum_tensor("pk", [128, 1024], F32))
        P01, P23 = pp[:, 0:1024], pp[:, 1024:2048]
        P2, P3 = pp[:, 1024:1536], pp[:, 1536:2048]

        kx_dram = nc.dram_tensor("kx_dram", [CB, HD, NH, S], F32, kind="Internal").ap()
        av_dram = nc.dram_tensor("av_dram", [CB, NH, HD, S], F32, kind="Internal").ap()
        ex_dram = nc.dram_tensor("ex_dram", [CB, NH, NH, S], F32, kind="Internal").ap()
        x1_dram = nc.dram_tensor("x1_dram", [128, NC, 2 * N], F32, kind="Internal").ap()

        s_load = sem("setup_loaded"); s_wdec = sem("w_dec_loaded"); s_const = sem("constants_set")
        s_tab = sem("tables_moved"); s_zero = sem("bd_zeroed"); s_ready = sem("setup_done")
        s_settled = sem("settled")
        ps_par = sem("ps_params"); ps_u0 = sem("ps_u_half0"); ps_u1 = sem("ps_u_half1"); ps_mh = sem("ps_mlp_hidden")
        ps_ss = sem("ps_demod_sums"); ps_h2 = sem("ps_mlp_out"); ps_vT = sem("ps_mlp_out_T"); ps_vec = sem("ps_vec")
        ps_tb = sem("ps_table_shifts")
        vs_par = sem("vs_params"); vs_sq = sem("vs_squares"); vs_ss = sem("vs_demod_sums"); vs_aw = sem("vs_aw")
        vs_w1 = sem("vs_w1_scaled"); vs_mlp = sem("vs_mlp_hidden"); vs_u = sem("vs_u"); vs_mv = sem("vs_mlp_variance")
        vs_vec = sem("vs_mlp_out"); vs_vT = sem("vs_mlp_out_T"); vs_row = sem("vs_vec_rows")
        vs_parts = sem("vs_parts"); vs_seq = sem("vs_seq")
        as_aw = sem("as_aw_exp"); as_mx = sem("as_mlp_pre"); as_mth = sem("as_mlp_tanh")
        gs_dem = sem("gs_demod"); gs_rs = sem("gs_mlp_rstd"); g_pw = sem("g_pw_now")
        d_x = sem("x_loaded"); d_x1w = sem("x1_stored"); d_x1r = sem("x1_back"); d_kxw = sem("kx_stored")
        d_td = sem("keys_loaded"); d_bdk = sem("key_blocks_loaded"); d_v = sem("values_loaded")
        d_exw = sem("exp_stored"); d_bde = sem("exp_blocks_loaded"); d_ow = sem("av_stored"); d_or = sem("attnT_loaded")
        d_idx = sem("indices_loaded"); d_pw = [sem(f"pw_gathered{i}") for i in range(NT)]; d_out = sem("out_stored")
        p_xT = sem("p_xT"); p_down = sem("p_down"); p_db = sem("p_db"); p_up = sem("p_up"); p_ub = sem("p_ub")
        p_u = sem("p_u"); p_v1 = sem("p_v1"); p_kx = sem("p_kx"); p_g = sem("p_scores"); 
        p_av = sem("p_av"); p_o = sem("p_o"); p_x2k = sem("p_x2k"); p_xnT = sem("p_xnT"); p_tg = sem("p_tm_gain")
        p_sg = sem("p_ms_gain"); p_cg = sem("p_cp_gain"); p_hnT = sem("p_hnT"); p_hx = sem("p_hid_x")
        p_ht = sem("p_hid_t"); p_hs = sem("p_hid_s"); p_hid = sem("p_hid"); p_y = sem("p_y")
        a_xT = sem("a_xT"); a_act0 = sem("a_act0"); a_kx = sem("a_kx"); a_ex = sem("a_ex"); a_x2k = sem("a_x2k")
        a_xnT = sem("a_xnT"); a_hnT = sem("a_hnT"); a_th = sem("a_th"); a_hid = sem("a_hid")
        v_t1 = sem("v_t1"); v_row_in = sem("v_row_in"); v_t2 = sem("v_t2"); v_max = sem("v_max")
        v_dif = sem("v_dif"); v_row_mid = sem("v_row_mid"); v_up = sem("v_up"); v_x0a = sem("v_x0a")
        v_x0 = sem("v_x0"); v_u1 = sem("v_u1"); v_x1 = sem("v_x1"); v_ys = sem("v_ys"); v_kx = sem("v_kx")
        v_o = sem("v_o"); v_x2 = sem("v_x2"); v_bn = [sem(f"v_bn{i}") for i in range(3)]
        v_mv = [sem(f"v_mv{i}") for i in range(3)]; v_xn = sem("v_xn"); v_h1a = sem("v_h1a"); v_h1 = sem("v_h1")
        v_hn = sem("v_hn"); v_tT = sem("v_tT"); v_sT = sem("v_sT"); v_hT = sem("v_hT"); v_hid = sem("v_hid")
        v_rz = sem("v_rz"); v_av = sem("v_av"); v_yn = sem("v_yn"); v_yg = sem("v_yg")
        g_uc = sem("g_u_chunk"); g_oh = sem("g_onehot"); g_ind = sem("g_ind"); g_ao = sem("g_ao")
        g_ve = [sem(f"g_ve{i}") for i in range(3)]; g_rs = [sem(f"g_rstd{i}") for i in range(3)]
        g_x2b = sem("g_x2b"); g_y = sem("g_y")

        def after(eng, s, c, n=1):
            if isinstance(c, int) and c < 0:
                return
            eng.wait_ge(s, (c + 1) * n)

        def settled(eng):
            eng.sem_inc(s_settled, 1)

        def per_batch(ap, rows_, c):
            return ap[:, bass.ds(c * CB, CB)].unsqueeze(2).to_broadcast([rows_, CB, S])

        def per_batch2(ap, c):
            return ap[:, :, bass.ds(c * CB, CB)].unsqueeze(3).to_broadcast([128, 2, CB, S])

        def by_batch(ap):
            return ap.rearrange("p (b s) -> p b s", s=S)

        def by_batch2(ap):
            return ap.rearrange("p a (b s) -> p a b s", s=S)

        def halves(ap):
            return ap.rearrange("p (a n) -> p a n", a=2)

        def stages(step, eng):
            step(0, None, None)
            step(1, 0, None)
            step(2, 1, 0)
            with eng.Fori(3, NC - 1) as i:
                step(i, i - 1, i - 2)
            step(NC - 1, NC - 2, NC - 3)
            step(None, NC - 1, NC - 2)
            step(None, None, NC - 1)

        block = ctx.enter_context(nc.Block())

        setup_loads = (
            (condT, t["condT"]), (c64T, t["c64T"]), (fsT, t["fsT"]),
            (dgam, t["dgam"]), (dbet, t["dbet"]), (ugam, t["ugam"]), (ubet, t["ubet"]),
            (affT[:, 0, :], t["kaffT"]), (affT[:, 1, :], t["oaffT"]), (cols[:, :], t["cols"]),
            (bdec, t["bdec"]), (bdec_last, t["bdec_last"]), (v1[:, :], t["V"]),
            (ident[:, :], t["ident"]),
            (batch_eye[:, :], t["batch_eye"]), (rowclass[:, :], t["rowclass"]),
            (w_down[:, :, 0:H0], t["down"]), (w_up[:, 0:D], t["up"]),
            (kwT[:, :, :], t["kwT"]), (owT[:, :, :], t["owT"]),
            (mw1["mem"], t["mem_W1"]), (mw1["noi"], t["noi_W1"]), (mw1["res"], t["res_W1"]),
            (aw, t["aw"].broadcast_to([128, 6])), (tabT, t["tabT"]),
            (mw2["mem"], t["mem_W2"]), (mw2["noi"], t["noi_W2"]), (mw2["res"], t["res_W2"]),
            (rows, t["rows"][0:1, 0:6, :].broadcast_to([B, 6, D])),
            (rows2, t["rows"][0:1, 6:10, :].broadcast_to([B, 4, D])),
            (w1[:, :, :], t["w1"]), (w2[:, :, :], t["w2"]),
            (last_gb[:, :, :], t["last_gb"].broadcast_to([128, 2, D])),
            (src5[:, 0:D], t["cp_g"]), (src5[:, D:2 * D], t["tm_g"]), (src3[:, 2 * D:3 * D], t["ms_g"]),
            (b2src, t["b2"]), (pw_idx[:, :], t["pw_idx"]))
        LOADED = 16 * len(setup_loads)

        @block.sync
        def _(sp):
            sp.dma_start(w_dec, t["w_dec"]).then_inc(s_wdec, 16)
            for dst, src in setup_loads:
                sp.dma_start(dst, src).then_inc(s_load, 16)
            sp.dma_start(xin[:, :, :], t["x"][:, 0:NT, :]).then_inc(d_x, 16)
            sp.wait_ge(vs_parts, 1)
            for s in range(3):
                sp.dma_start(tables[5 * s:5 * s + 5, :], parts5[:, s, :] if s < 2 else parts5l).then_inc(s_tab, 16)
                sp.dma_start(tables[15 + 3 * s:18 + 3 * s, :], parts3[:, s, :] if s < 2 else parts3l).then_inc(s_tab, 16)
                sp.dma_start(b2_parts[s:s + 1, :], b2p[:, s, :]).then_inc(s_tab, 16)
            sp.wait_ge(s_ready, 1)
            sp.wait_ge(s_zero, 1)

            def step(a, b, d):
                if d is not None:
                    after(sp, d_x1w, d, 16)
                    after(sp, v_x2, d - 1, 2)
                    sp.dma_start(x1r[:, :, :].rearrange("p a n -> p (a n)"),
                                 x1_dram[:, bass.ds(d, 1), :].rearrange("p c n -> p (c n)")).then_inc(d_x1r, 16)
                if a is not None and not (isinstance(a, int) and a == NC - 1):
                    after(sp, p_xT, a)
                    sp.dma_start(xin[:, :, :], t["x"][:, bass.ds((a + 1) * NT, NT), :]).then_inc(d_x, 16)
                if b is not None:
                    after(sp, a_ex, b)
                    settled(sp)
                    after(sp, d_bde, b - 1, 128)
                    sp.dma_start(ex_dram.rearrange("b h j s -> (b h) j s"), ex[:, :, :]).then_inc(d_exw, 16)
                    after(sp, d_exw, b, 16)
                    for q in range(CB):
                        r = slice(16 * q, 16 * q + 16)
                        sp.dma_start(bd[r, r, :], ex_dram[q].rearrange("h j s -> j h s")).then_inc(d_bde, 16)
                    after(sp, g_oh, b - 1)
                    sp.dma_start(idx_rows[0:15, :], t["c_idx"][0:1, bass.ds(b * N, N)].broadcast_to([15, N])
                                 ).then_inc(d_idx, 16)
                    sp.dma_start(idx_rows[15:24, :], t["m_idx"][0:1, bass.ds(b * N, N)].broadcast_to([9, N])
                                 ).then_inc(d_idx, 16)
                if a is not None:
                    after(sp, v_x1, a)
                    sp.dma_start(x1_dram[:, bass.ds(a, 1), :].rearrange("p c n -> p (c n)"),
                                 x1[:, :, :].rearrange("p a n -> p (a n)")).then_inc(d_x1w, 16)
                    after(sp, a_kx, a, 2)
                    settled(sp)
                    after(sp, d_v, a - 1, 128)
                    for f in range(2):
                        sp.dma_start(kx_dram[:, 8 * f:8 * f + 8, :, :].rearrange("b d h s -> (d h) b s"),
                                     kx[:, f, :].rearrange("p (b s) -> p b s", s=S)).then_inc(d_kxw, 16)
                    after(sp, d_kxw, a, 32)
                    after(sp, p_g, a - 1)
                    after(sp, d_bdk, a - 1, 128)
                    sp.dma_start(td[:, :, :], kx_dram.rearrange("b d h s -> (b d) h s")).then_inc(d_td, 16)
                if b is not None:
                    after(sp, v_av, b, 4)
                    settled(sp)
                    after(sp, d_or, b - 1, 32)
                    sp.dma_start(av_dram.rearrange("b h d s -> (b h) d s"), av[:, :, :]).then_inc(d_ow, 16)
                if a is not None:
                    after(sp, d_td, a, 16)
                    after(sp, p_av, a - 1, 4)
                    for q in range(CB):
                        r = slice(16 * q, 16 * q + 16)
                        sp.dma_start(bd[r, r, :], td[r, :, :]).then_inc(d_bdk, 16)
                if b is not None:
                    after(sp, d_ow, b, 16)
                    after(sp, p_o, b - 1)
                    for f in range(2):
                        sp.dma_start(attnT[:, f, :].rearrange("p (b s) -> p b s", s=S),
                                     av_dram[:, 8 * f:8 * f + 8, :, :].rearrange("b h d s -> (h d) b s")
                                     ).then_inc(d_or, 16)
                if a is not None:
                    for q in range(CB):
                        sp.dma_start(vt[16 * q:16 * q + 16, 0:HD, :],
                                     kx_dram[q].rearrange("d h s -> h d s")).then_inc(d_v, 16)

            stages(step, sp)
            sp.wait_ge(d_out, 16 * NC)
            sp.wait_ge(d_x1w, 16 * NC)
            sp.wait_ge(d_kxw, 32 * NC)
            sp.wait_ge(d_ow, 16 * NC)
            sp.wait_ge(d_exw, 16 * NC)

        @block.gpsimd
        def _(gp):
            gp.memset(neghalf[:, :], -0.5).then_inc(s_const, 1)
            gp.memset(w_down[:, :, H0:128], 1.0).then_inc(s_const, 1)
            gp.memset(w_up[:, D:D + H0], 1.0).then_inc(s_const, 1)
            gp.memset(ones3[:, :], 1.0).then_inc(s_const, 1)
            gp.memset(vt[:, HD:HD + 1, :], 1.0).then_inc(s_const, 1)
            gp.memset(src5[:, 2 * D:3 * D], 0.0).then_inc(s_const, 1)
            gp.memset(src3[:, 0:2 * D], 0.0).then_inc(s_const, 1)
            gp.wait_ge(s_const, 7)
            gp.wait_ge(vs_ss, 1)
            dm = demod[:, :, :, :].rearrange("p l a b -> p (l a b)")
            for l in range(2):
                q = dm[:, 128 * l:128 * l + 128]
                gp.tensor_tensor(q, q, neghalf[:, :], ALU.pow).then_inc(gs_dem, 1)
            gp.wait_ge(vs_mv, 1)
            gp.tensor_tensor(rstd[0:B, 0, 0:3], ve[0:B, 0, 0:3], neghalf[0:B, 0:3], ALU.pow).then_inc(gs_rs, 1)
            gp.wait_ge(ps_u1, 1)
            gp.memset(bd[:, :, :], 0.0).then_inc(s_zero, 1)
            gp.wait_ge(s_ready, 1)

            def rsqrt(i, c):
                after(gp, v_mv[i], c, NT)
                settled(gp)
                gp.tensor_scalar(ve[:, i, :], mv[:, i, :, 1], LN_EPS, None, ALU.add).then_inc(g_ve[i], 1)
                after(gp, g_ve[i], c)
                gp.tensor_tensor(rstd[:, i, :], ve[:, i, :], neghalf[:, 0:NT], ALU.pow).then_inc(g_rs[i], 1)

            def step(a, b, d):
                if a is not None:
                    after(gp, p_u, a - 1)
                    gp.tensor_copy(u_chunk[:, :, :, :], u_all[:, :, bass.ds(a * CB, CB), :]).then_inc(g_uc, 1)
                if d is not None:
                    after(gp, d_idx, d, 32)
                    after(gp, p_hid, d - 1)
                    settled(gp)
                    gp.tensor_scalar(onehot[:, :], idx_rows[:, :], rowclass[0:24, :], None, ALU.is_equal
                                     ).then_inc(g_oh, 1)
                    gp.tensor_copy(by_batch(ind[:, :]), per_batch(batch_eye[0:B, :], B, d)).then_inc(g_ind, 1)
                    after(gp, d_or, d, 32)
                    gp.tensor_tensor(by_batch2(attnT[:, :, :]), by_batch2(attnT[:, :, :]),
                                     per_batch2(style[:, 1, :, :], d), ALU.mult).then_inc(g_ao, 1)
                    rsqrt(0, d)
                    after(gp, v_xn, d, NT)
                    gp.tensor_tensor(x2k[:, :, :], x2k[:, :, :],
                                     last_gb[:, 1:2, :].to_broadcast([128, NT, D]), ALU.add).then_inc(g_x2b, 1)
                    rsqrt(1, d)
                if b is not None:
                    after(gp, v_h1, b - 1)
                    for j in range(NT):
                        after(gp, d_pw[j], b - 1, 16)
                    gp.tensor_copy(pw_now[:, :], pw_idx[:, bass.ds(b * NT, NT)]).then_inc(g_pw, 1)
                    after(gp, g_pw, b)
                    settled(gp)
                    for j in range(NT):
                        gp.indirect_dma_start(pwgb[:, j, :], None, t["pw_gb"],
                                              bass.IndirectOffsetOnAxis(ap=pw_now[:, j:j + 1], axis=0)
                                              ).then_inc(d_pw[j], 16)
                if d is not None:
                    rsqrt(2, d)
                    after(gp, v_yg, d)
                    after(gp, g_x2b, d)
                    gp.tensor_tensor(yn[:, :, :], yn[:, :, :], x2k[:, :, :], ALU.add).then_inc(g_y, 1)
                    after(gp, g_y, d)
                    gp.dma_start(out[:, bass.ds(d * NT, NT), :], yn[:, :, :]).then_inc(d_out, 16)

            stages(step, gp)

        @block.tensor
        def _(pe):
            mm, tr = pe.matmul, pe.transpose
            pe.wait_ge(s_load, LOADED)
            pe.wait_ge(s_const, 7)
            mm(ph[0:H0, 0:64], dgam, condT, start=True, stop=True)
            mm(ph[64:128, 64:128], condT, dbet, start=True, stop=True)
            for a in range(2):
                mm(ph[:, 128 + 64 * a:192 + 64 * a], ugam[:, 128 * a:128 * a + 128], condT, start=True, stop=True)
            for l in range(2):
                for a in range(2):
                    q = 256 + 64 * (2 * l + a)
                    mm(ph[:, q:q + 64], affT[:, l, 128 * a:128 * a + 128], condT, start=True, stop=True)
            mm(ph[0:B, 576:832], condT, ubet, start=True, stop=True)
            pe.wait_ge(s_wdec, 16)
            mm(ph[0:K1, 512:576], w_dec[:, :, D], condT, start=True, stop=True).then_inc(ps_par, 1)
            for m, (name, s) in enumerate(zip(MLPS, (condT, c64T, fsT))):
                for a in range(2):
                    q = 64 * (2 * m + a)
                    x = mm(pk[:, q:q + 64], mw1[name][:, 128 * a:128 * a + 128], s, start=True, stop=True)
            x.then_inc(ps_mh, 1)
            for k in range(K1):
                x = mm(pp[:, 64 * k:64 * k + 64], w_dec[:, k, 0:128], condT, start=True, stop=True)
            x.then_inc(ps_u0, 1)
            pe.wait_ge(vs_sq, 1)
            for l in range(2):
                for a in range(2):
                    q = 512 + 64 * (2 * l + a)
                    for k in range(2):
                        x = mm(pk[:, q:q + 64], sq[:, l, k, 128 * a:128 * a + 128], style2[:, l, k, :],
                               start=(k == 0), stop=(k == 1))
            x.then_inc(ps_ss, 1)
            pe.wait_ge(vs_mlp, 1)
            pe.wait_ge(vs_par, 1)
            for m, name in enumerate(MLPS):
                for k in range(2):
                    x = mm(ph[0:B, 256 * m:256 * m + 256], mx[:, m, k, :], mw2[name][:, k, :],
                           start=(k == 0), stop=(k == 1))
            x.then_inc(ps_h2, 1)
            pe.wait_ge(vs_vec, 1)
            for m in range(3):
                for a in range(2):
                    q = 64 * (2 * m + a)
                    x = tr(pk[:, q:q + 64], mvec[:, m, 128 * a:128 * a + 128], ident[0:B, 0:B])
            x.then_inc(ps_vT, 1)
            pe.wait_ge(vs_w1, 1)
            for n, (lo, hi, blk) in enumerate(((0, 5, 0), (5, 10, 2))):
                for k in range(2):
                    mm(ph[0:5, 0:D], tabT[:, k, lo:hi], w1[:, blk + k, :],
                       start=(n == 0 and k == 0), stop=(n == 1 and k == 1))
            for k in range(2):
                x = mm(ph[0:3, 512:512 + D], tabT[:, k, 10:13], w1[:, 10 + k, :], start=(k == 0), stop=(k == 1))
            x.then_inc(ps_tb, 1)
            pe.wait_ge(vs_vT, 1)
            pe.wait_ge(vs_ss, 1)
            for m in range(3):
                for k in range(2):
                    x = mm(pk[0:B, 512:768], mvT[:, m, k, :], w1[:, 4 + 2 * m + k, :],
                           start=(m == 0 and k == 0), stop=(m == 2 and k == 1))
            x.then_inc(ps_vec, 1)
            pe.wait_ge(vs_row, 1)
            pe.wait_ge(vs_parts, 1)
            for k in range(K1):
                o = pk[:, 64 * k:64 * k + 64] if k < 16 else ph[:, 64 * (k - 16):64 * (k - 16) + 64]
                x = mm(o, w_dec[:, k, 128:256], condT, start=True, stop=True)
            x.then_inc(ps_u1, 1)
            pe.wait_ge(s_ready, 1)

            def proj(dst, w, x, s):
                for o in range(2):
                    for k in range(2):
                        ins = mm(dst[:, 512 * o:512 * o + 512], w[:, k, 128 * o:128 * o + 128], x[:, k, :],
                                 start=(k == 0), stop=(k == 1))
                ins.then_inc(s, 1)

            def scores(g0, g1, b):
                for g in range(g0, g1):
                    ins = mm(pk[:, NH * g:NH * g + NH], bd[:, :, g], td[:, :, g], start=True, stop=True)
                if g1 == S:
                    ins.then_inc(p_g, 1)

            def gain(col, s):
                for o in range(2):
                    q = col + 128 * o
                    ins = mm(P01[:, 512 * o:512 * o + 512], tables[:, q:q + 128], onehot[:, :], start=True, stop=True)
                ins.then_inc(s, 1)

            def hidden(k0, x, s, stop=False):
                for o in range(2):
                    for k in range(2):
                        ins = mm(ph[:, 512 * o:512 * o + 512], w1[:, k0 + k, 128 * o:128 * o + 128], x[:, k, :],
                                 start=False, stop=stop and k == 1, skip_group_check=True)
                ins.then_inc(s, 1)

            def turn(dst, src, s):
                for j in range(NT):
                    for f in range(2):
                        q = 512 * f + 128 * j
                        ins = tr(dst[:, q:q + 128], src[:, j, 128 * f:128 * f + 128], ident[:, :])
                ins.then_inc(s, 1)

            def step(a, b, d):
                if a is not None:
                    after(pe, d_x, a, 16)
                    after(pe, v_sT, a - 3)
                    after(pe, v_hT, a - 3)
                    turn(P01, xin, p_xT)
                    after(pe, a_xT, a)
                    after(pe, a_hnT, a - 3)
                    for k in range(2):
                        ins = mm(P2, w_down[:, k, :], xT[:, k, :], start=(k == 0), stop=(k == 1))
                    ins.then_inc(p_down, 1)
                if b is not None:
                    after(pe, d_td, b, 16)
                    after(pe, d_bdk, b, 128)
                    after(pe, v_av, b - 1, 4)
                    scores(0, 16, b)
                if a is not None:
                    after(pe, v_row_in, a)
                    settled(pe)
                    mm(P3[0:H0, :], db_rows[64:128, :], row_in[64:128, :], start=True, stop=True).then_inc(p_db, 1)
                if b is not None:
                    scores(16, 32, b)
                if a is not None:
                    after(pe, a_act0, a)
                    for o in range(2):
                        mm(P01[:, 512 * o:512 * o + 512], w_up[:, 128 * o:128 * o + 128], act0[:, :],
                           start=True, stop=True)
                    mm(P2[0:B, :], w_up[:, D:D + H0], act0[:, :], start=True, stop=True).then_inc(p_up, 1)
                if b is not None:
                    scores(32, S, b)
                if d is not None:
                    after(pe, g_ao, d)
                    after(pe, v_yn, d - 1, NT)
                    proj(ph, owT, attnT, p_o)
                if a is not None:
                    after(pe, v_row_mid, a)
                    after(pe, v_t2, a)
                    for o in range(2):
                        ins = mm(P23[:, 512 * o:512 * o + 512], ub_rows[:, 128 * o:128 * o + 128], row_mid[:, :],
                                 start=True, stop=True)
                    ins.then_inc(p_ub, 1)
                if d is not None:
                    after(pe, v_x2, d, 2)
                    if a is not None:
                        after(pe, v_up, a)
                    else:
                        after(pe, v_x1, NC - 1)
                        after(pe, v_hT, d - 1)
                    for j in range(NT):
                        for f in range(2):
                            q = D * j + 128 * f
                            ins = tr(P01[:, q:q + 128], x2T[:, f, 128 * j:128 * j + 128], ident[:, :])
                    ins.then_inc(p_x2k, 1)
                if a is not None:
                    after(pe, v_x0, a)
                    after(pe, g_uc, a)
                    for q in range(CB):
                        for k in range(2):
                            ins = mm(P2[0:K1, S * q:S * q + S], u_chunk[:, k, q, :], x0[:, k, S * q:S * q + S],
                                     start=(k == 0), stop=(k == 1))
                    ins.then_inc(p_u, 1)
                if d is not None:
                    after(pe, g_ind, d)
                    after(pe, g_oh, d)
                    for o in range(2):
                        q = 3 * D + 128 * o
                        mm(ph[:, 512 * o:512 * o + 512], tables[:, q:q + 128], onehot[:, :], start=True, stop=False,
                           skip_group_check=True)
                    for o in range(2):
                        mm(ph[:, 512 * o:512 * o + 512], vec_rows[:, 128 * o:128 * o + 128], ind[:, :],
                           start=False, stop=False, skip_group_check=True)
                    hidden(4, x2T, p_hx)
                if a is not None:
                    after(pe, v_u1, a)
                    if d is not None:
                        after(pe, a_x2k, d)
                    else:
                        after(pe, v_up, a)
                    for o in range(2):
                        ins = mm(P01[:, 512 * o:512 * o + 512], v1[:, 128 * o:128 * o + 128], u1[:, :],
                                 start=True, stop=True)
                    ins.then_inc(p_v1, 1)
                if d is not None:
                    after(pe, v_xn, d, NT)
                    if a is not None:
                        after(pe, v_u1, a)
                    else:
                        after(pe, v_kx, NC - 1)
                        after(pe, a_hnT, d - 1)
                    turn(P23, xn, p_xnT)
                    if a is not None:
                        after(pe, v_x1, a)
                    else:
                        after(pe, a_x2k, d)
                    gain(D, p_tg)
                    after(pe, v_tT, d)
                    hidden(2, tT, p_ht)
                if a is not None:
                    after(pe, v_ys, a)
                    if d is not None:
                        after(pe, a_xnT, d)
                    proj(P23, kwT, ys, p_kx)
                if d is not None:
                    gain(2 * D, p_sg)
                    after(pe, v_sT, d)
                    hidden(10, xnT, p_hs)
                    after(pe, v_hn, d, NT)
                    if a is not None:
                        after(pe, v_kx, a)
                    else:
                        after(pe, a_xnT, d)
                    turn(P23, h1, p_hnT)
                    gain(0, p_cg)
                    after(pe, v_hT, d)
                    hidden(0, hnT, p_hid, stop=True)
                if b is not None:
                    after(pe, d_bde, b, 128)
                    after(pe, d_v, b, 128)
                    after(pe, v_dif, b)
                    for q in range(4):
                        if q >= 2:
                            pe.wait_ge(v_av, 4 * b + q - 1)
                        for g in range(QG):
                            o = 512 * (q % 2) + (HD + 1) * g
                            ins = mm(pk[:, o:o + HD + 1], bd[:, :, QG * q + g], vt[:, :, QG * q + g],
                                     start=True, stop=True)
                        ins.then_inc(p_av, 1)
                if d is not None:
                    after(pe, v_hid, d)
                    for j in range(NT):
                        o = ph[:, D * j:D * j + D]
                        for k in range(2):
                            mm(o, hid[:, k, 128 * j:128 * j + 128], w2[:, k, :], start=(k == 0), stop=False)
                        ins = mm(o, ones3[:, :], b2_parts[:, :], start=False, stop=True)
                    ins.then_inc(p_y, 1)

            stages(step, pe)

        @block.scalar
        def _(act):
            fn = act.activation
            act.wait_ge(vs_aw, 2)
            fn(awx[:, 0:6], aw, ACT.Exp).then_inc(as_aw, 1)
            act.wait_ge(s_load, LOADED)
            act.wait_ge(ps_mh, 1)
            for m in range(3):
                for a in range(2):
                    q = 64 * (2 * m + a)
                    fn(mx[:, m, a, :], pk[:, q:q + 64], ACT.Identity, bias=cols[:, 8 + 2 * m + a:9 + 2 * m + a]
                       ).then_inc(as_mx, 1)
            act.wait_ge(as_mx, 6)
            fn(mth, mx, ACT.Tanh, scale=0.5).then_inc(as_mth, 1)
            act.wait_ge(s_ready, 1)

            def step(a, b, d):
                if a is not None:
                    after(act, p_xT, a)
                    fn(xT[:, :, :], halves(P01), ACT.Copy).then_inc(a_xT, 1)
                    after(act, v_t2, a)
                    fn(act0[:, :], t1[:, :], ACT.Relu).then_inc(a_act0, 1)
                if b is not None:
                    after(act, v_dif, b)
                    after(act, d_exw, b - 1, 16)
                    fn(ex[:, :, :], dif[:, :].rearrange("p (s h) -> p h s", h=NH), ACT.Exp, scale=SCALE
                       ).then_inc(a_ex, 1)
                if d is not None:
                    after(act, p_x2k, d)
                    after(act, g_y, d - 1)
                    fn(x2k[:, :, :], P01.rearrange("p (j f) -> p j f", j=NT), ACT.Copy).then_inc(a_x2k, 1)
                    after(act, p_xnT, d)
                    after(act, p_hs, d - 1)
                    fn(xnT[:, :, :], halves(P23), ACT.Copy).then_inc(a_xnT, 1)
                if a is not None:
                    after(act, v_kx, a)
                    for f in range(2):
                        fn(kx[:, f, :], kx[:, f, :], ACT.Identity, bias=cols[:, 2 + f:3 + f]).then_inc(a_kx, 1)
                if d is not None:
                    after(act, p_hnT, d)
                    after(act, p_hid, d - 1)
                    fn(hnT[:, :, :], halves(P23), ACT.Copy).then_inc(a_hnT, 1)
                    after(act, p_hid, d)
                    after(act, p_y, d - 1)
                    fn(th[:, :, :], halves(ph[:, :]), ACT.Tanh, scale=0.5).then_inc(a_th, 1)
                    fn(hid[:, :, :], halves(ph[:, :]), ACT.Copy).then_inc(a_hid, 1)

            stages(step, act)

        @block.vector
        def _(ve_):
            tt, ts, stt, cp = ve_.tensor_tensor, ve_.tensor_scalar, ve_.scalar_tensor_tensor, ve_.tensor_copy
            seq = [0]

            def ordered(ins):
                seq[0] += 1
                ins.then_inc(vs_seq, 1)
                ve_.wait_ge(vs_seq, seq[0])

            ve_.wait_ge(s_load, LOADED)
            ordered(ve_.tensor_reduce(awx[:, 8:9], aw, AX.X, ALU.max))
            ts(aw, aw, awx[:, 8:9], None, ALU.subtract).then_inc(vs_aw, 2)
            tt(sq[:, 0, :, :], kwT[:, :, :], kwT[:, :, :], ALU.mult)
            ordered(tt(sq[:, 1, :, :], owT[:, :, :], owT[:, :, :], ALU.mult))
            ve_.wait_ge(as_aw, 1)
            ordered(ve_.reduce_sum(awx[:, 9:10], awx[:, 0:6], AX.X))
            ordered(ve_.reciprocal(awx[:, 10:11], awx[:, 9:10]))
            ordered(ts(awx[:, 0:6], awx[:, 0:6], awx[:, 10:11], None, ALU.mult))
            ve_.wait_ge(ps_par, 1)
            cp(dg[:, :], ph[0:H0, 0:64])
            cp(db_rows[64:128, :], ph[64:128, 64:128])
            cp(ug[:, :, :], ph[:, 128:256].rearrange("p (a b) -> p a b", a=2))
            for l in range(2):
                for a in range(2):
                    q = 256 + 64 * (2 * l + a)
                    ts(style[:, l, a, :], ph[:, q:q + 64], cols[:, 4 * l + a:4 * l + a + 1], None, ALU.add)
            cp(ub_rows[:, :], ph[0:B, 576:832])
            ts(u_last[:, :], ph[0:K1, 512:576], bdec_last, None, ALU.add).then_inc(vs_par, 1)
            ve_.wait_ge(vs_par, 1)
            ordered(tt(style2, style[:, :, :, :], style[:, :, :, :], ALU.mult))
            ve_.nop().then_inc(vs_sq, 1)
            ve_.wait_ge(as_mth, 1)
            ordered(stt(mx, mth, 1.0, mx, ALU.add, ALU.mult))
            ts(mx, mx, 0.5, None, ALU.mult).then_inc(vs_mlp, 1)
            ve_.wait_ge(ps_u0, 1)
            tt(u_all[:, 0, :, :], pp[:, 0:64 * K1].rearrange("p (k b) -> p b k", b=B),
               bdec[:, 0, :].unsqueeze(1).to_broadcast([128, B, K1]), ALU.add)
            ve_.wait_ge(ps_ss, 1)
            ts(demod[:, :, :, :], pk[:, 512:768].rearrange("p (l a b) -> p l a b", l=2, a=2), DEMOD_EPS, None,
               ALU.add).then_inc(vs_ss, 1)
            ve_.wait_ge(ps_h2, 1)
            ordered(tt(mvec, ph[0:B, 0:768].rearrange("p (m j) -> p m j", m=3), rows[:, 0:3, :], ALU.add))
            for m in range(3):
                ordered(ve_.bn_stats(stats[0:B, 0, m, :], mvec[:, m, :]))
                ordered(ve_.bn_aggr(mv[0:B, 0, m, :], stats[0:B, 0, m, :]))
            ts(ve[0:B, 0, 0:3], mv[0:B, 0, 0:3, 1], LN_EPS, None, ALU.add).then_inc(vs_mv, 1)
            for m in range(6):
                ts(w1[:, 2 * m:2 * m + 2, :], w1[:, 2 * m:2 * m + 2, :], awx[:, m:m + 1], None, ALU.mult)
            ordered(ts(w2[:, :, :], w2[:, :, :], 0.5, None, ALU.mult))
            ve_.nop().then_inc(vs_w1, 1)
            ve_.wait_ge(gs_rs, 1)
            for m in range(3):
                ordered(ts(mvec[:, m, :], mvec[:, m, :], mv[0:B, 0, m, 0:1], rstd[0:B, 0, m:m + 1],
                           ALU.subtract, ALU.mult))
            ordered(tt(mvec, mvec, rows[:, 3:6, :], ALU.mult))
            tt(mvec, mvec, rows2[:, 0:3, :], ALU.add).then_inc(vs_vec, 1)
            ve_.wait_ge(ps_vT, 1)
            cp(mvT, pk[:, 0:384].rearrange("p (m a b) -> p m a b", m=3, a=2)).then_inc(vs_vT, 1)
            ve_.wait_ge(ps_tb, 1)
            cp(src5[:, 3 * D:4 * D], ph[0:5, 0:D])
            ordered(cp(src3[:, 3 * D:4 * D], ph[0:3, 512:512 + D]))
            for src, dst in ((src5, (parts5[:, 0, :], parts5[:, 1, :], parts5l)),
                             (src3, (parts3[:, 0, :], parts3[:, 1, :], parts3l)),
                             (b2src, (b2p[:, 0, :], b2p[:, 1, :], b2p[:, 2, :]))):
                for s in range(3):
                    ordered(cp(dst[s], src))
                    if s < 2:
                        ordered(tt(src, src, dst[s], ALU.subtract))
            ve_.nop().then_inc(vs_parts, 1)
            ve_.wait_ge(ps_vec, 1)
            tt(vec_rows[:, :], pk[0:B, 512:768], rows2[:, 3, :], ALU.add).then_inc(vs_row, 1)
            ordered(tt(w1[:, 4:6, :], w1[:, 4:6, :], w1[:, 6:8, :], ALU.add))
            ordered(tt(w1[:, 4:6, :], w1[:, 4:6, :], w1[:, 8:10, :], ALU.add))
            ve_.wait_ge(ps_u1, 1)
            bd1 = bdec[:, 1, :].unsqueeze(1)
            tt(u_all[:, 1, :, 0:16], pk[:, :].rearrange("p (k b) -> p b k", b=B),
               bd1[:, :, 0:16].to_broadcast([128, B, 16]), ALU.add)
            ordered(tt(u_all[:, 1, :, 16:K1], ph[:, 0:64 * (K1 - 16)].rearrange("p (k b) -> p b k", b=B),
                       bd1[:, :, 16:K1].to_broadcast([128, B, K1 - 16]), ALU.add))
            ve_.wait_ge(s_tab, 9 * 16)
            ve_.wait_ge(gs_dem, 2)
            ve_.nop().then_inc(s_ready, 1)
            ve_.wait_ge(s_ready, 1)

            def moments(i, src, c):
                for j in range(NT):
                    ve_.bn_stats(stats[:, i, j, :], src[:, j, :]).then_inc(v_bn[i], 1)
                after(ve_, v_bn[i], c, NT)
                settled(ve_)
                for j in range(NT):
                    ve_.bn_aggr(mv[:, i, j, :], stats[:, i, j, :]).then_inc(v_mv[i], 1)

            def normalise(i, dst, src, c, s):
                after(ve_, v_mv[i], c, NT)
                after(ve_, g_rs[i], c)
                for j in range(NT):
                    ts(dst[:, j, :], src[:, j, :], mv[:, i, j, 0:1], rstd[:, i, j:j + 1], ALU.subtract, ALU.mult
                       ).then_inc(s, 1)

            def step(a, b, d):
                if a is not None:
                    after(ve_, p_down, a)
                    after(ve_, a_act0, a - 1)
                    tt(row_in[64:128, :].rearrange("p (b s) -> p b s", s=S), by_batch(P2[64:128, :]),
                       per_batch(batch_eye[64:128, :], 64, a), ALU.mult).then_inc(v_row_in, 1)
                    tt(by_batch(t1[:, :]), by_batch(P2[0:H0, :]), per_batch(dg[:, :], H0, a), ALU.mult
                       ).then_inc(v_t1, 1)
                    after(ve_, p_db, a)
                    after(ve_, v_t1, a)
                    tt(t1[:, :], t1[:, :], P3[0:H0, :], ALU.add).then_inc(v_t2, 1)
                    after(ve_, p_up, a)
                    tt(by_batch(row_mid[:, :]), by_batch(P2[0:B, :]), per_batch(batch_eye[0:B, :], B, a), ALU.mult
                       ).then_inc(v_row_mid, 1)
                    tt(by_batch2(x0[:, :, :]), by_batch2(halves(P01)), per_batch2(ug[:, :, :], a), ALU.mult
                       ).then_inc(v_up, 1)
                    after(ve_, v_up, a)
                    stt(x0[:, :, :], xT[:, :, :], 2.0, x0[:, :, :], ALU.mult, ALU.add).then_inc(v_x0a, 1)
                if b is not None:
                    after(ve_, p_g, b)
                    ve_.tensor_reduce(rowmax[:, :], pk[:, :].rearrange("p (s h) -> p s h", h=NH), AX.X, ALU.max
                                      ).then_inc(v_max, 1)
                    after(ve_, v_max, b)
                    after(ve_, a_ex, b - 1)
                    tt(dif[:, :].rearrange("p (s h) -> p s h", h=NH), pk[:, :].rearrange("p (s h) -> p s h", h=NH),
                       rowmax[:, :].unsqueeze(2).to_broadcast([128, S, NH]), ALU.subtract).then_inc(v_dif, 1)
                if d is not None:
                    after(ve_, p_o, d)
                    tt(by_batch2(tmp_o[:, :, :]), by_batch2(halves(ph[:, :])), per_batch2(demod[:, 1, :, :], d),
                       ALU.mult).then_inc(v_o, 1)
                    after(ve_, v_o, d)
                    after(ve_, d_x1r, d, 16)
                    for f in range(2):
                        stt(x2T[:, f, :], tmp_o[:, f, :], cols[:, 6 + f:7 + f], x1r[:, f, :], ALU.add, ALU.add
                            ).then_inc(v_x2, 1)
                if a is not None:
                    after(ve_, p_ub, a)
                    after(ve_, v_x0a, a)
                    tt(x0[:, :, :], x0[:, :, :], halves(P23), ALU.add).then_inc(v_x0, 1)
                if d is not None:
                    after(ve_, a_x2k, d)
                    moments(0, x2k, d)
                if a is not None:
                    after(ve_, p_u, a)
                    tt(by_batch(u1[:, :]), by_batch(P2[0:K1, :]), per_batch(u_last[:, :], K1, a), ALU.add
                       ).then_inc(v_u1, 1)
                if d is not None:
                    normalise(0, xn, x2k, d, v_xn)
                if a is not None:
                    after(ve_, p_v1, a)
                    after(ve_, d_x1w, a - 1, 16)
                    tt(x1[:, :, :], x0[:, :, :], halves(P01), ALU.add).then_inc(v_x1, 1)
                    after(ve_, v_x1, a)
                    tt(by_batch2(ys[:, :, :]), by_batch2(x1[:, :, :]), per_batch2(style[:, 0, :, :], a), ALU.mult
                       ).then_inc(v_ys, 1)
                if d is not None:
                    for j in range(NT):
                        after(ve_, d_pw[j], d, 16)
                    after(ve_, v_xn, d, NT)
                    tt(h1[:, :, :], xn[:, :, :], pwgb[:, :, 0:D], ALU.mult).then_inc(v_h1a, 1)
                    after(ve_, v_h1a, d)
                    tt(h1[:, :, :], h1[:, :, :], pwgb[:, :, D:2 * D], ALU.add).then_inc(v_h1, 1)
                    after(ve_, a_xnT, d)
                    after(ve_, p_tg, d)
                    tt(tT[:, :, :], xnT[:, :, :], halves(P01), ALU.mult).then_inc(v_tT, 1)
                    after(ve_, v_h1, d)
                    moments(1, h1, d)
                    after(ve_, p_sg, d)
                    after(ve_, v_tT, d)
                    tt(xnT[:, :, :], xnT[:, :, :], halves(P01), ALU.mult).then_inc(v_sT, 1)
                if a is not None:
                    after(ve_, p_kx, a)
                    after(ve_, d_kxw, a - 1, 32)
                    tt(by_batch2(kx[:, :, :]), by_batch2(halves(P23)), per_batch2(demod[:, 0, :, :], a), ALU.mult
                       ).then_inc(v_kx, 1)
                if d is not None:
                    normalise(1, h1, h1, d, v_hn)
                    after(ve_, a_hnT, d)
                    after(ve_, p_cg, d)
                    tt(hnT[:, :, :], hnT[:, :, :], halves(P01), ALU.mult).then_inc(v_hT, 1)
                    after(ve_, a_hid, d)
                    after(ve_, a_th, d)
                    stt(hid[:, :, :], th[:, :, :], 1.0, hid[:, :, :], ALU.add, ALU.mult).then_inc(v_hid, 1)
                if b is not None:
                    after(ve_, d_ow, b - 1, 16)
                    for q in range(4):
                        ve_.wait_ge(p_av, 4 * b + q + 1)
                        pkq = pk[:, 512 * (q % 2):512 * (q % 2) + (HD + 1) * QG].rearrange("p (s e) -> p e s", e=HD + 1)
                        ve_.reciprocal(rz[:, q, :], pkq[:, HD, :]).then_inc(v_rz, 1)
                        ve_.wait_ge(v_rz, 4 * b + q + 1)
                        tt(av[:, :, QG * q:QG * q + QG], pkq[:, 0:HD, :],
                           rz[:, q:q + 1, :].to_broadcast([128, HD, QG]), ALU.mult).then_inc(v_av, 1)
                if d is not None:
                    after(ve_, p_y, d)
                    y = ph[:, :].rearrange("p (j f) -> p j f", j=NT)
                    moments(2, y, d)
                    after(ve_, d_out, d - 1, 16)
                    normalise(2, yn, y, d, v_yn)
                    after(ve_, v_yn, d, NT)
                    tt(yn[:, :, :], yn[:, :, :], last_gb[:, 0:1, :].to_broadcast([128, NT, D]), ALU.mult
                       ).then_inc(v_yg, 1)

            stages(step, ve_)


def kernel(**inputs):
    import numpy as np
    import concourse.bacc as bacc
    from concourse.bass_utils import run_bass_kernel_spmd

    g = {k: np.asarray(v) for k, v in inputs.items()}
    p3 = lambda k: g["L3_cond_" + k]
    split = lambda a: a.reshape(2, 128, -1).transpose(1, 0, 2)
    col = lambda a: a.reshape(2, 128).T
    kperm = lambda a: a.reshape(NH, HD, -1).transpose(1, 0, 2).reshape(D, -1)
    f = np.float32
    w_dec = g["L1_cond_W_dec"].reshape(128, D + 1, K1)
    b_dec = g["L1_cond_b_dec"].reshape(D + 1, K1)
    rowclass = np.zeros((128, 1), f)
    rowclass[0:15, 0] = np.tile(np.arange(5), 3)
    rowclass[15:24, 0] = np.tile(np.arange(3), 3)
    arrays = {
        "x": g["x"].reshape(NC * NT, 128, D).transpose(1, 0, 2),
        "ident": np.eye(128, dtype=f),
        "batch_eye": np.tile(np.eye(B, dtype=f), (2, 1)),
        "rowclass": rowclass,
        "condT": g["cond_512"].T, "c64T": g["cond_64"].T, "fsT": g["fside_Bx32_0"].T,
        "dgam": g["L0_cond_down_gamma"], "dbet": g["L0_cond_down_beta"],
        "ugam": g["L0_cond_up_gamma"], "ubet": g["L0_cond_up_beta"],
        "down": split(g["L0_cond_down_project"]), "up": g["L0_cond_up_project"],
        "w_dec": w_dec.transpose(0, 2, 1), "bdec": b_dec[:D].reshape(2, 128, K1).transpose(1, 0, 2),
        "bdec_last": b_dec[D].reshape(K1, 1), "V": g["L1_cond_V"],
        "kaffT": g["L2_cond_k_aff_w"].T, "oaffT": g["L2_cond_o_aff_w"].T,
        "kwT": split(kperm(g["L2_cond_k_w"]).T), "owT": split(g["L2_cond_o_w"].T),
        "cols": np.concatenate([col(g["L2_cond_k_aff_b"]), col(kperm(g["L2_cond_k_b"])), col(g["L2_cond_o_aff_b"]),
                                col(g["L2_cond_o_b"])] + [col(p3(m + "_b1")) for m in MLPS], axis=1),
        "w1": p3("int_W1").reshape(12, 128, D).transpose(1, 0, 2), "w2": split(p3("int_W2")),
        **{m + "_W1": p3(m + "_W1") for m in MLPS}, **{m + "_W2": split(p3(m + "_W2")) for m in MLPS},
        "rows": np.stack([p3(m + k) for k in ("_b2", "_g", "_be") for m in MLPS] + [p3("int_b1")])[None],
        "last_gb": np.stack([p3("int_g"), p3("int_be")])[None], "aw": p3("aw").reshape(1, 6),
        "tabT": split(np.concatenate([p3("cp_b"), p3("tm_b"), p3("ms_b")]).T),
        "cp_g": p3("cp_g"), "tm_g": p3("tm_g"), "ms_g": p3("ms_g"), "b2": p3("int_b2").reshape(1, D),
        "pw_gb": np.concatenate([p3("pw_g"), p3("pw_b")], axis=1),
        "pw_idx": g["itok_BxS_0_999"].reshape(NC * NT, 128).T,
        "c_idx": g["itok_BxS_0_4"].reshape(1, B * S), "m_idx": g["mask_BxS_ik0"].reshape(1, B * S),
    }
    arrays = {k: np.ascontiguousarray(v) for k, v in arrays.items()}
    nc = bacc.Bacc("TRN2", target_bir_lowering=False, num_devices=1)
    t = {k: nc.dram_tensor("in_" + k, list(v.shape), mybir.dt.from_np(v.dtype), kind="ExternalInput").ap()
         for k, v in arrays.items()}
    out = nc.dram_tensor("out", [B * S, D], F32, kind="ExternalOutput").ap()
    build(nc, t, out.rearrange("(n p) f -> p n f", p=128))
    r = run_bass_kernel_spmd(nc, [{"in_" + k: v for k, v in arrays.items()}], core_ids=[0])
    return np.asarray(r.results[0]["out"]).reshape(B, S, D)
```

```python
from contextlib import ExitStack

import concourse.bass as bass
from concourse import mybir

F32 = mybir.dt.float32
BF16 = mybir.dt.bfloat16
I32 = mybir.dt.int32
ALU = mybir.AluOpType
ACT = mybir.ActivationFunctionType
AX = mybir.AxisListType

B, S, D = 64, 64, 256
CB = 8
N = CB * S
NC = B // CB
NT = N // 128
NH, HD = 16, 16
H0 = 64
K1 = 30
NP = 3
TERMS = ((0, 0), (0, 1), (1, 0), (1, 1), (0, 2), (2, 0))
LN_EPS = 1e-5
DEMOD_EPS = 1e-8
SCALE = HD ** -0.5
QG = 16
MLPS = ("mem", "noi", "res")


def build(nc, t, out):
    ctx = ExitStack()
    with ctx:
        def sb(name, shape, dt=F32):
            return ctx.enter_context(nc.sbuf_tensor(name, shape, dt))

        def sem(name):
            return ctx.enter_context(nc.semaphore(name))

        ident = sb("ident", [128, 128])
        batch_eye = sb("batch_eye", [128, B])
        rowclass = sb("rowclass", [128, 1])
        neghalf = sb("neghalf", [128, 128])
        ones3 = sb("ones3", [3, 128], BF16)
        w_down = sb("w_down", [128, 2, 128])
        w_up = sb("w_up", [H0, D + H0])
        db_rows = sb("db_rows", [128, H0])
        ub_rows = sb("ub_rows", [128, D])
        dg = sb("dg", [H0, B])
        ug = sb("ug", [128, 2, B])
        u_last = sb("u_last", [K1, B])
        v1 = sb("v1", [K1, D])
        kwT = sb("kwT", [128, 2, D])
        owT = sb("owT", [128, 2, D])
        style = sb("style", [128, 2, 2, B])
        demod = sb("demod", [128, 2, 2, B])
        cols = sb("cols", [128, 14])
        w1 = sb("w1", [128, 12, D])
        w2 = sb("w2", [128, 2, D])
        tables = sb("tables", [24, 4 * D], BF16)
        b2_parts = sb("b2_parts", [3, D], BF16)
        last_gb = sb("last_gb", [128, 2, D])
        vec_rows = sb("vec_rows", [B, D])
        pw_idx = sb("pw_idx", [128, NC * NT], I32)
        pw_now = sb("pw_now", [128, NT], I32)
        bd = sb("bd", [128, 128, NP, S], BF16)
        bd_f32 = bd[:, :, :, :].rearrange("p a c b -> p (a c b)").bitcast(F32)
        w_dec = bd_f32[:, 0:K1 * (D + 1)].rearrange("p (k i) -> p k i", k=K1)

        xin = sb("xin", [128, NT, D])
        xT = sb("xT", [128, 2, N])
        down0 = sb("down0", [128, N])
        mid0 = sb("mid0", [128, N])
        t1, row_in = down0[0:H0, :], down0[64:128, :]
        act0, row_mid = mid0[0:H0, :], mid0[64:128, :]
        x0 = sb("x0", [128, 2, N])
        u_chunk = sb("u_chunk", [128, 2, CB, 32])
        u1 = sb("u1", [K1, N])
        ys = sb("ys", [128, 2, N])
        x1 = sb("x1", [128, 2, N])
        kx = sb("kx", [128, 2, N])
        kp = sb("kp", [128, 2, CB, NP, S], BF16)
        td = sb("td", [128, NH, NP, S], BF16)
        vt = sb("vt", [128, HD + 1, NP, S], BF16)
        rowmax = sb("rowmax", [128, S])
        ex = sb("ex", [128, NH, S])
        ep = sb("ep", [128, NH, NP, S], BF16)
        rz = sb("rz", [128, 4, QG])
        av = sb("av", [128, HD, S])
        attnT = sb("attnT", [128, 2, N])
        tT = sb("tT", [128, 2, N])
        tmp_o, th = tT, tT
        x1r = sb("x1r", [128, 2, N])
        x2T = sb("x2T", [128, 2, N])
        x2k = sb("x2k", [128, NT, D])
        stats = sb("stats", [128, 3, NT, 6])
        mv = sb("mv", [128, 3, NT, 2])
        ve = sb("ve", [128, 3, NT])
        rstd = sb("rstd", [128, 3, NT])
        xn = sb("xn", [128, NT, D])
        h1 = sb("h1", [128, NT, D])
        pwgb = sb("pwgb", [128, NT, 2 * D])
        xnT = sb("xnT", [128, 2, N])
        hnT = sb("hnT", [128, 2, N])
        idx_rows = sb("idx_rows", [24, N], I32)
        onehot = sb("onehot", [24, N], BF16)
        ind = sb("ind", [B, N])
        hid = sb("hid", [128, 2, N])
        yn = h1

        ex_flat = ex[:, :, :].rearrange("p a b -> p (a b)")
        av_flat = av[:, :, :].rearrange("p a b -> p (a b)")
        u_pieces = [xT, x0, x1, ys]
        u_piece = [u[:, :, :].rearrange("p a n -> p (a n)").rearrange("p (b k) -> p b k", k=32) for u in u_pieces]
        condT = xnT[:, 0, 0:B]
        c64T = xnT[0:64, 0, 64:64 + B]
        fsT = xnT[0:32, 0, 128:128 + B]
        dgam = xnT[:, 0, 192:256]
        dbet = xnT[:, 0, 256:320]
        bdec = xnT[:, 1, 0:60].rearrange("p (a k) -> p a k", a=2)
        bdec_last = xnT[0:K1, 1, 64:65]
        aw = xnT[:, 1, 72:78]
        awx = xnT[:, 1, 80:96]
        tabT = xnT[:, 1, 96:122].rearrange("p (a r) -> p a r", a=2)
        style2 = xnT[:, 1, 128:384].rearrange("p (l a b) -> p l a b", l=2, a=2)
        ugam = hnT[:, 0, 0:D]
        ubet = hnT[:, 0, D:2 * D]
        affT = hnT[:, 1, :].rearrange("p (l i) -> p l i", l=2)
        mw1 = {"mem": hid[:, 0, 0:D], "noi": hid[0:64, 0, D:2 * D], "res": hid[0:32, 1, 0:D]}
        mw2 = {"mem": tmp_o[:, 0, :].rearrange("p (k j) -> p k j", k=2),
               "noi": tmp_o[:, 1, :].rearrange("p (k j) -> p k j", k=2),
               "res": x2T[:, 0, :].rearrange("p (k j) -> p k j", k=2)}
        sq = x1r[:, :, :].rearrange("p l (k o) -> p l k o", k=2)
        rows = pwgb[0:B, :, :].rearrange("p a b -> p (a b)")[:, 0:6 * D].rearrange("p (r j) -> p r j", r=6)
        rows2 = attnT[0:B, :, :].rearrange("p a b -> p (a b)").rearrange("p (r j) -> p r j", r=4)
        mx = ex_flat[:, 0:384].rearrange("p (m a b) -> p m a b", m=3, a=2)
        mth = ex_flat[:, 384:768].rearrange("p (m a b) -> p m a b", m=3, a=2)
        mvec = xn[0:B, 0:3, :]
        mvT = av_flat[:, 0:384].rearrange("p (m a b) -> p m a b", m=3, a=2)
        src5 = ep[0:5, :, :, :].rearrange("p a b c -> p (a b c)").bitcast(F32)[:, 0:4 * D]
        src3 = x2k[0:3, :, :].rearrange("p a b -> p (a b)")
        parts5 = h1[0:5, :, :].rearrange("p a b -> p (a b)").bitcast(BF16)[:, 0:2048].rearrange("p (s c) -> p s c", s=2)
        parts5l = av_flat[0:5, 384:896].bitcast(BF16)
        parts3 = kx[0:3, :, :].rearrange("p a b -> p (a b)").bitcast(BF16).rearrange("p (s c) -> p s c", s=2)
        parts3l = ind[0:3, :].bitcast(BF16)
        b2src = idx_rows[0:1, 0:D].bitcast(F32)
        b2p = x2T[0:1, 1, 0:3 * D // 2].bitcast(BF16).rearrange("p (s c) -> p s c", s=3)

        pp = ctx.enter_context(nc.psum_tensor("pp", [128, 4 * 512], F32))
        ph = ctx.enter_context(nc.psum_tensor("ph", [128, 1024], F32))
        pk = ctx.enter_context(nc.psum_tensor("pk", [128, 1024], F32))
        P01, P23 = pp[:, 0:1024], pp[:, 1024:2048]
        P2, P3 = pp[:, 1024:1536], pp[:, 1536:2048]

        kx_dram = nc.dram_tensor("kx_dram", [CB, HD, NH, NP * S], BF16, kind="Internal").ap()
        av_dram = nc.dram_tensor("av_dram", [CB, NH, HD, S], F32, kind="Internal").ap()
        ex_dram = nc.dram_tensor("ex_dram", [CB, NH, NH, NP * S], BF16, kind="Internal").ap()
        u_dram = nc.dram_tensor("u_dram", [128, 2, B * 32], F32, kind="Internal").ap()
        x1_dram = nc.dram_tensor("x1_dram", [128, NC, 2 * N], F32, kind="Internal").ap()

        s_load = sem("setup_loaded"); s_wdec = sem("w_dec_loaded"); s_const = sem("constants_set")
        s_tab = sem("tables_moved"); s_zero = sem("bd_zeroed"); s_ready = sem("setup_done")
        s_settled = sem("settled")
        ps_par = sem("ps_params"); ps_u0 = sem("ps_u_half0"); ps_u1 = sem("ps_u_half1"); ps_mh = sem("ps_mlp_hidden")
        ps_ss = sem("ps_demod_sums"); ps_h2 = sem("ps_mlp_out"); ps_vT = sem("ps_mlp_out_T"); ps_vec = sem("ps_vec")
        ps_tb = sem("ps_table_shifts")
        vs_par = sem("vs_params"); vs_sq = sem("vs_squares"); vs_ss = sem("vs_demod_sums"); vs_aw = sem("vs_aw")
        vs_w1 = sem("vs_w1_scaled"); vs_mlp = sem("vs_mlp_hidden"); vs_u = sem("vs_u"); d_usave = sem("u_saved"); d_u = sem("u_chunk_loaded"); vs_mv = sem("vs_mlp_variance")
        vs_vec = sem("vs_mlp_out"); vs_vT = sem("vs_mlp_out_T"); vs_row = sem("vs_vec_rows")
        vs_parts = sem("vs_parts"); vs_seq = sem("vs_seq")
        as_aw = sem("as_aw_exp"); as_mx = sem("as_mlp_pre"); as_mth = sem("as_mlp_tanh")
        gs_dem = sem("gs_demod"); gs_rs = sem("gs_mlp_rstd"); g_pw = sem("g_pw_now")
        d_x = sem("x_loaded"); d_x1w = sem("x1_stored"); d_x1r = sem("x1_back"); d_kxw = sem("kx_stored")
        d_td = sem("keys_loaded"); d_bdk = sem("key_blocks_loaded"); d_v = sem("values_loaded")
        d_exw = sem("exp_stored"); d_bde = sem("exp_blocks_loaded"); d_ow = sem("av_stored"); d_or = sem("attnT_loaded")
        d_idx = sem("indices_loaded"); d_pw = [sem(f"pw_gathered{i}") for i in range(NT)]; d_out = sem("out_stored")
        p_xT = sem("p_xT"); p_down = sem("p_down"); p_db = sem("p_db"); p_up = sem("p_up"); p_ub = sem("p_ub")
        p_u = sem("p_u"); p_v1 = sem("p_v1"); p_kx = sem("p_kx"); p_g = sem("p_scores"); 
        p_av = sem("p_av"); p_o = sem("p_o"); p_x2k = sem("p_x2k"); p_xnT = sem("p_xnT"); p_tg = sem("p_tm_gain")
        p_sg = sem("p_ms_gain"); p_cg = sem("p_cp_gain"); p_hnT = sem("p_hnT"); p_hx = sem("p_hid_x")
        p_ht = sem("p_hid_t"); p_hs = sem("p_hid_s"); p_hid = sem("p_hid"); p_y = sem("p_y")
        a_xT = sem("a_xT"); a_act0 = sem("a_act0"); a_kx = sem("a_kx"); a_ex = sem("a_ex"); a_kp0 = sem("a_kp0");
        a_kp1 = sem("a_kp1"); a_ep0 = sem("a_ep0"); a_ep1 = sem("a_ep1")
        v_er = sem("v_ex_rest"); v_ep = sem("v_ex_parts"); v_kr = sem("v_kx_rest"); v_kp = sem("v_kx_parts")
        a_x2k = sem("a_x2k")
        a_xnT = sem("a_xnT"); a_hnT = sem("a_hnT"); a_th = sem("a_th"); a_hid = sem("a_hid")
        v_t1 = sem("v_t1"); v_row_in = sem("v_row_in"); v_t2 = sem("v_t2"); v_max = sem("v_max")
        v_dif = sem("v_dif"); v_row_mid = sem("v_row_mid"); v_up = sem("v_up"); v_x0a = sem("v_x0a")
        v_x0 = sem("v_x0"); v_u1 = sem("v_u1"); v_x1 = sem("v_x1"); v_ys = sem("v_ys"); v_kx = sem("v_kx")
        v_o = sem("v_o"); v_x2 = sem("v_x2"); v_bn = [sem(f"v_bn{i}") for i in range(3)]
        v_mv = [sem(f"v_mv{i}") for i in range(3)]; v_xn = sem("v_xn"); v_h1a = sem("v_h1a"); v_h1 = sem("v_h1")
        v_hn = sem("v_hn"); v_tT = sem("v_tT"); v_sT = sem("v_sT"); v_hT = sem("v_hT"); v_hid = sem("v_hid")
        v_rz = sem("v_rz"); v_av = sem("v_av"); v_yn = sem("v_yn"); v_yg = sem("v_yg")
        g_oh = sem("g_onehot"); g_ind = sem("g_ind"); g_ao = sem("g_ao")
        g_ve = [sem(f"g_ve{i}") for i in range(3)]; g_rs = [sem(f"g_rstd{i}") for i in range(3)]
        g_x2b = sem("g_x2b"); g_y = sem("g_y")

        def after(eng, s, c, n=1):
            if isinstance(c, int) and c < 0:
                return
            eng.wait_ge(s, (c + 1) * n)

        def settled(eng):
            eng.sem_inc(s_settled, 1)

        def per_batch(ap, rows_, c):
            return ap[:, bass.ds(c * CB, CB)].unsqueeze(2).to_broadcast([rows_, CB, S])

        def per_batch2(ap, c):
            return ap[:, :, bass.ds(c * CB, CB)].unsqueeze(3).to_broadcast([128, 2, CB, S])

        def by_batch(ap):
            return ap.rearrange("p (b s) -> p b s", s=S)

        def by_batch2(ap):
            return ap.rearrange("p a (b s) -> p a b s", s=S)

        def halves(ap):
            return ap.rearrange("p (a n) -> p a n", a=2)

        def stages(step, eng):
            step(0, None, None)
            step(1, 0, None)
            step(2, 1, 0)
            with eng.Fori(3, NC - 1) as i:
                step(i, i - 1, i - 2)
            step(NC - 1, NC - 2, NC - 3)
            step(None, NC - 1, NC - 2)
            step(None, None, NC - 1)

        block = ctx.enter_context(nc.Block())

        setup_loads = (
            (condT, t["condT"]), (c64T, t["c64T"]), (fsT, t["fsT"]),
            (dgam, t["dgam"]), (dbet, t["dbet"]), (ugam, t["ugam"]), (ubet, t["ubet"]),
            (affT[:, 0, :], t["kaffT"]), (affT[:, 1, :], t["oaffT"]), (cols[:, :], t["cols"]),
            (bdec, t["bdec"]), (bdec_last, t["bdec_last"]), (v1[:, :], t["V"]),
            (ident[:, :], t["ident"]),
            (batch_eye[:, :], t["batch_eye"]), (rowclass[:, :], t["rowclass"]),
            (w_down[:, :, 0:H0], t["down"]), (w_up[:, 0:D], t["up"]),
            (kwT[:, :, :], t["kwT"]), (owT[:, :, :], t["owT"]),
            (mw1["mem"], t["mem_W1"]), (mw1["noi"], t["noi_W1"]), (mw1["res"], t["res_W1"]),
            (aw, t["aw"].broadcast_to([128, 6])), (tabT, t["tabT"]),
            (mw2["mem"], t["mem_W2"]), (mw2["noi"], t["noi_W2"]), (mw2["res"], t["res_W2"]),
            (rows, t["rows"][0:1, 0:6, :].broadcast_to([B, 6, D])),
            (rows2, t["rows"][0:1, 6:10, :].broadcast_to([B, 4, D])),
            (w1[:, :, :], t["w1"]), (w2[:, :, :], t["w2"]),
            (last_gb[:, :, :], t["last_gb"].broadcast_to([128, 2, D])),
            (src5[:, 0:D], t["cp_g"]), (src5[:, D:2 * D], t["tm_g"]), (src3[:, 2 * D:3 * D], t["ms_g"]),
            (b2src, t["b2"]), (pw_idx[:, :], t["pw_idx"]))
        LOADED = 16 * len(setup_loads)

        @block.sync
        def _(sp):
            sp.dma_start(w_dec, t["w_dec"]).then_inc(s_wdec, 16)
            for dst, src in setup_loads:
                sp.dma_start(dst, src).then_inc(s_load, 16)
            sp.dma_start(xin[:, :, :], t["x"][:, 0:NT, :]).then_inc(d_x, 16)
            sp.wait_ge(vs_parts, 1)
            for s in range(3):
                sp.dma_start(tables[5 * s:5 * s + 5, :], parts5[:, s, :] if s < 2 else parts5l).then_inc(s_tab, 16)
                sp.dma_start(tables[15 + 3 * s:18 + 3 * s, :], parts3[:, s, :] if s < 2 else parts3l).then_inc(s_tab, 16)
                sp.dma_start(b2_parts[s:s + 1, :], b2p[:, s, :]).then_inc(s_tab, 16)
            for i in range(4):
                sp.wait_ge(vs_u, i + 1)
                sp.wait_ge(s_const, 12)
                sp.dma_start(u_dram[:, i // 2, 1024 * (i % 2):1024 * (i % 2) + 1024], u_pieces[i][:, :, :].rearrange("p a n -> p (a n)")).then_inc(d_usave, 16)
            sp.wait_ge(s_ready, 1)
            sp.wait_ge(s_zero, 1)

            def step(a, b, d):
                if a is not None:
                    after(sp, p_u, a - 1)
                    sp.dma_start(u_chunk[:, :, :, :].rearrange("p i b k -> p i (b k)"),
                                 u_dram[:, :, bass.ds(a * CB * 32, CB * 32)]).then_inc(d_u, 16)
                if d is not None:
                    after(sp, d_x1w, d, 16)
                    after(sp, v_x2, d - 1, 2)
                    sp.dma_start(x1r[:, :, :].rearrange("p a n -> p (a n)"),
                                 x1_dram[:, bass.ds(d, 1), :].rearrange("p c n -> p (c n)")).then_inc(d_x1r, 16)
                if a is not None and not (isinstance(a, int) and a == NC - 1):
                    after(sp, p_xT, a)
                    sp.dma_start(xin[:, :, :], t["x"][:, bass.ds((a + 1) * NT, NT), :]).then_inc(d_x, 16)
                if b is not None:
                    after(sp, v_ep, b)
                    settled(sp)
                    after(sp, d_bde, b - 1, 128)
                    sp.dma_start(ex_dram.rearrange("b h j s -> (b h) j s"), ep[:, :, :, :].rearrange("p j c s -> p j (c s)")
                                 ).then_inc(d_exw, 16)
                    after(sp, d_exw, b, 16)
                    for q in range(CB):
                        r = slice(16 * q, 16 * q + 16)
                        sp.dma_start(bd[r, r, :, :].rearrange("j h c s -> j h (c s)"),
                                     ex_dram[q].rearrange("h j s -> j h s")).then_inc(d_bde, 16)
                    after(sp, g_oh, b - 1)
                    sp.dma_start(idx_rows[0:15, :], t["c_idx"][0:1, bass.ds(b * N, N)].broadcast_to([15, N])
                                 ).then_inc(d_idx, 16)
                    sp.dma_start(idx_rows[15:24, :], t["m_idx"][0:1, bass.ds(b * N, N)].broadcast_to([9, N])
                                 ).then_inc(d_idx, 16)
                if a is not None:
                    after(sp, v_x1, a)
                    sp.dma_start(x1_dram[:, bass.ds(a, 1), :].rearrange("p c n -> p (c n)"),
                                 x1[:, :, :].rearrange("p a n -> p (a n)")).then_inc(d_x1w, 16)
                    after(sp, v_kp, a)
                    settled(sp)
                    after(sp, d_v, a - 1, 128)
                    for f in range(2):
                        sp.dma_start(kx_dram[:, 8 * f:8 * f + 8, :, :].rearrange("b d h s -> (d h) b s"),
                                     kp[:, f, :, :, :].rearrange("p b c s -> p b (c s)")).then_inc(d_kxw, 16)
                    after(sp, d_kxw, a, 32)
                    after(sp, p_g, a - 1)
                    after(sp, d_bdk, a - 1, 128)
                    sp.dma_start(td[:, :, :, :].rearrange("p h c s -> p h (c s)"), kx_dram.rearrange("b d h s -> (b d) h s")).then_inc(d_td, 16)
                if a is not None:
                    after(sp, d_td, a, 16)
                    settled(sp)
                    after(sp, p_av, a - 1, 4)
                    for q in range(CB):
                        r = slice(16 * q, 16 * q + 16)
                        sp.dma_start(bd[r, r, :, :].rearrange("p h c s -> p h (c s)"),
                                     td[r, :, :, :].rearrange("p h c s -> p h (c s)")).then_inc(d_bdk, 16)
                if b is not None:
                    after(sp, v_av, b, 4)
                    settled(sp)
                    after(sp, d_or, b - 1, 32)
                    sp.dma_start(av_dram.rearrange("b h d s -> (b h) d s"), av[:, :, :]).then_inc(d_ow, 16)
                if b is not None:
                    after(sp, d_ow, b, 16)
                    after(sp, p_o, b - 1)
                    for f in range(2):
                        sp.dma_start(attnT[:, f, :].rearrange("p (b s) -> p b s", s=S),
                                     av_dram[:, 8 * f:8 * f + 8, :, :].rearrange("b h d s -> (h d) b s")
                                     ).then_inc(d_or, 16)
                if a is not None:
                    for q in range(CB):
                        sp.dma_start(vt[16 * q:16 * q + 16, 0:HD, :, :].rearrange("p d c s -> p d (c s)"),
                                     kx_dram[q].rearrange("d h s -> h d s")).then_inc(d_v, 16)

            stages(step, sp)
            sp.wait_ge(d_out, 16 * NC)
            sp.wait_ge(d_x1w, 16 * NC)
            sp.wait_ge(d_kxw, 32 * NC)
            sp.wait_ge(d_ow, 16 * NC)
            sp.wait_ge(d_exw, 16 * NC)

        @block.gpsimd
        def _(gp):
            gp.memset(neghalf[:, :], -0.5).then_inc(s_const, 1)
            gp.memset(w_down[:, :, H0:128], 1.0).then_inc(s_const, 1)
            gp.memset(w_up[:, D:D + H0], 1.0).then_inc(s_const, 1)
            gp.memset(ones3[:, :], 1.0).then_inc(s_const, 1)
            gp.memset(vt[:, HD:HD + 1, 0:1, :], 1.0).then_inc(s_const, 1)
            gp.memset(vt[:, HD:HD + 1, 1:NP, :], 0.0).then_inc(s_const, 1)
            gp.memset(src5[:, 2 * D:3 * D], 0.0).then_inc(s_const, 1)
            gp.memset(src3[:, 0:2 * D], 0.0).then_inc(s_const, 1)
            for i in range(4):
                gp.memset(u_piece[i][:, :, K1:32], 0.0).then_inc(s_const, 1)
            gp.wait_ge(s_const, 12)
            gp.wait_ge(vs_ss, 1)
            dm = demod[:, :, :, :].rearrange("p l a b -> p (l a b)")
            for l in range(2):
                q = dm[:, 128 * l:128 * l + 128]
                gp.tensor_tensor(q, q, neghalf[:, :], ALU.pow).then_inc(gs_dem, 1)
            gp.wait_ge(vs_mv, 1)
            gp.tensor_tensor(rstd[0:B, 0, 0:3], ve[0:B, 0, 0:3], neghalf[0:B, 0:3], ALU.pow).then_inc(gs_rs, 1)
            gp.wait_ge(ps_u1, 1)
            gp.memset(bd_f32, 0.0).then_inc(s_zero, 1)
            gp.wait_ge(s_ready, 1)

            def rsqrt(i, c):
                after(gp, v_mv[i], c, NT)
                settled(gp)
                gp.tensor_scalar(ve[:, i, :], mv[:, i, :, 1], LN_EPS, None, ALU.add).then_inc(g_ve[i], 1)
                after(gp, g_ve[i], c)
                gp.tensor_tensor(rstd[:, i, :], ve[:, i, :], neghalf[:, 0:NT], ALU.pow).then_inc(g_rs[i], 1)

            def step(a, b, d):
                if d is not None:
                    after(gp, d_or, d, 32)
                    gp.tensor_tensor(by_batch2(attnT[:, :, :]), by_batch2(attnT[:, :, :]),
                                     per_batch2(style[:, 1, :, :], d), ALU.mult).then_inc(g_ao, 1)
                    after(gp, d_idx, d, 32)
                    after(gp, p_hid, d - 1)
                    settled(gp)
                    gp.tensor_scalar(onehot[:, :], idx_rows[:, :], rowclass[0:24, :], None, ALU.is_equal
                                     ).then_inc(g_oh, 1)
                    gp.tensor_copy(by_batch(ind[:, :]), per_batch(batch_eye[0:B, :], B, d)).then_inc(g_ind, 1)
                    rsqrt(0, d)
                    after(gp, v_xn, d, NT)
                    gp.tensor_tensor(x2k[:, :, :], x2k[:, :, :],
                                     last_gb[:, 1:2, :].to_broadcast([128, NT, D]), ALU.add).then_inc(g_x2b, 1)
                    rsqrt(1, d)
                if b is not None:
                    after(gp, v_h1, b - 1)
                    for j in range(NT):
                        after(gp, d_pw[j], b - 1, 16)
                    gp.tensor_copy(pw_now[:, :], pw_idx[:, bass.ds(b * NT, NT)]).then_inc(g_pw, 1)
                    after(gp, g_pw, b)
                    settled(gp)
                    for j in range(NT):
                        gp.indirect_dma_start(pwgb[:, j, :], None, t["pw_gb"],
                                              bass.IndirectOffsetOnAxis(ap=pw_now[:, j:j + 1], axis=0)
                                              ).then_inc(d_pw[j], 16)
                if d is not None:
                    rsqrt(2, d)
                    after(gp, v_yg, d)
                    after(gp, g_x2b, d)
                    gp.tensor_tensor(yn[:, :, :], yn[:, :, :], x2k[:, :, :], ALU.add).then_inc(g_y, 1)
                    after(gp, g_y, d)
                    gp.dma_start(out[:, bass.ds(d * NT, NT), :], yn[:, :, :]).then_inc(d_out, 16)

            stages(step, gp)

        @block.tensor
        def _(pe):
            mm, tr = pe.matmul, pe.transpose
            pe.wait_ge(s_load, LOADED)
            pe.wait_ge(s_const, 12)
            mm(ph[0:H0, 0:64], dgam, condT, start=True, stop=True)
            mm(ph[64:128, 64:128], condT, dbet, start=True, stop=True)
            for a in range(2):
                mm(ph[:, 128 + 64 * a:192 + 64 * a], ugam[:, 128 * a:128 * a + 128], condT, start=True, stop=True)
            for l in range(2):
                for a in range(2):
                    q = 256 + 64 * (2 * l + a)
                    mm(ph[:, q:q + 64], affT[:, l, 128 * a:128 * a + 128], condT, start=True, stop=True)
            mm(ph[64:128, 576:832], condT, ubet, start=True, stop=True)
            pe.wait_ge(s_wdec, 16)
            mm(ph[0:K1, 512:576], w_dec[:, :, D], condT, start=True, stop=True).then_inc(ps_par, 1)
            for m, (name, s) in enumerate(zip(MLPS, (condT, c64T, fsT))):
                for a in range(2):
                    q = 64 * (2 * m + a)
                    x = mm(pk[:, q:q + 64], mw1[name][:, 128 * a:128 * a + 128], s, start=True, stop=True)
            x.then_inc(ps_mh, 1)
            for k in range(K1):
                x = mm(pp[:, 64 * k:64 * k + 64], w_dec[:, k, 0:128], condT, start=True, stop=True)
            x.then_inc(ps_u0, 1)
            pe.wait_ge(vs_sq, 1)
            for l in range(2):
                for a in range(2):
                    q = 512 + 64 * (2 * l + a)
                    for k in range(2):
                        x = mm(pk[:, q:q + 64], sq[:, l, k, 128 * a:128 * a + 128], style2[:, l, k, :],
                               start=(k == 0), stop=(k == 1))
            x.then_inc(ps_ss, 1)
            pe.wait_ge(vs_mlp, 1)
            pe.wait_ge(vs_par, 1)
            for m, name in enumerate(MLPS):
                for k in range(2):
                    x = mm(ph[0:B, 256 * m:256 * m + 256], mx[:, m, k, :], mw2[name][:, k, :],
                           start=(k == 0), stop=(k == 1))
            x.then_inc(ps_h2, 1)
            pe.wait_ge(vs_vec, 1)
            for m in range(3):
                for a in range(2):
                    q = 64 * (2 * m + a)
                    x = tr(pk[:, q:q + 64], mvec[:, m, 128 * a:128 * a + 128], ident[0:B, 0:B])
            x.then_inc(ps_vT, 1)
            pe.wait_ge(vs_w1, 1)
            for n, (lo, hi, blk) in enumerate(((0, 5, 0), (5, 10, 2))):
                for k in range(2):
                    mm(ph[0:5, 0:D], tabT[:, k, lo:hi], w1[:, blk + k, :],
                       start=(n == 0 and k == 0), stop=(n == 1 and k == 1))
            for k in range(2):
                x = mm(ph[0:3, 512:512 + D], tabT[:, k, 10:13], w1[:, 10 + k, :], start=(k == 0), stop=(k == 1))
            x.then_inc(ps_tb, 1)
            pe.wait_ge(vs_vT, 1)
            pe.wait_ge(vs_ss, 1)
            for m in range(3):
                for k in range(2):
                    x = mm(pk[0:B, 512:768], mvT[:, m, k, :], w1[:, 4 + 2 * m + k, :],
                           start=(m == 0 and k == 0), stop=(m == 2 and k == 1))
            x.then_inc(ps_vec, 1)
            pe.wait_ge(vs_row, 1)
            pe.wait_ge(vs_parts, 1)
            for k in range(K1):
                o = pk[:, 64 * k:64 * k + 64] if k < 16 else ph[:, 64 * (k - 16):64 * (k - 16) + 64]
                x = mm(o, w_dec[:, k, 128:256], condT, start=True, stop=True)
            x.then_inc(ps_u1, 1)
            pe.wait_ge(s_ready, 1)

            def proj(dst, w, x, s):
                for o in range(2):
                    for k in range(2):
                        ins = mm(dst[:, 512 * o:512 * o + 512], w[:, k, 128 * o:128 * o + 128], x[:, k, :],
                                 start=(k == 0), stop=(k == 1))
                ins.then_inc(s, 1)

            def scores(g0, g1, b):
                for g in range(g0, g1):
                    for n, (p, q) in enumerate(TERMS):
                        ins = mm(pk[:, NH * g:NH * g + NH], bd[:, :, p, g], td[:, :, q, g],
                                 start=(n == 0), stop=(n == len(TERMS) - 1))
                if g1 == S:
                    ins.then_inc(p_g, 1)

            def gain(dst, col, s):
                for o in range(2):
                    q = col + 128 * o
                    ins = mm(dst[:, 512 * o:512 * o + 512], tables[:, q:q + 128], onehot[:, :], start=True, stop=True)
                ins.then_inc(s, 1)

            def hidden(k0, x, s, stop=False):
                for o in range(2):
                    for k in range(2):
                        ins = mm(ph[:, 512 * o:512 * o + 512], w1[:, k0 + k, 128 * o:128 * o + 128], x[:, k, :],
                                 start=False, stop=stop and k == 1, skip_group_check=True)
                ins.then_inc(s, 1)

            def turn(dst, src, s):
                for j in range(NT):
                    for f in range(2):
                        q = 512 * f + 128 * j
                        ins = tr(dst[:, q:q + 128], src[:, j, 128 * f:128 * f + 128], ident[:, :])
                ins.then_inc(s, 1)

            def values(q, b):
                if q == 0:
                    after(pe, d_bde, b, 128)
                    after(pe, d_v, b, 128)
                    after(pe, v_dif, b)
                if q >= 2:
                    pe.wait_ge(v_av, 4 * b + q - 1)
                for g in range(QG):
                    o = 512 * (q % 2) + (HD + 1) * g
                    for n, (p, r) in enumerate(TERMS):
                        ins = mm(pk[:, o:o + HD + 1], bd[:, :, p, QG * q + g], vt[:, :, r, QG * q + g],
                                 start=(n == 0), stop=(n == len(TERMS) - 1))
                ins.then_inc(p_av, 1)

            def step(a, b, d):
                if a is not None:
                    after(pe, d_x, a, 16)
                    after(pe, v_hT, a - 3)
                    turn(P01, xin, p_xT)
                    after(pe, a_xT, a)
                    after(pe, a_hnT, a - 3)
                    for k in range(2):
                        ins = mm(P2, w_down[:, k, :], xT[:, k, :], start=(k == 0), stop=(k == 1))
                    ins.then_inc(p_down, 1)
                if b is not None:
                    after(pe, d_td, b, 16)
                    after(pe, d_bdk, b, 128)
                    after(pe, v_av, b - 1, 4)
                    scores(0, 16, b)
                if a is not None:
                    after(pe, v_row_in, a)
                    settled(pe)
                    mm(P3[0:H0, :], db_rows[64:128, :], row_in, start=True, stop=True).then_inc(p_db, 1)
                if b is not None:
                    scores(16, 40, b)
                if a is not None:
                    after(pe, a_act0, a)
                    for o in range(2):
                        mm(P01[:, 512 * o:512 * o + 512], w_up[:, 128 * o:128 * o + 128], act0,
                           start=True, stop=True)
                    mm(P2[64:128, :], w_up[:, D:D + H0], act0, start=True, stop=True).then_inc(p_up, 1)
                if b is not None:
                    scores(40, S, b)
                if a is not None:
                    after(pe, v_row_mid, a)
                    after(pe, v_t2, a)
                    for o in range(2):
                        ins = mm(P23[:, 512 * o:512 * o + 512], ub_rows[64:128, 128 * o:128 * o + 128], row_mid,
                                 start=True, stop=True)
                    ins.then_inc(p_ub, 1)
                if d is not None:
                    after(pe, g_ao, d)
                    after(pe, v_yn, d - 1, NT)
                    proj(ph, owT, attnT, p_o)
                if a is not None:
                    after(pe, v_x0, a)
                    after(pe, d_u, a, 16)
                    for q in range(CB):
                        for k in range(2):
                            ins = mm(P2[0:32, S * q:S * q + S], u_chunk[:, k, q, :], x0[:, k, S * q:S * q + S],
                                     start=(k == 0), stop=(k == 1))
                    ins.then_inc(p_u, 1)
                if d is not None:
                    after(pe, v_x2, d, 2)
                    if a is None:
                        after(pe, v_hT, d - 1)
                    for j in range(NT):
                        for f in range(2):
                            q = D * j + 128 * f
                            ins = tr(P01[:, q:q + 128], x2T[:, f, 128 * j:128 * j + 128], ident[:, :])
                    ins.then_inc(p_x2k, 1)
                    after(pe, g_ind, d)
                    after(pe, g_oh, d)
                    for o in range(2):
                        q = 3 * D + 128 * o
                        mm(ph[:, 512 * o:512 * o + 512], tables[:, q:q + 128], onehot[:, :], start=True, stop=False,
                           skip_group_check=True)
                    for o in range(2):
                        mm(ph[:, 512 * o:512 * o + 512], vec_rows[:, 128 * o:128 * o + 128], ind[:, :],
                           start=False, stop=False, skip_group_check=True)
                if a is not None:
                    after(pe, v_u1, a)
                    if d is not None:
                        after(pe, a_x2k, d)
                    for o in range(2):
                        ins = mm(P01[:, 512 * o:512 * o + 512], v1[:, 128 * o:128 * o + 128], u1[:, :],
                                 start=True, stop=True)
                    ins.then_inc(p_v1, 1)
                if d is not None:
                    hidden(4, x2T, p_hx)
                if a is not None:
                    after(pe, v_ys, a)
                    proj(P23, kwT, ys, p_kx)
                if d is not None:
                    after(pe, v_xn, d, NT)
                    if a is None:
                        after(pe, a_x2k, d)
                    turn(P01, xn, p_xnT)
                if b is not None:
                    values(0, b)
                if d is not None:
                    if a is not None:
                        after(pe, v_kx, a)
                    else:
                        after(pe, v_kx, NC - 1)
                        after(pe, a_hnT, d - 1)
                    gain(P23, D, p_tg)
                    after(pe, a_xnT, d)
                    gain(P01, 2 * D, p_sg)
                if b is not None:
                    values(1, b)
                if d is not None:
                    after(pe, v_tT, d)
                    hidden(2, tT, p_ht)
                    after(pe, v_sT, d)
                    hidden(10, xnT, p_hs)
                    after(pe, v_hn, d, NT)
                    turn(P23, h1, p_hnT)
                    gain(P01, 0, p_cg)
                if b is not None:
                    values(2, b)
                if d is not None:
                    after(pe, v_hT, d)
                    hidden(0, hnT, p_hid, stop=True)
                if b is not None:
                    values(3, b)
                if d is not None:
                    after(pe, v_hid, d)
                    for j in range(NT):
                        o = ph[:, D * j:D * j + D]
                        for k in range(2):
                            mm(o, hid[:, k, 128 * j:128 * j + 128], w2[:, k, :], start=(k == 0), stop=False)
                        ins = mm(o, ones3[:, :], b2_parts[:, :], start=False, stop=True)
                    ins.then_inc(p_y, 1)

            stages(step, pe)

        @block.scalar
        def _(act):
            fn = act.activation
            act.wait_ge(vs_aw, 2)
            fn(awx[:, 0:6], aw, ACT.Exp).then_inc(as_aw, 1)
            act.wait_ge(s_load, LOADED)
            act.wait_ge(ps_mh, 1)
            for m in range(3):
                for a in range(2):
                    q = 64 * (2 * m + a)
                    fn(mx[:, m, a, :], pk[:, q:q + 64], ACT.Identity, bias=cols[:, 8 + 2 * m + a:9 + 2 * m + a]
                       ).then_inc(as_mx, 1)
            act.wait_ge(as_mx, 6)
            fn(mth, mx, ACT.Tanh, scale=0.5).then_inc(as_mth, 1)
            act.wait_ge(s_ready, 1)

            def step(a, b, d):
                if a is not None:
                    after(act, p_xT, a)
                    fn(xT[:, :, :], halves(P01), ACT.Copy).then_inc(a_xT, 1)
                    after(act, v_t2, a)
                    fn(act0, t1, ACT.Relu).then_inc(a_act0, 1)
                if b is not None:
                    after(act, v_dif, b)
                    fn(ex[:, :, :], ex[:, :, :], ACT.Exp, scale=SCALE).then_inc(a_ex, 1)
                    after(act, a_ex, b)
                    after(act, d_exw, b - 1, 16)
                    fn(ep[:, :, 0, :], ex[:, :, :], ACT.Copy).then_inc(a_ep0, 1)
                    after(act, v_er, b)
                    fn(ep[:, :, 1, :], ex[:, :, :], ACT.Copy).then_inc(a_ep1, 1)
                if d is not None:
                    after(act, p_x2k, d)
                    after(act, g_y, d - 1)
                    fn(x2k[:, :, :], P01.rearrange("p (j f) -> p j f", j=NT), ACT.Copy).then_inc(a_x2k, 1)
                    after(act, p_xnT, d)
                    after(act, p_hs, d - 1)
                    fn(xnT[:, :, :], halves(P01), ACT.Copy).then_inc(a_xnT, 1)
                if a is not None:
                    after(act, v_kx, a)
                    for f in range(2):
                        fn(kx[:, f, :], kx[:, f, :], ACT.Identity, bias=cols[:, 2 + f:3 + f]).then_inc(a_kx, 1)
                    after(act, a_kx, a, 2)
                    after(act, d_kxw, a - 1, 32)
                    fn(kp[:, :, :, 0, :], by_batch2(kx[:, :, :]), ACT.Copy).then_inc(a_kp0, 1)
                    after(act, v_kr, a)
                    fn(kp[:, :, :, 1, :], by_batch2(kx[:, :, :]), ACT.Copy).then_inc(a_kp1, 1)
                if d is not None:
                    after(act, p_hnT, d)
                    after(act, p_hid, d - 1)
                    fn(hnT[:, :, :], halves(P23), ACT.Copy).then_inc(a_hnT, 1)
                    after(act, p_hid, d)
                    after(act, p_y, d - 1)
                    fn(th[:, :, :], halves(ph[:, :]), ACT.Tanh, scale=0.5).then_inc(a_th, 1)
                    fn(hid[:, :, :], halves(ph[:, :]), ACT.Copy).then_inc(a_hid, 1)

            stages(step, act)

        @block.vector
        def _(ve_):
            tt, ts, stt, cp = ve_.tensor_tensor, ve_.tensor_scalar, ve_.scalar_tensor_tensor, ve_.tensor_copy
            seq = [0]

            def ordered(ins):
                seq[0] += 1
                ins.then_inc(vs_seq, 1)
                ve_.wait_ge(vs_seq, seq[0])

            ve_.wait_ge(s_load, LOADED)
            ordered(ve_.tensor_reduce(awx[:, 8:9], aw, AX.X, ALU.max))
            ts(aw, aw, awx[:, 8:9], None, ALU.subtract).then_inc(vs_aw, 2)
            tt(sq[:, 0, :, :], kwT[:, :, :], kwT[:, :, :], ALU.mult)
            ordered(tt(sq[:, 1, :, :], owT[:, :, :], owT[:, :, :], ALU.mult))
            ve_.wait_ge(as_aw, 1)
            ordered(ve_.reduce_sum(awx[:, 9:10], awx[:, 0:6], AX.X))
            ordered(ve_.reciprocal(awx[:, 10:11], awx[:, 9:10]))
            ordered(ts(awx[:, 0:6], awx[:, 0:6], awx[:, 10:11], None, ALU.mult))
            ve_.wait_ge(ps_par, 1)
            cp(dg[:, :], ph[0:H0, 0:64])
            cp(db_rows[64:128, :], ph[64:128, 64:128])
            cp(ug[:, :, :], ph[:, 128:256].rearrange("p (a b) -> p a b", a=2))
            for l in range(2):
                for a in range(2):
                    q = 256 + 64 * (2 * l + a)
                    ts(style[:, l, a, :], ph[:, q:q + 64], cols[:, 4 * l + a:4 * l + a + 1], None, ALU.add)
            cp(ub_rows[64:128, :], ph[64:128, 576:832])
            ts(u_last[:, :], ph[0:K1, 512:576], bdec_last, None, ALU.add).then_inc(vs_par, 1)
            ve_.wait_ge(vs_par, 1)
            ordered(tt(style2, style[:, :, :, :], style[:, :, :, :], ALU.mult))
            ve_.nop().then_inc(vs_sq, 1)
            ve_.wait_ge(as_mth, 1)
            ordered(stt(mx, mth, 1.0, mx, ALU.add, ALU.mult))
            ts(mx, mx, 0.5, None, ALU.mult).then_inc(vs_mlp, 1)
            ve_.wait_ge(ps_u0, 1)
            bd0, bd1 = bdec[:, 0, :].unsqueeze(1), bdec[:, 1, :].unsqueeze(1)
            for i in range(2):
                r = slice(32 * i, 32 * i + 32)
                tt(u_piece[i][:, :, 0:K1], pp[:, 0:64 * K1].rearrange("p (k b) -> p b k", b=B)[:, r, :],
                   bd0.to_broadcast([128, 32, K1]), ALU.add).then_inc(vs_u, 1)
            ve_.wait_ge(ps_ss, 1)
            ts(demod[:, :, :, :], pk[:, 512:768].rearrange("p (l a b) -> p l a b", l=2, a=2), DEMOD_EPS, None,
               ALU.add).then_inc(vs_ss, 1)
            ve_.wait_ge(ps_h2, 1)
            ordered(tt(mvec, ph[0:B, 0:768].rearrange("p (m j) -> p m j", m=3), rows[:, 0:3, :], ALU.add))
            for m in range(3):
                ordered(ve_.bn_stats(stats[0:B, 0, m, :], mvec[:, m, :]))
                ordered(ve_.bn_aggr(mv[0:B, 0, m, :], stats[0:B, 0, m, :]))
            ts(ve[0:B, 0, 0:3], mv[0:B, 0, 0:3, 1], LN_EPS, None, ALU.add).then_inc(vs_mv, 1)
            for m in range(6):
                ts(w1[:, 2 * m:2 * m + 2, :], w1[:, 2 * m:2 * m + 2, :], awx[:, m:m + 1], None, ALU.mult)
            ordered(ts(w2[:, :, :], w2[:, :, :], 0.5, None, ALU.mult))
            ve_.nop().then_inc(vs_w1, 1)
            ve_.wait_ge(gs_rs, 1)
            for m in range(3):
                ordered(ts(mvec[:, m, :], mvec[:, m, :], mv[0:B, 0, m, 0:1], rstd[0:B, 0, m:m + 1],
                           ALU.subtract, ALU.mult))
            ordered(tt(mvec, mvec, rows[:, 3:6, :], ALU.mult))
            tt(mvec, mvec, rows2[:, 0:3, :], ALU.add).then_inc(vs_vec, 1)
            ve_.wait_ge(ps_vT, 1)
            cp(mvT, pk[:, 0:384].rearrange("p (m a b) -> p m a b", m=3, a=2)).then_inc(vs_vT, 1)
            ve_.wait_ge(ps_tb, 1)
            cp(src5[:, 3 * D:4 * D], ph[0:5, 0:D])
            ordered(cp(src3[:, 3 * D:4 * D], ph[0:3, 512:512 + D]))
            for src, dst in ((src5, (parts5[:, 0, :], parts5[:, 1, :], parts5l)),
                             (src3, (parts3[:, 0, :], parts3[:, 1, :], parts3l)),
                             (b2src, (b2p[:, 0, :], b2p[:, 1, :], b2p[:, 2, :]))):
                for s in range(3):
                    ordered(cp(dst[s], src))
                    if s < 2:
                        ordered(tt(src, src, dst[s], ALU.subtract))
            ve_.nop().then_inc(vs_parts, 1)
            ve_.wait_ge(ps_vec, 1)
            tt(vec_rows[:, :], pk[0:B, 512:768], rows2[:, 3, :], ALU.add).then_inc(vs_row, 1)
            ordered(tt(w1[:, 4:6, :], w1[:, 4:6, :], w1[:, 6:8, :], ALU.add))
            ordered(tt(w1[:, 4:6, :], w1[:, 4:6, :], w1[:, 8:10, :], ALU.add))
            ve_.wait_ge(ps_u1, 1)
            for i in range(2):
                r = slice(32 * i, 32 * i + 32)
                tt(u_piece[2 + i][:, :, 0:16], pk[:, :].rearrange("p (k b) -> p b k", b=B)[:, r, :],
                   bd1[:, :, 0:16].to_broadcast([128, 32, 16]), ALU.add).then_inc(vs_seq, 1)
                seq[0] += 1
                tt(u_piece[2 + i][:, :, 16:K1], ph[:, 0:64 * (K1 - 16)].rearrange("p (k b) -> p b k", b=B)[:, r, :],
                   bd1[:, :, 16:K1].to_broadcast([128, 32, K1 - 16]), ALU.add).then_inc(vs_u, 1)
            ve_.wait_ge(d_usave, 64)
            ve_.wait_ge(s_tab, 9 * 16)
            ve_.wait_ge(gs_dem, 2)
            ve_.nop().then_inc(s_ready, 1)
            ve_.wait_ge(s_ready, 1)

            def moments(i, src, c):
                for j in range(NT):
                    ve_.bn_stats(stats[:, i, j, :], src[:, j, :]).then_inc(v_bn[i], 1)
                after(ve_, v_bn[i], c, NT)
                settled(ve_)
                for j in range(NT):
                    ve_.bn_aggr(mv[:, i, j, :], stats[:, i, j, :]).then_inc(v_mv[i], 1)

            def normalise(i, dst, src, c, s):
                after(ve_, v_mv[i], c, NT)
                after(ve_, g_rs[i], c)
                for j in range(NT):
                    ts(dst[:, j, :], src[:, j, :], mv[:, i, j, 0:1], rstd[:, i, j:j + 1], ALU.subtract, ALU.mult
                       ).then_inc(s, 1)

            def quotients(q, b):
                ve_.wait_ge(p_av, 4 * b + q + 1)
                if q == 0:
                    after(ve_, d_ow, b - 1, 16)
                pkq = pk[:, 512 * (q % 2):512 * (q % 2) + (HD + 1) * QG].rearrange("p (s e) -> p e s", e=HD + 1)
                ve_.reciprocal(rz[:, q, :], pkq[:, HD, :]).then_inc(v_rz, 1)
                ve_.wait_ge(v_rz, 4 * b + q + 1)
                tt(av[:, :, QG * q:QG * q + QG], pkq[:, 0:HD, :],
                   rz[:, q:q + 1, :].to_broadcast([128, HD, QG]), ALU.mult).then_inc(v_av, 1)

            def step(a, b, d):
                if a is not None:
                    after(ve_, p_down, a)
                    after(ve_, a_act0, a - 1)
                    tt(by_batch(row_in), by_batch(P2[64:128, :]),
                       per_batch(batch_eye[64:128, :], 64, a), ALU.mult).then_inc(v_row_in, 1)
                    tt(by_batch(t1), by_batch(P2[0:H0, :]), per_batch(dg[:, :], H0, a), ALU.mult
                       ).then_inc(v_t1, 1)
                    after(ve_, p_db, a)
                    after(ve_, v_t1, a)
                    tt(t1, t1, P3[0:H0, :], ALU.add).then_inc(v_t2, 1)
                    after(ve_, p_up, a)
                    tt(by_batch(row_mid), by_batch(P2[64:128, :]), per_batch(batch_eye[64:128, :], B, a), ALU.mult
                       ).then_inc(v_row_mid, 1)
                    tt(by_batch2(x0[:, :, :]), by_batch2(halves(P01)), per_batch2(ug[:, :, :], a), ALU.mult
                       ).then_inc(v_up, 1)
                    after(ve_, v_up, a)
                    stt(x0[:, :, :], xT[:, :, :], 2.0, x0[:, :, :], ALU.mult, ALU.add).then_inc(v_x0a, 1)
                if b is not None:
                    after(ve_, p_g, b)
                    ve_.tensor_reduce(rowmax[:, :], pk[:, :].rearrange("p (s h) -> p s h", h=NH), AX.X, ALU.max
                                      ).then_inc(v_max, 1)
                    after(ve_, v_max, b)
                    tt(ex[:, :, :].rearrange("p h s -> p s h"), pk[:, :].rearrange("p (s h) -> p s h", h=NH),
                       rowmax[:, :].unsqueeze(2).to_broadcast([128, S, NH]), ALU.subtract).then_inc(v_dif, 1)
                if a is not None:
                    after(ve_, p_ub, a)
                    after(ve_, v_x0a, a)
                    tt(x0[:, :, :], x0[:, :, :], halves(P23), ALU.add).then_inc(v_x0, 1)
                if b is not None:
                    after(ve_, a_ep0, b)
                    tt(ex[:, :, :], ex[:, :, :], ep[:, :, 0, :], ALU.subtract).then_inc(v_er, 1)
                if d is not None:
                    after(ve_, p_o, d)
                    tt(by_batch2(tmp_o[:, :, :]), by_batch2(halves(ph[:, :])), per_batch2(demod[:, 1, :, :], d),
                       ALU.mult).then_inc(v_o, 1)
                    after(ve_, v_o, d)
                    after(ve_, d_x1r, d, 16)
                    for f in range(2):
                        stt(x2T[:, f, :], tmp_o[:, f, :], cols[:, 6 + f:7 + f], x1r[:, f, :], ALU.add, ALU.add
                            ).then_inc(v_x2, 1)
                if b is not None:
                    after(ve_, a_ep1, b)
                    tt(ep[:, :, 2, :], ex[:, :, :], ep[:, :, 1, :], ALU.subtract).then_inc(v_ep, 1)
                if a is not None:
                    after(ve_, p_u, a)
                    tt(by_batch(u1[:, :]), by_batch(P2[0:K1, :]), per_batch(u_last[:, :], K1, a), ALU.add
                       ).then_inc(v_u1, 1)
                if d is not None:
                    after(ve_, a_x2k, d)
                    moments(0, x2k, d)
                if a is not None:
                    after(ve_, p_v1, a)
                    after(ve_, d_x1w, a - 1, 16)
                    tt(x1[:, :, :], x0[:, :, :], halves(P01), ALU.add).then_inc(v_x1, 1)
                    after(ve_, v_x1, a)
                    tt(by_batch2(ys[:, :, :]), by_batch2(x1[:, :, :]), per_batch2(style[:, 0, :, :], a), ALU.mult
                       ).then_inc(v_ys, 1)
                if d is not None:
                    normalise(0, xn, x2k, d, v_xn)
                    for j in range(NT):
                        after(ve_, d_pw[j], d, 16)
                    after(ve_, d_out, d - 1, 16)
                    after(ve_, v_xn, d, NT)
                    tt(h1[:, :, :], xn[:, :, :], pwgb[:, :, 0:D], ALU.mult).then_inc(v_h1a, 1)
                    after(ve_, v_h1a, d)
                    tt(h1[:, :, :], h1[:, :, :], pwgb[:, :, D:2 * D], ALU.add).then_inc(v_h1, 1)
                    after(ve_, v_h1, d)
                    moments(1, h1, d)
                if a is not None:
                    after(ve_, p_kx, a)
                    after(ve_, v_kp, a - 1)
                    tt(by_batch2(kx[:, :, :]), by_batch2(halves(P23)), per_batch2(demod[:, 0, :, :], a), ALU.mult
                       ).then_inc(v_kx, 1)
                if b is not None:
                    quotients(0, b)
                if d is not None:
                    after(ve_, a_xnT, d)
                    after(ve_, p_tg, d)
                    tt(tT[:, :, :], xnT[:, :, :], halves(P23), ALU.mult).then_inc(v_tT, 1)
                    after(ve_, p_sg, d)
                    after(ve_, v_tT, d)
                    tt(xnT[:, :, :], xnT[:, :, :], halves(P01), ALU.mult).then_inc(v_sT, 1)
                if b is not None:
                    quotients(1, b)
                if a is not None:
                    after(ve_, a_kp0, a)
                    tt(by_batch2(kx[:, :, :]), by_batch2(kx[:, :, :]), kp[:, :, :, 0, :], ALU.subtract
                       ).then_inc(v_kr, 1)
                if d is not None:
                    normalise(1, h1, h1, d, v_hn)
                if a is not None:
                    after(ve_, a_kp1, a)
                    tt(kp[:, :, :, 2, :], by_batch2(kx[:, :, :]), kp[:, :, :, 1, :], ALU.subtract).then_inc(v_kp, 1)
                if d is not None:
                    after(ve_, a_hnT, d)
                    after(ve_, p_cg, d)
                    tt(hnT[:, :, :], hnT[:, :, :], halves(P01), ALU.mult).then_inc(v_hT, 1)
                if b is not None:
                    quotients(2, b)
                if d is not None:
                    after(ve_, a_hid, d)
                    after(ve_, a_th, d)
                    stt(hid[:, :, :], th[:, :, :], 1.0, hid[:, :, :], ALU.add, ALU.mult).then_inc(v_hid, 1)
                if b is not None:
                    quotients(3, b)
                if d is not None:
                    after(ve_, p_y, d)
                    y = ph[:, :].rearrange("p (j f) -> p j f", j=NT)
                    moments(2, y, d)
                    normalise(2, yn, y, d, v_yn)
                    after(ve_, v_yn, d, NT)
                    tt(yn[:, :, :], yn[:, :, :], last_gb[:, 0:1, :].to_broadcast([128, NT, D]), ALU.mult
                       ).then_inc(v_yg, 1)

            stages(step, ve_)


def kernel(**inputs):
    import numpy as np
    import concourse.bacc as bacc
    from concourse.bass_utils import run_bass_kernel_spmd

    g = {k: np.asarray(v) for k, v in inputs.items()}
    p3 = lambda k: g["L3_cond_" + k]
    split = lambda a: a.reshape(2, 128, -1).transpose(1, 0, 2)
    col = lambda a: a.reshape(2, 128).T
    kperm = lambda a: a.reshape(NH, HD, -1).transpose(1, 0, 2).reshape(D, -1)
    f = np.float32
    w_dec = g["L1_cond_W_dec"].reshape(128, D + 1, K1)
    b_dec = g["L1_cond_b_dec"].reshape(D + 1, K1)
    rowclass = np.zeros((128, 1), f)
    rowclass[0:15, 0] = np.tile(np.arange(5), 3)
    rowclass[15:24, 0] = np.tile(np.arange(3), 3)
    arrays = {
        "x": g["x"].reshape(NC * NT, 128, D).transpose(1, 0, 2),
        "ident": np.eye(128, dtype=f),
        "batch_eye": np.tile(np.eye(B, dtype=f), (2, 1)),
        "rowclass": rowclass,
        "condT": g["cond_512"].T, "c64T": g["cond_64"].T, "fsT": g["fside_Bx32_0"].T,
        "dgam": g["L0_cond_down_gamma"], "dbet": g["L0_cond_down_beta"],
        "ugam": g["L0_cond_up_gamma"], "ubet": g["L0_cond_up_beta"],
        "down": split(g["L0_cond_down_project"]), "up": g["L0_cond_up_project"],
        "w_dec": w_dec.transpose(0, 2, 1), "bdec": b_dec[:D].reshape(2, 128, K1).transpose(1, 0, 2),
        "bdec_last": b_dec[D].reshape(K1, 1), "V": g["L1_cond_V"],
        "kaffT": g["L2_cond_k_aff_w"].T, "oaffT": g["L2_cond_o_aff_w"].T,
        "kwT": split(kperm(g["L2_cond_k_w"]).T), "owT": split(g["L2_cond_o_w"].T),
        "cols": np.concatenate([col(g["L2_cond_k_aff_b"]), col(kperm(g["L2_cond_k_b"])), col(g["L2_cond_o_aff_b"]),
                                col(g["L2_cond_o_b"])] + [col(p3(m + "_b1")) for m in MLPS], axis=1),
        "w1": p3("int_W1").reshape(12, 128, D).transpose(1, 0, 2), "w2": split(p3("int_W2")),
        **{m + "_W1": p3(m + "_W1") for m in MLPS}, **{m + "_W2": split(p3(m + "_W2")) for m in MLPS},
        "rows": np.stack([p3(m + k) for k in ("_b2", "_g", "_be") for m in MLPS] + [p3("int_b1")])[None],
        "last_gb": np.stack([p3("int_g"), p3("int_be")])[None], "aw": p3("aw").reshape(1, 6),
        "tabT": split(np.concatenate([p3("cp_b"), p3("tm_b"), p3("ms_b")]).T),
        "cp_g": p3("cp_g"), "tm_g": p3("tm_g"), "ms_g": p3("ms_g"), "b2": p3("int_b2").reshape(1, D),
        "pw_gb": np.concatenate([p3("pw_g"), p3("pw_b")], axis=1),
        "pw_idx": g["itok_BxS_0_999"].reshape(NC * NT, 128).T,
        "c_idx": g["itok_BxS_0_4"].reshape(1, B * S), "m_idx": g["mask_BxS_ik0"].reshape(1, B * S),
    }
    arrays = {k: np.ascontiguousarray(v) for k, v in arrays.items()}
    nc = bacc.Bacc("TRN2", target_bir_lowering=False, num_devices=1)
    t = {k: nc.dram_tensor("in_" + k, list(v.shape), mybir.dt.from_np(v.dtype), kind="ExternalInput").ap()
         for k, v in arrays.items()}
    out = nc.dram_tensor("out", [B * S, D], F32, kind="ExternalOutput").ap()
    build(nc, t, out.rearrange("(n p) f -> p n f", p=128))
    r = run_bass_kernel_spmd(nc, [{"in_" + k: v for k, v in arrays.items()}], core_ids=[0])
    return np.asarray(r.results[0]["out"]).reshape(B, S, D)
```

```python
from contextlib import ExitStack

import concourse.bass as bass
from concourse import mybir

F32 = mybir.dt.float32
BF16 = mybir.dt.bfloat16
I32 = mybir.dt.int32
ALU = mybir.AluOpType
ACT = mybir.ActivationFunctionType
AX = mybir.AxisListType

B, S, D = 64, 64, 256
CB = 8
N = CB * S
NC = B // CB
NT = N // 128
NH, HD = 16, 16
H0 = 64
K1 = 30
NP = 3
TERMS = ((0, 0), (0, 1), (1, 0), (1, 1), (0, 2), (2, 0))
LN_EPS = 1e-5
DEMOD_EPS = 1e-8
SCALE = HD ** -0.5
QG = 16
MLPS = ("mem", "noi", "res")


def build(nc, t, out):
    ctx = ExitStack()
    with ctx:
        def sb(name, shape, dt=F32):
            return ctx.enter_context(nc.sbuf_tensor(name, shape, dt))

        def sem(name):
            return ctx.enter_context(nc.semaphore(name))

        ident = sb("ident", [128, 128])
        batch_eye = sb("batch_eye", [128, B])
        rowclass = sb("rowclass", [128, 1])
        neghalf = sb("neghalf", [128, 128])
        ones3 = sb("ones3", [3, 128], BF16)
        w_down = sb("w_down", [128, 2, 128])
        w_up = sb("w_up", [H0, D + H0])
        db_rows = sb("db_rows", [128, H0])
        ub_rows = sb("ub_rows", [128, D])
        dg = sb("dg", [H0, B])
        ug = sb("ug", [128, 2, B])
        u_last = sb("u_last", [K1, B])
        v1 = sb("v1", [K1, D])
        kwT = sb("kwT", [128, 2, D])
        owT = sb("owT", [128, 2, D])
        style = sb("style", [128, 2, 2, B])
        demod = sb("demod", [128, 2, 2, B])
        cols = sb("cols", [128, 14])
        w1 = sb("w1", [128, 12, D])
        w2 = sb("w2", [128, 2, D])
        tables = sb("tables", [24, 4 * D], BF16)
        b2_parts = sb("b2_parts", [3, D], BF16)
        last_gb = sb("last_gb", [128, 2, D])
        vec_rows = sb("vec_rows", [B, D])
        pw_idx = sb("pw_idx", [128, NC * NT], I32)
        pw_now = sb("pw_now", [128, NT], I32)
        bd = sb("bd", [128, 128, NP, S], BF16)
        bd_f32 = bd[:, :, :, :].rearrange("p a c b -> p (a c b)").bitcast(F32)
        w_dec = bd_f32[:, 0:K1 * (D + 1)].rearrange("p (k i) -> p k i", k=K1)

        xin = sb("xin", [128, NT, D])
        xT = sb("xT", [128, 2, N])
        down0 = sb("down0", [128, N])
        mid0 = sb("mid0", [128, N])
        t1, row_in = down0[0:H0, :], down0[64:128, :]
        act0, row_mid = mid0[0:H0, :], mid0[64:128, :]
        x0 = sb("x0", [128, 2, N])
        u_chunk = sb("u_chunk", [128, 2, CB, 32])
        u1 = sb("u1", [K1, N])
        ys = sb("ys", [128, 2, N])
        x1 = sb("x1", [128, 2, N])
        kx = sb("kx", [128, 2, N])
        kp = sb("kp", [128, 2, CB, NP, S], BF16)
        td = sb("td", [128, NH, NP, S], BF16)
        vt = sb("vt", [128, HD + 1, NP, S], BF16)
        rowmax = sb("rowmax", [128, S])
        ex = sb("ex", [128, NH, S])
        ep = sb("ep", [128, NH, NP, S], BF16)
        rz = sb("rz", [128, 4, QG])
        av = sb("av", [128, HD, S])
        attnT = sb("attnT", [128, 2, N])
        tT = sb("tT", [128, 2, N])
        tmp_o, th = tT, tT
        x1r = sb("x1r", [128, 2, N])
        x2T = sb("x2T", [128, 2, N])
        x2k = sb("x2k", [128, NT, D])
        stats = sb("stats", [128, 3, NT, 6])
        mv = sb("mv", [128, 3, NT, 2])
        ve = sb("ve", [128, 3, NT])
        rstd = sb("rstd", [128, 3, NT])
        xn = sb("xn", [128, NT, D])
        h1 = sb("h1", [128, NT, D])
        pwgb = sb("pwgb", [128, NT, 2 * D])
        xnT = sb("xnT", [128, 2, N])
        hnT = sb("hnT", [128, 2, N])
        idx_rows = sb("idx_rows", [24, N], I32)
        onehot = sb("onehot", [24, N], BF16)
        ind = sb("ind", [B, N])
        hid = sb("hid", [128, 2, N])
        yn = h1

        def flat(ap):
            return ap.rearrange("p a b -> p (a b)")

        u_pieces = [flat(u[:, :, :]) for u in (kx, av, ex, attnT)]
        u_piece = [u.rearrange("p (b k) -> p b k", k=32) for u in u_pieces]
        condT = xnT[:, 0, 0:B]
        c64T = xnT[0:64, 0, 64:64 + B]
        fsT = xnT[0:32, 0, 128:128 + B]
        dgam = xnT[:, 0, 192:256]
        dbet = xnT[:, 0, 256:320]
        bdec = xnT[:, 1, 0:60].rearrange("p (a k) -> p a k", a=2)
        bdec_last = xnT[0:K1, 1, 64:65]
        aw = xnT[:, 1, 72:78]
        awx = xnT[:, 1, 80:96]
        tabT = xnT[:, 1, 96:122].rearrange("p (a r) -> p a r", a=2)
        style2 = xnT[:, 1, 128:384].rearrange("p (l a b) -> p l a b", l=2, a=2)
        ugam = hnT[:, 0, 0:D]
        ubet = hnT[:, 0, D:2 * D]
        affT = hnT[:, 1, :].rearrange("p (l i) -> p l i", l=2)
        mw1 = {"mem": hid[:, 0, 0:D], "noi": hid[0:64, 0, D:2 * D], "res": hid[0:32, 1, 0:D]}
        ep_f32 = ep[:, :, :, :].rearrange("p a b c -> p (a b c)").bitcast(F32)
        mw2 = {"mem": tmp_o[:, 0, :].rearrange("p (k j) -> p k j", k=2),
               "noi": tmp_o[:, 1, :].rearrange("p (k j) -> p k j", k=2),
               "res": ep_f32[:, 0:2 * D].rearrange("p (k j) -> p k j", k=2)}
        sq = x1r[:, :, :].rearrange("p l (k o) -> p l k o", k=2)
        rows = flat(pwgb[0:B, :, :])[:, 0:6 * D].rearrange("p (r j) -> p r j", r=6)
        rows2 = h1[0:B, :, :]
        mx = ep_f32[:, 512:896].rearrange("p (m a b) -> p m a b", m=3, a=2)
        mth = ep_f32[:, 896:1280].rearrange("p (m a b) -> p m a b", m=3, a=2)
        mvec = xn[0:B, 0:3, :]
        mvT = flat(x1r[:, :, :])[:, 0:384].rearrange("p (m a b) -> p m a b", m=3, a=2)
        src5 = flat(x2T[0:5, :, :])
        src3 = flat(x2k[0:3, :, :])
        parts5 = flat(hid[0:5, :, :]).bitcast(BF16).rearrange("p (s c) -> p s c", s=2)
        parts5l = tT[0:5, 0, :].bitcast(BF16)
        parts3 = flat(hnT[0:3, :, :]).bitcast(BF16).rearrange("p (s c) -> p s c", s=2)
        parts3l = ind[0:3, :].bitcast(BF16)
        b2src = x2k[32:33, 0, :]
        b2p = flat(x2k[32:33, :, :])[:, D:D + 3 * D // 2].bitcast(BF16).rearrange("p (s c) -> p s c", s=3)

        pp = ctx.enter_context(nc.psum_tensor("pp", [128, 4 * 512], F32))
        ph = ctx.enter_context(nc.psum_tensor("ph", [128, 1024], F32))
        pk = ctx.enter_context(nc.psum_tensor("pk", [128, 1024], F32))
        P01, P23 = pp[:, 0:1024], pp[:, 1024:2048]
        P0, P1, P2 = pp[:, 0:512], pp[:, 512:1024], pp[:, 1024:1536]

        kx_dram = nc.dram_tensor("kx_dram", [CB, HD, NH, NP * S], BF16, kind="Internal").ap()
        av_dram = nc.dram_tensor("av_dram", [CB, NH, HD, S], F32, kind="Internal").ap()
        ex_dram = nc.dram_tensor("ex_dram", [CB, NH, NH, NP * S], BF16, kind="Internal").ap()
        u_dram = nc.dram_tensor("u_dram", [128, 2, B * 32], F32, kind="Internal").ap()
        x1_dram = nc.dram_tensor("x1_dram", [128, NC, 2 * N], F32, kind="Internal").ap()

        s_cond = sem("conditioning_loaded"); s_load = sem("layers_loaded"); s_late = sem("late_loads")
        s_wdec = [sem("w_dec_half0"), sem("w_dec_half1")]
        s_const = sem("constants_set"); s_tab = sem("tables_moved"); s_zero = sem("bd_zeroed")
        s_settled = sem("settled")
        ps_par = sem("ps_params"); ps_u = sem("ps_u_parts"); ps_mh = sem("ps_mlp_hidden")
        ps_ss = sem("ps_demod_sums"); ps_h2 = sem("ps_mlp_out"); ps_vT = sem("ps_mlp_out_T"); ps_vec = sem("ps_vec")
        ps_tb = sem("ps_table_shifts")
        vs_par = sem("vs_params"); vs_sq = sem("vs_squares"); vs_ss = sem("vs_demod_sums"); vs_aw = sem("vs_aw")
        vs_w1 = sem("vs_w1_scaled"); vs_mlp = sem("vs_mlp_hidden"); vs_u = sem("vs_u"); d_usave = sem("u_saved")
        d_u = sem("u_chunk_loaded"); vs_mv = sem("vs_mlp_variance")
        vs_vec = sem("vs_mlp_out"); vs_vT = sem("vs_mlp_out_T"); vs_row = sem("vs_vec_rows")
        vs_parts = sem("vs_parts"); vs_seq = sem("vs_seq"); vs_last = sem("vs_setup_done")
        vs_last_u = sem("vs_u_last")
        as_aw = sem("as_aw_exp"); as_mx = sem("as_mlp_pre"); as_mth = sem("as_mlp_tanh")
        gs_dem = sem("gs_demod"); gs_rs = sem("gs_mlp_rstd"); g_pw = sem("g_pw_now")
        d_x = sem("x_loaded"); d_x1w = sem("x1_stored"); d_x1r = sem("x1_back"); d_kxw = sem("kx_stored")
        d_td = sem("keys_loaded"); d_bdk = sem("key_blocks_loaded"); d_v = sem("values_loaded")
        d_exw = sem("exp_stored"); d_bde = sem("exp_blocks_loaded"); d_ow = sem("av_stored"); d_or = sem("attnT_loaded")
        d_idx = sem("indices_loaded"); d_pw = [sem(f"pw_gathered{i}") for i in range(NT)]; d_out = sem("out_stored")
        p_xT = sem("p_xT"); p_down = sem("p_down"); p_db = sem("p_db"); p_up = sem("p_up"); p_ub = sem("p_ub")
        p_u = sem("p_u"); p_v1 = sem("p_v1"); p_kx = sem("p_kx"); p_g = sem("p_scores"); 
        p_av = sem("p_av"); p_o = sem("p_o"); p_x2k = sem("p_x2k"); p_xnT = sem("p_xnT"); p_tg = sem("p_tm_gain")
        p_sg = sem("p_ms_gain"); p_cg = sem("p_cp_gain"); p_hnT = sem("p_hnT"); p_hx = sem("p_hid_x")
        p_ht = sem("p_hid_t"); p_hs = sem("p_hid_s"); p_hid = sem("p_hid"); p_y = sem("p_y")
        a_xT = sem("a_xT"); a_act0 = sem("a_act0"); a_ex = sem("a_ex"); a_kp0 = sem("a_kp0");
        a_kp1 = sem("a_kp1"); a_ep0 = sem("a_ep0"); a_ep1 = sem("a_ep1")
        v_er = sem("v_ex_rest"); v_ep = sem("v_ex_parts"); v_kr = sem("v_kx_rest"); v_kp = sem("v_kx_parts")
        a_x2k = sem("a_x2k")
        a_xnT = sem("a_xnT"); a_hnT = sem("a_hnT"); a_th = sem("a_th")
        v_t1 = sem("v_t1"); v_row_in = sem("v_row_in"); v_t2 = sem("v_t2"); v_max = sem("v_max")
        v_dif = sem("v_dif"); v_row_mid = sem("v_row_mid"); v_up = sem("v_up"); v_x0a = sem("v_x0a")
        v_x0 = sem("v_x0"); v_u1 = sem("v_u1"); v_x1 = sem("v_x1"); v_ys = sem("v_ys"); v_kx = sem("v_kx")
        v_o = sem("v_o"); v_x2 = sem("v_x2"); v_bn = [sem(f"v_bn{i}") for i in range(3)]
        v_mv = [sem(f"v_mv{i}") for i in range(3)]; v_xn = sem("v_xn"); v_h1a = sem("v_h1a"); v_h1 = sem("v_h1")
        v_hn = sem("v_hn"); v_tT = sem("v_tT"); v_sT = sem("v_sT"); v_hT = sem("v_hT"); v_hid = sem("v_hid")
        v_rz = sem("v_rz"); v_av = sem("v_av"); v_yn = sem("v_yn"); v_yg = sem("v_yg")
        g_oh = sem("g_onehot"); g_ind = sem("g_ind"); g_ao = sem("g_ao")
        g_ve = [sem(f"g_ve{i}") for i in range(3)]; g_rs = [sem(f"g_rstd{i}") for i in range(3)]
        g_x2b = sem("g_x2b"); g_y = sem("g_y")

        def after(eng, s, c, n=1):
            if isinstance(c, int) and c < 0:
                return
            eng.wait_ge(s, (c + 1) * n)

        def settled(eng):
            eng.sem_inc(s_settled, 1)

        def per_batch(ap, rows_, c):
            return ap[:, bass.ds(c * CB, CB)].unsqueeze(2).to_broadcast([rows_, CB, S])

        def per_batch2(ap, c):
            return ap[:, :, bass.ds(c * CB, CB)].unsqueeze(3).to_broadcast([128, 2, CB, S])

        def by_batch(ap):
            return ap.rearrange("p (b s) -> p b s", s=S)

        def by_batch2(ap):
            return ap.rearrange("p a (b s) -> p a b s", s=S)

        def halves(ap):
            return ap.rearrange("p (a n) -> p a n", a=2)

        def first(c):
            return isinstance(c, int) and c == 0

        def stages(step, eng, networks=None, small_tables=None):
            step(0, None, None, None)
            if networks:
                networks()
            step(1, 0, None, None)
            if small_tables:
                small_tables()
            step(2, 1, 0, None)
            with eng.Fori(3, NC - 1) as i:
                step(i, i - 1, i - 2, i - 3)
            step(NC - 1, NC - 2, NC - 3, NC - 4)
            step(None, NC - 1, NC - 2, NC - 3)
            step(None, None, NC - 1, NC - 2)
            step(None, None, None, NC - 1)

        block = ctx.enter_context(nc.Block())

        cond_loads = (
            (condT, t["condT"]), (dgam, t["dgam"]), (dbet, t["dbet"]), (ugam, t["ugam"]), (ubet, t["ubet"]),
            (affT[:, 0, :], t["kaffT"]), (affT[:, 1, :], t["oaffT"]), (cols[:, :], t["cols"]),
            (bdec_last, t["bdec_last"]), (ident[:, :], t["ident"]))
        layer_loads = (
            (batch_eye[:, :], t["batch_eye"]), (w_down[:, :, 0:H0], t["down"]), (bdec, t["bdec"]),
            (w_up[:, 0:D], t["up"]), (kwT[:, :, :], t["kwT"]), (owT[:, :, :], t["owT"]), (v1[:, :], t["V"]))
        late_loads = (
            (c64T, t["c64T"]), (fsT, t["fsT"]), (aw, t["aw"].broadcast_to([128, 6])),
            (mw1["mem"], t["mem_W1"]), (mw1["noi"], t["noi_W1"]), (mw1["res"], t["res_W1"]),
            (mw2["mem"], t["mem_W2"]), (mw2["noi"], t["noi_W2"]), (mw2["res"], t["res_W2"]),
            (rows, t["rows"][0:1, 0:6, :].broadcast_to([B, 6, D])),
            (rows2, t["rows"][0:1, 6:10, :].broadcast_to([B, 4, D])),
            (w1[:, :, :], t["w1"]), (w2[:, :, :], t["w2"]), (tabT, t["tabT"]),
            (src5[:, 0:D], t["cp_g"]), (src5[:, D:2 * D], t["tm_g"]), (src3[:, 2 * D:3 * D], t["ms_g"]),
            (b2src, t["b2"]), (pw_idx[:, :], t["pw_idx"]), (rowclass[:, :], t["rowclass"]),
            (last_gb[:, :, :], t["last_gb"].broadcast_to([128, 2, D])))
        COND, LAYERS, LATE = 16 * len(cond_loads), 16 * len(layer_loads), 16 * len(late_loads)

        @block.sync
        def _(sp):
            for dst, src in cond_loads:
                sp.dma_start(dst, src).then_inc(s_cond, 16)
            sp.dma_start(xin[:, :, :], t["x"][:, 0:NT, :]).then_inc(d_x, 16)
            for f in range(2):
                sp.dma_start(w_dec[:, :, 128 * f:128 + f * (D - 127)],
                             t["w_dec"][:, :, 128 * f:128 + f * (D - 127)]).then_inc(s_wdec[f], 16)
            for dst, src in layer_loads:
                sp.dma_start(dst, src).then_inc(s_load, 16)
            for dst, src in late_loads:
                sp.dma_start(dst, src).then_inc(s_late, 16)
            sp.wait_ge(s_const, 12)
            for i in range(4):
                sp.wait_ge(vs_u, 4 * (i // 2) + 4)
                sp.dma_start(u_dram[:, i // 2, 1024 * (i % 2):1024 * (i % 2) + 1024], u_pieces[i]
                             ).then_inc(d_usave, 16)
            sp.wait_ge(d_usave, 64)

            def small_tables():
                sp.wait_ge(vs_parts, 1)
                for s in range(3):
                    sp.dma_start(tables[5 * s:5 * s + 5, :], parts5[:, s, :] if s < 2 else parts5l
                                 ).then_inc(s_tab, 16)
                    sp.dma_start(tables[15 + 3 * s:18 + 3 * s, :], parts3[:, s, :] if s < 2 else parts3l
                                 ).then_inc(s_tab, 16)
                    sp.dma_start(b2_parts[s:s + 1, :], b2p[:, s, :]).then_inc(s_tab, 16)

            def step(a, b, d, e):
                if a is not None:
                    after(sp, p_u, a - 1)
                    sp.dma_start(u_chunk[:, :, :, :].rearrange("p i b k -> p i (b k)"),
                                 u_dram[:, :, bass.ds(a * CB * 32, CB * 32)]).then_inc(d_u, 16)
                if d is not None:
                    after(sp, d_x1w, d, 16)
                    after(sp, v_x2, d - 1, 2)
                    sp.dma_start(x1r[:, :, :].rearrange("p a n -> p (a n)"),
                                 x1_dram[:, bass.ds(d, 1), :].rearrange("p c n -> p (c n)")).then_inc(d_x1r, 16)
                if a is not None and not (isinstance(a, int) and a == NC - 1):
                    after(sp, p_xT, a)
                    sp.dma_start(xin[:, :, :], t["x"][:, bass.ds((a + 1) * NT, NT), :]).then_inc(d_x, 16)
                if b is not None:
                    after(sp, v_ep, b, 2)
                    settled(sp)
                    after(sp, d_bde, b - 1, 128)
                    sp.dma_start(ex_dram.rearrange("b h j s -> (b h) j s"),
                                 ep[:, :, :, :].rearrange("p j c s -> p j (c s)")
                                 ).then_inc(d_exw, 16)
                    after(sp, d_exw, b, 16)
                    for q in range(CB):
                        r = slice(16 * q, 16 * q + 16)
                        sp.dma_start(bd[r, r, :, :].rearrange("j h c s -> j h (c s)"),
                                     ex_dram[q].rearrange("h j s -> j h s")).then_inc(d_bde, 16)
                    after(sp, g_oh, b - 1)
                    sp.dma_start(idx_rows[0:15, :], t["c_idx"][0:1, bass.ds(b * N, N)].broadcast_to([15, N])
                                 ).then_inc(d_idx, 16)
                    sp.dma_start(idx_rows[15:24, :], t["m_idx"][0:1, bass.ds(b * N, N)].broadcast_to([9, N])
                                 ).then_inc(d_idx, 16)
                if a is not None:
                    after(sp, v_x1, a)
                    sp.dma_start(x1_dram[:, bass.ds(a, 1), :].rearrange("p c n -> p (c n)"),
                                 x1[:, :, :].rearrange("p a n -> p (a n)")).then_inc(d_x1w, 16)
                    after(sp, v_kp, a)
                    settled(sp)
                    after(sp, d_v, a - 1, 128)
                    for f in range(2):
                        sp.dma_start(kx_dram[:, 8 * f:8 * f + 8, :, :].rearrange("b d h s -> (d h) b s"),
                                     kp[:, f, :, :, :].rearrange("p b c s -> p b (c s)")).then_inc(d_kxw, 16)
                    after(sp, d_kxw, a, 32)
                    after(sp, p_g, a - 1)
                    after(sp, d_bdk, a - 1, 128)
                    sp.dma_start(td[:, :, :, :].rearrange("p h c s -> p h (c s)"),
                                 kx_dram.rearrange("b d h s -> (b d) h s")).then_inc(d_td, 16)
                    after(sp, p_av, a - 1, 4)
                    if first(a):
                        sp.wait_ge(s_zero, 1)
                    for q in range(CB):
                        r = slice(16 * q, 16 * q + 16)
                        sp.dma_start(bd[r, r, :, :].rearrange("p h c s -> p h (c s)"),
                                     kx_dram[q].rearrange("d h s -> d h s")).then_inc(d_bdk, 16)
                if b is not None:
                    after(sp, v_av, b, 4)
                    settled(sp)
                    after(sp, d_or, b - 1, 32)
                    sp.dma_start(av_dram.rearrange("b h d s -> (b h) d s"), av[:, :, :]).then_inc(d_ow, 16)
                if b is not None:
                    after(sp, d_ow, b, 16)
                    after(sp, p_o, b - 1)
                    for f in range(2):
                        sp.dma_start(attnT[:, f, :].rearrange("p (b s) -> p b s", s=S),
                                     av_dram[:, 8 * f:8 * f + 8, :, :].rearrange("b h d s -> (h d) b s")
                                     ).then_inc(d_or, 16)
                if a is not None:
                    for q in range(CB):
                        sp.dma_start(vt[16 * q:16 * q + 16, 0:HD, :, :].rearrange("p d c s -> p d (c s)"),
                                     kx_dram[q].rearrange("d h s -> h d s")).then_inc(d_v, 16)

            stages(step, sp, small_tables=small_tables)
            sp.wait_ge(d_out, 16 * NC)
            sp.wait_ge(d_x1w, 16 * NC)
            sp.wait_ge(d_kxw, 32 * NC)
            sp.wait_ge(d_ow, 16 * NC)
            sp.wait_ge(d_exw, 16 * NC)

        @block.gpsimd
        def _(gp):
            gp.memset(neghalf[:, :], -0.5).then_inc(s_const, 1)
            gp.memset(w_down[:, :, H0:128], 1.0).then_inc(s_const, 1)
            gp.memset(w_up[:, D:D + H0], 1.0).then_inc(s_const, 1)
            gp.memset(ones3[:, :], 1.0).then_inc(s_const, 1)
            gp.memset(vt[:, HD:HD + 1, 0:1, :], 1.0).then_inc(s_const, 1)
            gp.memset(vt[:, HD:HD + 1, 1:NP, :], 0.0).then_inc(s_const, 1)
            gp.memset(src5[:, 2 * D:3 * D], 0.0).then_inc(s_const, 1)
            gp.memset(src3[:, 0:2 * D], 0.0).then_inc(s_const, 1)
            for i in range(4):
                gp.memset(u_piece[i][:, :, K1:32], 0.0).then_inc(s_const, 1)
            gp.wait_ge(s_const, 12)

            def networks():
                gp.wait_ge(vs_mv, 1)
                gp.tensor_tensor(rstd[0:B, 0, 0:3], ve[0:B, 0, 0:3], neghalf[0:B, 0:3], ALU.pow).then_inc(gs_rs, 1)

            def rsqrt(i, c):
                after(gp, v_mv[i], c, NT)
                settled(gp)
                gp.tensor_scalar(ve[:, i, :], mv[:, i, :, 1], LN_EPS, None, ALU.add).then_inc(g_ve[i], 1)
                after(gp, g_ve[i], c)
                gp.tensor_tensor(rstd[:, i, :], ve[:, i, :], neghalf[:, 0:NT], ALU.pow).then_inc(g_rs[i], 1)

            def step(a, b, d, e):
                if e is not None:
                    rsqrt(2, e)
                if d is not None:
                    after(gp, d_or, d, 32)
                    gp.tensor_tensor(by_batch2(attnT[:, :, :]), by_batch2(attnT[:, :, :]),
                                     per_batch2(style[:, 1, :, :], d), ALU.mult).then_inc(g_ao, 1)
                    after(gp, d_idx, d, 32)
                    after(gp, p_hs, d - 1)
                    after(gp, p_cg, d - 1)
                    settled(gp)
                    gp.tensor_scalar(onehot[:, :], idx_rows[:, :], rowclass[0:24, :], None, ALU.is_equal
                                     ).then_inc(g_oh, 1)
                    if first(d):
                        gp.wait_ge(s_tab, 9 * 16)
                    gp.tensor_copy(by_batch(ind[:, :]), per_batch(batch_eye[0:B, :], B, d)).then_inc(g_ind, 1)
                if e is not None:
                    after(gp, v_yg, e)
                    after(gp, g_x2b, e)
                    gp.tensor_tensor(yn[:, :, :], yn[:, :, :], x2k[:, :, :], ALU.add).then_inc(g_y, 1)
                    after(gp, g_y, e)
                    gp.dma_start(out[:, bass.ds(e * NT, NT), :], yn[:, :, :]).then_inc(d_out, 16)
                if d is not None:
                    rsqrt(0, d)
                if a is not None:
                    if first(a):
                        gp.wait_ge(vs_ss, 1)
                    q = demod[:, :, :, bass.ds(a * CB, CB)]
                    gp.tensor_tensor(q, q, neghalf[:, 0:4 * CB].rearrange("p (l a b) -> p l a b", l=2, a=2), ALU.pow
                                     ).then_inc(gs_dem, 1)
                    if first(a):
                        gp.wait_ge(ps_u, 4)
                        gp.memset(bd_f32, 0.0).then_inc(s_zero, 1)
                if d is not None:
                    after(gp, v_xn, d, NT)
                    gp.tensor_tensor(x2k[:, :, :], x2k[:, :, :],
                                     last_gb[:, 1:2, :].to_broadcast([128, NT, D]), ALU.add).then_inc(g_x2b, 1)
                if b is not None:
                    if first(b):
                        gp.wait_ge(vs_vec, 1)
                        gp.wait_ge(s_late, LATE)
                    after(gp, v_h1, b - 1)
                    for j in range(NT):
                        after(gp, d_pw[j], b - 1, 16)
                    gp.tensor_copy(pw_now[:, :], pw_idx[:, bass.ds(b * NT, NT)]).then_inc(g_pw, 1)
                    after(gp, g_pw, b)
                    settled(gp)
                    for j in range(NT):
                        gp.indirect_dma_start(pwgb[:, j, :], None, t["pw_gb"],
                                              bass.IndirectOffsetOnAxis(ap=pw_now[:, j:j + 1], axis=0)
                                              ).then_inc(d_pw[j], 16)
                if d is not None:
                    rsqrt(1, d)

            stages(step, gp, networks=networks)

        @block.tensor
        def _(pe):
            mm, tr = pe.matmul, pe.transpose
            pe.wait_ge(s_cond, COND)
            mm(ph[0:H0, 0:64], dgam, condT, start=True, stop=True)
            mm(ph[64:128, 64:128], condT, dbet, start=True, stop=True)
            for a in range(2):
                mm(ph[:, 128 + 64 * a:192 + 64 * a], ugam[:, 128 * a:128 * a + 128], condT, start=True, stop=True)
            for l in range(2):
                for a in range(2):
                    q = 256 + 64 * (2 * l + a)
                    mm(ph[:, q:q + 64], affT[:, l, 128 * a:128 * a + 128], condT, start=True, stop=True)
            mm(ph[64:128, 576:832], condT, ubet, start=True, stop=True).then_inc(ps_par, 1)

            def first_factor(i):
                bank, ks = (pk, range(0, 16)) if i % 2 == 0 else (ph, range(16, K1))
                pe.wait_ge(s_wdec[i // 2], 16)
                if i == 1:
                    pe.wait_ge(vs_par, 1)
                if i >= 2:
                    pe.wait_ge(vs_u, 2 * i - 2)
                for n, k in enumerate(ks):
                    ins = mm(bank[:, 64 * n:64 * n + 64], w_dec[:, k, 128 * (i // 2):128 * (i // 2) + 128], condT,
                             start=True, stop=True)
                if i == 3:
                    ins = mm(ph[0:K1, 896:960], w_dec[:, :, D], condT, start=True, stop=True)
                ins.then_inc(ps_u, 1)

            def demod_sums():
                pe.wait_ge(vs_sq, 2)
                pe.wait_ge(vs_u, 6)
                for l in range(2):
                    for a in range(2):
                        q = 64 * (2 * l + a)
                        for k in range(2):
                            ins = mm(pk[:, q:q + 64], sq[:, l, k, 128 * a:128 * a + 128], style2[:, l, k, :],
                                     start=(k == 0), stop=(k == 1))
                ins.then_inc(ps_ss, 1)

            def networks_hidden():
                pe.wait_ge(s_late, LATE)
                pe.wait_ge(vs_ss, 1)
                for m, (name, s) in enumerate(zip(MLPS, (condT, c64T, fsT))):
                    for a in range(2):
                        q = 64 * (2 * m + a)
                        ins = mm(pk[:, q:q + 64], mw1[name][:, 128 * a:128 * a + 128], s, start=True, stop=True)
                ins.then_inc(ps_mh, 1)

            def networks_out():
                pe.wait_ge(vs_mlp, 1)
                pe.wait_ge(vs_u, 8)
                for m, name in enumerate(MLPS):
                    for k in range(2):
                        ins = mm(ph[0:B, 256 * m:256 * m + 256], mx[:, m, k, :], mw2[name][:, k, :],
                                 start=(k == 0), stop=(k == 1))
                ins.then_inc(ps_h2, 1)

            def small_tables():
                pe.wait_ge(vs_vec, 1)
                for m in range(3):
                    for a in range(2):
                        q = 64 * (2 * m + a)
                        ins = tr(ph[:, q:q + 64], mvec[:, m, 128 * a:128 * a + 128], ident[0:B, 0:B])
                ins.then_inc(ps_vT, 1)
                pe.wait_ge(vs_vT, 1)
                pe.wait_ge(vs_w1, 1)
                for n, (lo, hi, blk) in enumerate(((0, 5, 0), (5, 10, 2))):
                    for k in range(2):
                        mm(ph[0:5, 0:D], tabT[:, k, lo:hi], w1[:, blk + k, :],
                           start=(n == 0 and k == 0), stop=(n == 1 and k == 1))
                for k in range(2):
                    ins = mm(ph[0:3, D:2 * D], tabT[:, k, 10:13], w1[:, 10 + k, :], start=(k == 0), stop=(k == 1))
                ins.then_inc(ps_tb, 1)
                for m in range(3):
                    for k in range(2):
                        ins = mm(ph[0:B, 512:768], mvT[:, m, k, :], w1[:, 4 + 2 * m + k, :],
                                 start=(m == 0 and k == 0), stop=(m == 2 and k == 1))
                ins.then_inc(ps_vec, 1)

            def proj(dst, w, x, s):
                for o in range(2):
                    for k in range(2):
                        ins = mm(dst[:, 512 * o:512 * o + 512], w[:, k, 128 * o:128 * o + 128], x[:, k, :],
                                 start=(k == 0), stop=(k == 1))
                ins.then_inc(s, 1)

            def scores(g0, g1, b):
                for g in range(g0, g1):
                    for n, (p, q) in enumerate(TERMS):
                        ins = mm(pk[:, NH * g:NH * g + NH], bd[:, :, p, g], td[:, :, q, g],
                                 start=(n == 0), stop=(n == len(TERMS) - 1))
                if g1 == S:
                    ins.then_inc(p_g, 1)

            def down_shift(a):
                after(pe, v_row_in, a)
                settled(pe)
                mm(P1[0:H0, :], db_rows[64:128, :], row_in, start=True, stop=True).then_inc(p_db, 1)

            def gain(dst, col, s):
                for o in range(2):
                    q = col + 128 * o
                    ins = mm(dst[:, 512 * o:512 * o + 512], tables[:, q:q + 128], onehot[:, :], start=True, stop=True)
                ins.then_inc(s, 1)

            def hidden(k0, x, s, start=False, stop=False, between=None):
                for o in range(2):
                    for k in range(2):
                        ins = mm(ph[:, 512 * o:512 * o + 512], w1[:, k0 + k, 128 * o:128 * o + 128], x[:, k, :],
                                 start=start and k == 0, stop=stop and k == 1, skip_group_check=True)
                    if o == 0 and between:
                        between()
                ins.then_inc(s, 1)

            def turn(dst, src, s):
                for j in range(NT):
                    for f in range(2):
                        q = 512 * f + 128 * j
                        ins = tr(dst[:, q:q + 128], src[:, j, 128 * f:128 * f + 128], ident[:, :])
                ins.then_inc(s, 1)

            def values(q, b):
                if b is None:
                    return
                if q == 0:
                    after(pe, d_bde, b, 128)
                    after(pe, d_v, b, 128)
                    after(pe, v_dif, b, 2)
                if q >= 2:
                    pe.wait_ge(v_av, 4 * b + q - 1)
                for g in range(QG):
                    o = 512 * (q % 2) + (HD + 1) * g
                    for n, (p, r) in enumerate(TERMS):
                        ins = mm(pk[:, o:o + HD + 1], bd[:, :, p, QG * q + g], vt[:, :, r, QG * q + g],
                                 start=(n == 0), stop=(n == len(TERMS) - 1))
                ins.then_inc(p_av, 1)

            def step(a, b, d, e):
                if a is not None:
                    after(pe, d_x, a, 16)
                    if isinstance(a, int) and a < 3:
                        after(pe, v_kx, a - 1)
                    else:
                        after(pe, a_hnT, a - 3)
                    turn(P23, xin, p_xT)
                if first(a):
                    first_factor(0)
                if e is not None:
                    after(pe, v_hT, e)
                    hidden(0, hnT, p_hid, stop=True)
                if a is not None:
                    if first(a):
                        pe.wait_ge(s_load, LAYERS)
                        pe.wait_ge(s_const, 12)
                    after(pe, a_xT, a)
                    after(pe, v_hT, a - 3)
                    for k in range(2):
                        ins = mm(P0, w_down[:, k, :], xT[:, k, :], start=(k == 0), stop=(k == 1))
                    ins.then_inc(p_down, 1)
                if first(a):
                    first_factor(1)
                if e is not None:
                    after(pe, v_hid, e)
                    for j in range(NT):
                        o = ph[:, D * j:D * j + D]
                        for k in range(2):
                            mm(o, hid[:, k, 128 * j:128 * j + 128], w2[:, k, :], start=(k == 0), stop=False)
                        ins = mm(o, ones3[:, :], b2_parts[:, :], start=False, stop=True)
                        if j == 0 and a is not None:
                            down_shift(a)
                    ins.then_inc(p_y, 1)
                elif a is not None:
                    down_shift(a)
                if a is not None:
                    after(pe, a_act0, a)
                    for o in range(2):
                        mm(P23[:, 512 * o:512 * o + 512], w_up[:, 128 * o:128 * o + 128], act0,
                           start=True, stop=True)
                    mm(P0[64:128, :], w_up[:, D:D + H0], act0, start=True, stop=True).then_inc(p_up, 1)
                if first(a):
                    first_factor(2)
                if b is not None:
                    after(pe, d_td, b, 16)
                    after(pe, d_bdk, b, 128)
                    after(pe, v_av, b - 1, 4)
                    scores(0, 5 if a is not None else S, b)
                if a is not None:
                    after(pe, v_row_mid, a)
                    after(pe, v_t2, a)
                    for o in range(2):
                        ins = mm(P01[:, 512 * o:512 * o + 512], ub_rows[64:128, 128 * o:128 * o + 128], row_mid,
                                 start=True, stop=True)
                    ins.then_inc(p_ub, 1)
                if first(a):
                    first_factor(3)
                    demod_sums()
                    networks_hidden()
                if a is not None and b is not None:
                    scores(5, 8, b)
                if d is not None:
                    after(pe, g_ao, d)
                    after(pe, v_yn, d - 1, NT)
                    if first(d):
                        pe.wait_ge(vs_row, 1)
                    proj(ph, owT, attnT, p_o)
                if a is not None and b is not None:
                    scores(8, 30, b)
                if d is not None:
                    after(pe, v_x2, d, 2)
                    if a is not None:
                        after(pe, v_x0, a)
                    else:
                        after(pe, a_hnT, d - 1)
                        after(pe, v_kx, NC - 1)
                    for j in range(NT):
                        for f in range(2):
                            q = D * j + 128 * f
                            ins = tr(P23[:, q:q + 128], x2T[:, f, 128 * j:128 * j + 128], ident[:, :])
                    ins.then_inc(p_x2k, 1)
                if a is not None and b is not None:
                    scores(30, S, b)
                if a is not None:
                    after(pe, v_x0, a)
                    after(pe, d_u, a, 16)
                    if d is not None:
                        after(pe, a_x2k, d)
                    for q in range(CB):
                        for k in range(2):
                            ins = mm(P2[0:32, S * q:S * q + S], u_chunk[:, k, q, :], x0[:, k, S * q:S * q + S],
                                     start=(k == 0), stop=(k == 1))
                    ins.then_inc(p_u, 1)
                if d is not None:
                    if first(d):
                        pe.wait_ge(s_tab, 9 * 16)
                        pe.wait_ge(vs_last, 1)
                    after(pe, v_o, d)
                    hidden(4, x2T, p_hx, start=True)
                if a is not None:
                    after(pe, v_u1, a)
                    for o in range(2):
                        ins = mm(P01[:, 512 * o:512 * o + 512], v1[:, 128 * o:128 * o + 128], u1[:, :],
                                 start=True, stop=True)
                    ins.then_inc(p_v1, 1)
                    if first(b):
                        small_tables()
                if d is not None:
                    after(pe, g_oh, d)
                    for o in range(2):
                        q = 3 * D + 128 * o
                        mm(ph[:, 512 * o:512 * o + 512], tables[:, q:q + 128], onehot[:, :], start=False, stop=False,
                           skip_group_check=True)
                    after(pe, g_ind, d)
                    for o in range(2):
                        mm(ph[:, 512 * o:512 * o + 512], vec_rows[:, 128 * o:128 * o + 128], ind[:, :],
                           start=False, stop=False, skip_group_check=True)
                    after(pe, v_xn, d, NT)
                    if a is not None:
                        after(pe, v_x1, a)
                    else:
                        after(pe, v_hT, d - 1)
                    turn(P01, xn, p_xnT)
                    if b is not None:
                        after(pe, v_dif, b, 2)
                    else:
                        after(pe, v_av, NC - 1, 4)
                    gain(pk, D, p_tg)
                if a is not None:
                    after(pe, v_ys, a)
                    proj(P23, kwT, ys, p_kx)
                    if first(a):
                        networks_out()
                if d is not None:
                    after(pe, v_tT, d)
                    hidden(2, tT, p_ht)
                    if a is not None:
                        after(pe, v_kx, a)
                    else:
                        after(pe, a_x2k, d)
                    gain(P23, 2 * D, p_sg)
                if b is not None:
                    values(0, b)
                if d is not None:
                    after(pe, v_sT, d)
                    hidden(10, xnT, p_hs, between=lambda: values(1, b))
                elif b is not None:
                    values(1, b)
                if b is not None:
                    values(2, b)
                if d is not None:
                    after(pe, v_hn, d, NT)
                    turn(P23, h1, p_hnT)
                    after(pe, a_xnT, d)
                    gain(P01, 0, p_cg)
                if b is not None:
                    values(3, b)

            stages(step, pe)

        @block.scalar
        def _(act):
            fn = act.activation

            def networks():
                act.wait_ge(vs_aw, 2)
                fn(awx[:, 0:6], aw, ACT.Exp).then_inc(as_aw, 1)
                act.wait_ge(ps_mh, 1)
                for m in range(3):
                    for a in range(2):
                        q = 64 * (2 * m + a)
                        fn(mx[:, m, a, :], pk[:, q:q + 64], ACT.Identity, bias=cols[:, 8 + 2 * m + a:9 + 2 * m + a]
                           ).then_inc(as_mx, 1)
                act.wait_ge(as_mx, 6)
                fn(mth, mx, ACT.Tanh, scale=0.5).then_inc(as_mth, 1)

            def step(a, b, d, e):
                if a is not None:
                    after(act, p_xT, a)
                    fn(xT[:, :, :], halves(P23), ACT.Copy).then_inc(a_xT, 1)
                if e is not None:
                    after(act, p_hid, e)
                    fn(th[:, :, :], halves(ph[:, :]), ACT.Tanh, scale=0.5).then_inc(a_th, 1)
                if a is not None:
                    after(act, v_t2, a)
                    fn(act0, t1, ACT.Relu).then_inc(a_act0, 1)
                if d is not None and (a is not None or b is None):
                    after(act, p_x2k, d)
                    after(act, g_y, d - 1)
                    fn(x2k[:, :, :], P23.rearrange("p (j f) -> p j f", j=NT), ACT.Copy).then_inc(a_x2k, 1)
                if first(a):
                    networks()
                if b is not None:
                    for f in range(2):
                        h = slice(8 * f, 8 * f + 8)
                        act.wait_ge(v_dif, 2 * b + f + 1)
                        fn(ex[:, h, :], ex[:, h, :], ACT.Exp, scale=SCALE).then_inc(a_ex, 1)
                        act.wait_ge(a_ex, 2 * b + f + 1)
                        if f == 0:
                            after(act, d_exw, b - 1, 16)
                        fn(ep[:, h, 0, :], ex[:, h, :], ACT.Copy).then_inc(a_ep0, 1)
                    for f in range(2):
                        h = slice(8 * f, 8 * f + 8)
                        act.wait_ge(v_er, 2 * b + f + 1)
                        fn(ep[:, h, 1, :], ex[:, h, :], ACT.Copy).then_inc(a_ep1, 1)
                if d is not None and a is None and b is not None:
                    after(act, p_x2k, d)
                    after(act, g_y, d - 1)
                    fn(x2k[:, :, :], P23.rearrange("p (j f) -> p j f", j=NT), ACT.Copy).then_inc(a_x2k, 1)
                if d is not None:
                    after(act, p_xnT, d)
                    after(act, p_hs, d - 1)
                    fn(xnT[:, :, :], halves(P01), ACT.Copy).then_inc(a_xnT, 1)
                if a is not None:
                    after(act, v_kx, a)
                    after(act, d_kxw, a - 1, 32)
                    for f in range(2):
                        fn(kp[:, f, :, 0, :], by_batch(kx[:, f, :]), ACT.Identity, bias=cols[:, 2 + f:3 + f]
                           ).then_inc(a_kp0, 1)
                    after(act, v_kr, a, 2)
                    fn(kp[:, :, :, 1, :], by_batch2(kx[:, :, :]), ACT.Copy).then_inc(a_kp1, 1)
                if d is not None:
                    after(act, p_hnT, d)
                    after(act, p_hid, d - 1)
                    fn(hnT[:, :, :], halves(P23), ACT.Copy).then_inc(a_hnT, 1)

            stages(step, act)

        @block.vector
        def _(ve_):
            tt, ts, stt, cp = ve_.tensor_tensor, ve_.tensor_scalar, ve_.scalar_tensor_tensor, ve_.tensor_copy
            seq = [0]

            def ordered(ins):
                seq[0] += 1
                ins.then_inc(vs_seq, 1)
                ve_.wait_ge(vs_seq, seq[0])

            ve_.wait_ge(s_cond, COND)
            ve_.wait_ge(ps_par, 1)
            cp(dg[:, :], ph[0:H0, 0:64])
            cp(db_rows[64:128, :], ph[64:128, 64:128])
            cp(ug[:, :, :], ph[:, 128:256].rearrange("p (a b) -> p a b", a=2))
            for l in range(2):
                for a in range(2):
                    q = 256 + 64 * (2 * l + a)
                    ts(style[:, l, a, :], ph[:, q:q + 64], cols[:, 4 * l + a:4 * l + a + 1], None, ALU.add)
            cp(ub_rows[64:128, :], ph[64:128, 576:832]).then_inc(vs_par, 1)
            ve_.wait_ge(vs_par, 1)
            tt(style2, style[:, :, :, :], style[:, :, :, :], ALU.mult).then_inc(vs_sq, 1)
            ve_.wait_ge(s_load, LAYERS)

            def first_factor(i):
                bank, k0, k1 = (pk, 0, 16) if i % 2 == 0 else (ph, 16, K1)
                ve_.wait_ge(ps_u, i + 1)
                src = bank[:, 0:64 * (k1 - k0)].rearrange("p (k b) -> p b k", b=B)
                for j in range(2):
                    tt(u_piece[2 * (i // 2) + j][:, :, k0:k1], src[:, 32 * j:32 * j + 32, :],
                       bdec[:, i // 2, k0:k1].unsqueeze(1).to_broadcast([128, 32, k1 - k0]), ALU.add
                       ).then_inc(vs_u, 1)

            def last_feature():
                ts(u_last[:, :], ph[0:K1, 896:960], bdec_last, None, ALU.add).then_inc(vs_last_u, 1)
                ve_.wait_ge(vs_last_u, 1)

            def squares():
                tt(sq[:, 0, :, :], kwT[:, :, :], kwT[:, :, :], ALU.mult)
                tt(sq[:, 1, :, :], owT[:, :, :], owT[:, :, :], ALU.mult).then_inc(vs_sq, 1)

            def demod_sums():
                ve_.wait_ge(ps_ss, 1)
                ts(demod[:, :, :, :], pk[:, 0:256].rearrange("p (l a b) -> p l a b", l=2, a=2), DEMOD_EPS, None,
                   ALU.add).then_inc(vs_ss, 1)

            def networks_hidden():
                ve_.wait_ge(s_late, LATE)
                ordered(ve_.tensor_reduce(awx[:, 8:9], aw, AX.X, ALU.max))
                ts(aw, aw, awx[:, 8:9], None, ALU.subtract).then_inc(vs_aw, 2)
                ve_.wait_ge(as_aw, 1)
                ordered(ve_.reduce_sum(awx[:, 9:10], awx[:, 0:6], AX.X))
                ordered(ve_.reciprocal(awx[:, 10:11], awx[:, 9:10]))
                ordered(ts(awx[:, 0:6], awx[:, 0:6], awx[:, 10:11], None, ALU.mult))
                ve_.wait_ge(as_mth, 1)
                ordered(stt(mx, mth, 1.0, mx, ALU.add, ALU.mult))
                ts(mx, mx, 0.5, None, ALU.mult).then_inc(vs_mlp, 1)
                for m in range(6):
                    ts(w1[:, 2 * m:2 * m + 2, :], w1[:, 2 * m:2 * m + 2, :], awx[:, m:m + 1], None, ALU.mult)
                ts(w2[:, :, :], w2[:, :, :], 0.5, None, ALU.mult).then_inc(vs_w1, 1)

            def networks_moments():
                ve_.wait_ge(ps_h2, 1)
                ordered(tt(mvec, ph[0:B, 0:768].rearrange("p (m j) -> p m j", m=3), rows[:, 0:3, :], ALU.add))
                for m in range(3):
                    ordered(ve_.bn_stats(stats[0:B, 0, m, :], mvec[:, m, :]))
                for m in range(3):
                    ordered(ve_.bn_aggr(mv[0:B, 0, m, :], stats[0:B, 0, m, :]))
                ts(ve[0:B, 0, 0:3], mv[0:B, 0, 0:3, 1], LN_EPS, None, ALU.add).then_inc(vs_mv, 1)

            def networks_norm():
                ve_.wait_ge(gs_rs, 1)
                for m in range(3):
                    ordered(ts(mvec[:, m, :], mvec[:, m, :], mv[0:B, 0, m, 0:1], rstd[0:B, 0, m:m + 1],
                               ALU.subtract, ALU.mult))
                ordered(tt(mvec, mvec, rows[:, 3:6, :], ALU.mult))
                tt(mvec, mvec, rows2[:, 0:3, :], ALU.add).then_inc(vs_vec, 1)

            def small_tables():
                ve_.wait_ge(ps_vT, 1)
                cp(mvT, ph[:, 0:384].rearrange("p (m a b) -> p m a b", m=3, a=2)).then_inc(vs_vT, 1)
                ve_.wait_ge(ps_vec, 1)
                tt(vec_rows[:, :], ph[0:B, 512:768], rows2[:, 3, :], ALU.add)
                cp(src5[:, 3 * D:4 * D], ph[0:5, 0:D])
                cp(src3[:, 3 * D:4 * D], ph[0:3, D:2 * D]).then_inc(vs_row, 1)
                ve_.wait_ge(vs_row, 1)
                work = ((src5, (parts5[:, 0, :], parts5[:, 1, :], parts5l)),
                        (src3, (parts3[:, 0, :], parts3[:, 1, :], parts3l)),
                        (b2src, (b2p[:, 0, :], b2p[:, 1, :], b2p[:, 2, :])))
                for s in range(3):
                    for src, dst in work:
                        ordered(cp(dst[s], src))
                    for src, dst in work:
                        if s < 2:
                            ordered(tt(src, src, dst[s], ALU.subtract))
                ve_.nop().then_inc(vs_parts, 1)
                ordered(tt(w1[:, 4:6, :], w1[:, 4:6, :], w1[:, 6:8, :], ALU.add))
                tt(w1[:, 4:6, :], w1[:, 4:6, :], w1[:, 8:10, :], ALU.add).then_inc(vs_last, 1)

            def moments(i, src, c):
                for j in range(NT):
                    ve_.bn_stats(stats[:, i, j, :], src[:, j, :]).then_inc(v_bn[i], 1)
                after(ve_, v_bn[i], c, NT)
                settled(ve_)
                for j in range(NT):
                    ve_.bn_aggr(mv[:, i, j, :], stats[:, i, j, :]).then_inc(v_mv[i], 1)

            def normalise(i, dst, src, c, s):
                after(ve_, v_mv[i], c, NT)
                after(ve_, g_rs[i], c)
                for j in range(NT):
                    ts(dst[:, j, :], src[:, j, :], mv[:, i, j, 0:1], rstd[:, i, j:j + 1], ALU.subtract, ALU.mult
                       ).then_inc(s, 1)

            def quotients(q, b):
                ve_.wait_ge(p_av, 4 * b + q + 1)
                if q == 0:
                    after(ve_, d_ow, b - 1, 16)
                pkq = pk[:, 512 * (q % 2):512 * (q % 2) + (HD + 1) * QG].rearrange("p (s e) -> p e s", e=HD + 1)
                ve_.reciprocal(rz[:, q, :], pkq[:, HD, :]).then_inc(v_rz, 1)
                ve_.wait_ge(v_rz, 4 * b + q + 1)
                tt(av[:, :, QG * q:QG * q + QG], pkq[:, 0:HD, :],
                   rz[:, q:q + 1, :].to_broadcast([128, HD, QG]), ALU.mult).then_inc(v_av, 1)

            def shifted_scores(b):
                after(ve_, p_g, b)
                ve_.tensor_reduce(rowmax[:, :], pk[:, :].rearrange("p (s h) -> p s h", h=NH), AX.X, ALU.max
                                  ).then_inc(v_max, 1)
                after(ve_, v_max, b)
                for f in range(2):
                    h = slice(8 * f, 8 * f + 8)
                    tt(ex[:, h, :].rearrange("p h s -> p s h"),
                       pk[:, :].rearrange("p (s h) -> p s h", h=NH)[:, :, h],
                       rowmax[:, :].unsqueeze(2).to_broadcast([128, S, 8]), ALU.subtract).then_inc(v_dif, 1)

            def exponential_parts(b):
                for f in range(2):
                    h = slice(8 * f, 8 * f + 8)
                    ve_.wait_ge(a_ep0, 2 * b + f + 1)
                    tt(ex[:, h, :], ex[:, h, :], ep[:, h, 0, :], ALU.subtract).then_inc(v_er, 1)
                for f in range(2):
                    h = slice(8 * f, 8 * f + 8)
                    ve_.wait_ge(a_ep1, 2 * b + f + 1)
                    tt(ep[:, h, 2, :], ex[:, h, :], ep[:, h, 1, :], ALU.subtract).then_inc(v_ep, 1)

            def step(a, b, d, e):
                if first(a):
                    first_factor(0)
                if e is not None:
                    after(ve_, a_th, e)
                    after(ve_, p_y, e - 1)
                    stt(hid[:, :, :], th[:, :, :], 1.0, halves(ph[:, :]), ALU.add, ALU.mult).then_inc(v_hid, 1)
                if a is not None:
                    after(ve_, p_down, a)
                    after(ve_, a_act0, a - 1)
                    tt(by_batch(row_in), by_batch(P0[64:128, :]),
                       per_batch(batch_eye[64:128, :], 64, a), ALU.mult).then_inc(v_row_in, 1)
                    tt(by_batch(t1), by_batch(P0[0:H0, :]), per_batch(dg[:, :], H0, a), ALU.mult
                       ).then_inc(v_t1, 1)
                if first(a):
                    first_factor(1)
                if a is not None:
                    after(ve_, p_db, a)
                    after(ve_, v_t1, a)
                    tt(t1, t1, P1[0:H0, :], ALU.add).then_inc(v_t2, 1)
                if e is not None:
                    after(ve_, p_y, e)
                    y = ph[:, :].rearrange("p (j f) -> p j f", j=NT)
                    moments(2, y, e)
                if a is not None:
                    after(ve_, p_up, a)
                    tt(by_batch(row_mid), by_batch(P0[64:128, :]), per_batch(batch_eye[64:128, :], B, a), ALU.mult
                       ).then_inc(v_row_mid, 1)
                if e is not None:
                    normalise(2, yn, y, e, v_yn)
                if a is not None:
                    tt(by_batch2(x0[:, :, :]), by_batch2(halves(P23)), per_batch2(ug[:, :, :], a), ALU.mult
                       ).then_inc(v_up, 1)
                    if first(b):
                        networks_norm()
                    after(ve_, v_up, a)
                    stt(x0[:, :, :], xT[:, :, :], 2.0, x0[:, :, :], ALU.mult, ALU.add).then_inc(v_x0a, 1)
                if first(a):
                    squares()
                    first_factor(2)
                if a is not None:
                    after(ve_, p_ub, a)
                    after(ve_, v_x0a, a)
                    tt(x0[:, :, :], x0[:, :, :], halves(P01), ALU.add).then_inc(v_x0, 1)
                if a is None and b is not None:
                    shifted_scores(b)
                    exponential_parts(b)
                if e is not None:
                    after(ve_, v_yn, e, NT)
                    tt(yn[:, :, :], yn[:, :, :], last_gb[:, 0:1, :].to_broadcast([128, NT, D]), ALU.mult
                       ).then_inc(v_yg, 1)
                if d is not None:
                    after(ve_, p_o, d)
                    if first(d):
                        ve_.wait_ge(s_tab, 9 * 16)
                    tt(by_batch2(tmp_o[:, :, :]), by_batch2(halves(ph[:, :])), per_batch2(demod[:, 1, :, :], d),
                       ALU.mult).then_inc(v_o, 1)
                    after(ve_, v_o, d)
                    after(ve_, d_x1r, d, 16)
                    for f in range(2):
                        stt(x2T[:, f, :], tmp_o[:, f, :], cols[:, 6 + f:7 + f], x1r[:, f, :], ALU.add, ALU.add
                            ).then_inc(v_x2, 1)
                if d is not None:
                    after(ve_, a_x2k, d)
                    moments(0, x2k, d)
                    normalise(0, xn, x2k, d, v_xn)
                if a is not None and b is not None:
                    shifted_scores(b)
                if first(a):
                    first_factor(3)
                    last_feature()
                    demod_sums()
                    networks_hidden()
                if a is not None:
                    after(ve_, p_u, a)
                    tt(by_batch(u1[:, :]), by_batch(P2[0:K1, :]), per_batch(u_last[:, :], K1, a), ALU.add
                       ).then_inc(v_u1, 1)
                if a is not None and b is not None:
                    exponential_parts(b)
                if a is not None:
                    after(ve_, p_v1, a)
                    after(ve_, d_x1w, a - 1, 16)
                    tt(x1[:, :, :], x0[:, :, :], halves(P01), ALU.add).then_inc(v_x1, 1)
                    after(ve_, v_x1, a)
                    tt(by_batch2(ys[:, :, :]), by_batch2(x1[:, :, :]), per_batch2(style[:, 0, :, :], a), ALU.mult
                       ).then_inc(v_ys, 1)
                    if first(b):
                        small_tables()
                if d is not None:
                    for j in range(NT):
                        after(ve_, d_pw[j], d, 16)
                    after(ve_, d_out, d - 1, 16)
                    after(ve_, v_xn, d, NT)
                    tt(h1[:, :, :], xn[:, :, :], pwgb[:, :, 0:D], ALU.mult).then_inc(v_h1a, 1)
                    after(ve_, a_xnT, d)
                    after(ve_, p_tg, d)
                    tt(tT[:, :, :], xnT[:, :, :], halves(pk[:, :]), ALU.mult).then_inc(v_tT, 1)
                    after(ve_, v_h1a, d)
                    tt(h1[:, :, :], h1[:, :, :], pwgb[:, :, D:2 * D], ALU.add).then_inc(v_h1, 1)
                if a is not None:
                    after(ve_, p_kx, a)
                    after(ve_, v_kp, a - 1)
                    after(ve_, gs_dem, a)
                    if first(a):
                        ve_.wait_ge(d_usave, 64)
                    tt(by_batch2(kx[:, :, :]), by_batch2(halves(P23)), per_batch2(demod[:, 0, :, :], a), ALU.mult
                       ).then_inc(v_kx, 1)
                if d is not None:
                    after(ve_, v_h1, d)
                    moments(1, h1, d)
                if a is not None:
                    after(ve_, a_kp0, a, 2)
                    for f in range(2):
                        stt(by_batch(kx[:, f, :]), by_batch(kx[:, f, :]), cols[:, 2 + f:3 + f], kp[:, f, :, 0, :],
                            ALU.add, ALU.subtract).then_inc(v_kr, 1)
                if d is not None:
                    after(ve_, p_sg, d)
                    after(ve_, v_tT, d)
                    tt(xnT[:, :, :], xnT[:, :, :], halves(P23), ALU.mult).then_inc(v_sT, 1)
                if a is not None:
                    after(ve_, a_kp1, a)
                    tt(kp[:, :, :, 2, :], by_batch2(kx[:, :, :]), kp[:, :, :, 1, :], ALU.subtract).then_inc(v_kp, 1)
                    if first(a):
                        networks_moments()
                if b is not None:
                    quotients(0, b)
                    quotients(1, b)
                if d is not None:
                    normalise(1, h1, h1, d, v_hn)
                if b is not None:
                    quotients(2, b)
                if d is not None:
                    after(ve_, a_hnT, d)
                    after(ve_, p_cg, d)
                    tt(hnT[:, :, :], hnT[:, :, :], halves(P01), ALU.mult).then_inc(v_hT, 1)
                if b is not None:
                    quotients(3, b)

            stages(step, ve_)


def kernel(**inputs):
    import numpy as np
    import concourse.bacc as bacc
    from concourse.bass_utils import run_bass_kernel_spmd

    g = {k: np.asarray(v) for k, v in inputs.items()}
    p3 = lambda k: g["L3_cond_" + k]
    split = lambda a: a.reshape(2, 128, -1).transpose(1, 0, 2)
    col = lambda a: a.reshape(2, 128).T
    kperm = lambda a: a.reshape(NH, HD, -1).transpose(1, 0, 2).reshape(D, -1)
    f = np.float32
    w_dec = g["L1_cond_W_dec"].reshape(128, D + 1, K1)
    b_dec = g["L1_cond_b_dec"].reshape(D + 1, K1)
    rowclass = np.zeros((128, 1), f)
    rowclass[0:15, 0] = np.tile(np.arange(5), 3)
    rowclass[15:24, 0] = np.tile(np.arange(3), 3)
    arrays = {
        "x": g["x"].reshape(NC * NT, 128, D).transpose(1, 0, 2),
        "ident": np.eye(128, dtype=f),
        "batch_eye": np.tile(np.eye(B, dtype=f), (2, 1)),
        "rowclass": rowclass,
        "condT": g["cond_512"].T, "c64T": g["cond_64"].T, "fsT": g["fside_Bx32_0"].T,
        "dgam": g["L0_cond_down_gamma"], "dbet": g["L0_cond_down_beta"],
        "ugam": g["L0_cond_up_gamma"], "ubet": g["L0_cond_up_beta"],
        "down": split(g["L0_cond_down_project"]), "up": g["L0_cond_up_project"],
        "w_dec": w_dec.transpose(0, 2, 1), "bdec": b_dec[:D].reshape(2, 128, K1).transpose(1, 0, 2),
        "bdec_last": b_dec[D].reshape(K1, 1), "V": g["L1_cond_V"],
        "kaffT": g["L2_cond_k_aff_w"].T, "oaffT": g["L2_cond_o_aff_w"].T,
        "kwT": split(kperm(g["L2_cond_k_w"]).T), "owT": split(g["L2_cond_o_w"].T),
        "cols": np.concatenate([col(g["L2_cond_k_aff_b"]), col(kperm(g["L2_cond_k_b"])), col(g["L2_cond_o_aff_b"]),
                                col(g["L2_cond_o_b"])] + [col(p3(m + "_b1")) for m in MLPS], axis=1),
        "w1": p3("int_W1").reshape(12, 128, D).transpose(1, 0, 2), "w2": split(p3("int_W2")),
        **{m + "_W1": p3(m + "_W1") for m in MLPS}, **{m + "_W2": split(p3(m + "_W2")) for m in MLPS},
        "rows": np.stack([p3(m + k) for k in ("_b2", "_g", "_be") for m in MLPS] + [p3("int_b1")])[None],
        "last_gb": np.stack([p3("int_g"), p3("int_be")])[None], "aw": p3("aw").reshape(1, 6),
        "tabT": split(np.concatenate([p3("cp_b"), p3("tm_b"), p3("ms_b")]).T),
        "cp_g": p3("cp_g"), "tm_g": p3("tm_g"), "ms_g": p3("ms_g"), "b2": p3("int_b2").reshape(1, D),
        "pw_gb": np.concatenate([p3("pw_g"), p3("pw_b")], axis=1),
        "pw_idx": g["itok_BxS_0_999"].reshape(NC * NT, 128).T,
        "c_idx": g["itok_BxS_0_4"].reshape(1, B * S), "m_idx": g["mask_BxS_ik0"].reshape(1, B * S),
    }
    arrays = {k: np.ascontiguousarray(v) for k, v in arrays.items()}
    nc = bacc.Bacc("TRN2", target_bir_lowering=False, num_devices=1)
    t = {k: nc.dram_tensor("in_" + k, list(v.shape), mybir.dt.from_np(v.dtype), kind="ExternalInput").ap()
         for k, v in arrays.items()}
    out = nc.dram_tensor("out", [B * S, D], F32, kind="ExternalOutput").ap()
    build(nc, t, out.rearrange("(n p) f -> p n f", p=128))
    r = run_bass_kernel_spmd(nc, [{"in_" + k: v for k, v in arrays.items()}], core_ids=[0])
    return np.asarray(r.results[0]["out"]).reshape(B, S, D)
```
